# Optimizing a Trainium2 kernel written in Bass

```python
import numpy as np
import jax
import jax.numpy as jnp

def _softmax(x, axis=-1):
    return jax.nn.softmax(x, axis=axis)

def _gelu(x):
    return jax.nn.gelu(x, approximate=True)

def _silu(x):
    return jax.nn.silu(x)

def _sigmoid(x):
    return jax.nn.sigmoid(x)

def _layernorm(x, axis=-1, eps=1e-05):
    m = jnp.mean(x, axis=axis, keepdims=True)
    v = jnp.var(x, axis=axis, keepdims=True)
    return (x - m) / jnp.sqrt(v + eps)

def _scatter_add(tgt, idx, src, axis=0):
    return tgt.at[idx].add(src)

def _segment_sum(src, seg, n):
    return jax.ops.segment_sum(src, seg, n)
kernel_name = 'mk_adaln_d1_jaxref_r8_807a4a'

def setup_inputs(seed: int=0):
    np.random.seed(seed)
    _w = jnp.asarray

    def _L0_attn_setup():
        import jax, jax.numpy as jnp
        import numpy as np
        NUM_HEADS = 16
        D_MODEL = 128
        D_K = D_MODEL // NUM_HEADS
        MAX_SEQ_LEN = 512
        ROPE_BASE = 10000.0
        BATCH = 2
        SEQ_LEN = 256

        def _rope_tables(seq_len, d_k, base=ROPE_BASE):
            theta = 1.0 / base ** (jnp.arange(0, d_k, 2, dtype=jnp.float32) / d_k)
            m = jnp.arange(seq_len, dtype=jnp.float32)
            m_theta = jnp.outer(m, theta)
            ang = jnp.concatenate([m_theta, m_theta], axis=-1)
            return (jnp.cos(ang), jnp.sin(ang))

        def _apply_rope(x, cos, sin):
            d2 = x.shape[-1] // 2
            x1, x2 = (x[..., :d2], x[..., d2:])
            x_flip = jnp.concatenate([-x2, x1], axis=-1)
            return x * cos + x_flip * sin
        key = jax.random.key(seed)
        kx, kq, kk, kv, ko = jax.random.split(key, 5)
        s = 1.0 / np.sqrt(D_MODEL)
        x = jax.random.normal(kx, (BATCH, SEQ_LEN, D_MODEL), dtype=jnp.float32)
        W_Q = jax.random.uniform(kq, (D_MODEL, D_MODEL), jnp.float32, -s, s)
        W_K = jax.random.uniform(kk, (D_MODEL, D_MODEL), jnp.float32, -s, s)
        W_V = jax.random.uniform(kv, (D_MODEL, D_MODEL), jnp.float32, -s, s)
        W_O = jax.random.uniform(ko, (D_MODEL, D_MODEL), jnp.float32, -s, s)
        return {'x': x, 'W_Q': W_Q, 'W_K': W_K, 'W_V': W_V, 'W_O': W_O}
    _L0_attn_in = _L0_attn_setup()

    def _L0_ffn_setup():
        import jax, jax.numpy as jnp
        import numpy as np
        E = 8
        K = 2
        key = jax.random.key(seed)
        ks = jax.random.split(key, 6)
        B, S, D, F = (4, 256, 128, 512)
        s_d = 1.0 / np.sqrt(D).astype(np.float32)
        s_f = 1.0 / np.sqrt(F).astype(np.float32)
        return {'x': jax.random.normal(ks[0], (B, S, D), jnp.float32), 'ln_w': jnp.ones((D,), jnp.float32), 'Wg': jax.random.normal(ks[1], (D, E), jnp.float32) * s_d, 'bg': jnp.zeros((E,), jnp.float32), 'W1a': jax.random.normal(ks[2], (E, D, F), jnp.float32) * s_d, 'b1a': jnp.zeros((E, F), jnp.float32), 'W1b': jax.random.normal(ks[3], (E, D, F), jnp.float32) * s_d, 'b1b': jnp.zeros((E, F), jnp.float32), 'W2': jax.random.normal(ks[4], (E, F, D), jnp.float32) * s_f, 'b2': jnp.zeros((E, D), jnp.float32)}
    _L0_ffn_in = _L0_ffn_setup()
    _L0_c = _w((lambda *s: np.random.randn(*s).astype(np.float32) * 0.05)(16, 128))
    _L0_wmod = _w((lambda *s: np.random.randn(*s).astype(np.float32) * 0.05)(128, 6 * 128) * 128 ** (-0.5))
    _d = {'L0_attn_x': _L0_attn_in['x'], 'L0_attn_W_Q': _L0_attn_in['W_Q'], 'L0_attn_W_K': _L0_attn_in['W_K'], 'L0_attn_W_V': _L0_attn_in['W_V'], 'L0_attn_W_O': _L0_attn_in['W_O'], 'L0_ffn_ln_w': _L0_ffn_in['ln_w'], 'L0_ffn_Wg': _L0_ffn_in['Wg'], 'L0_ffn_bg': _L0_ffn_in['bg'], 'L0_ffn_W1a': _L0_ffn_in['W1a'], 'L0_ffn_b1a': _L0_ffn_in['b1a'], 'L0_ffn_W1b': _L0_ffn_in['W1b'], 'L0_ffn_b1b': _L0_ffn_in['b1b'], 'L0_ffn_W2': _L0_ffn_in['W2'], 'L0_ffn_b2': _L0_ffn_in['b2'], 'L0_c': _L0_c, 'L0_wmod': _L0_wmod}
    _x0 = _d['L0_attn_x']
    _d['L0_attn_x'] = jax.random.normal(jax.random.fold_in(jax.random.key(seed), 1), (16, 256, 128), dtype=_x0.dtype)
    del _x0
    return _d

def reference(L0_attn_x, L0_attn_W_Q, L0_attn_W_K, L0_attn_W_V, L0_attn_W_O, L0_ffn_ln_w, L0_ffn_Wg, L0_ffn_bg, L0_ffn_W1a, L0_ffn_b1a, L0_ffn_W1b, L0_ffn_b1b, L0_ffn_W2, L0_ffn_b2, L0_c, L0_wmod):

    def _L0_attn_ref(x, W_Q, W_K, W_V, W_O):
        import jax, jax.numpy as jnp
        import numpy as np
        NUM_HEADS = 16
        D_MODEL = 128
        D_K = D_MODEL // NUM_HEADS
        MAX_SEQ_LEN = 512
        ROPE_BASE = 10000.0
        BATCH = 2
        SEQ_LEN = 256

        def _rope_tables(seq_len, d_k, base=ROPE_BASE):
            theta = 1.0 / base ** (jnp.arange(0, d_k, 2, dtype=jnp.float32) / d_k)
            m = jnp.arange(seq_len, dtype=jnp.float32)
            m_theta = jnp.outer(m, theta)
            ang = jnp.concatenate([m_theta, m_theta], axis=-1)
            return (jnp.cos(ang), jnp.sin(ang))

        def _apply_rope(x, cos, sin):
            d2 = x.shape[-1] // 2
            x1, x2 = (x[..., :d2], x[..., d2:])
            x_flip = jnp.concatenate([-x2, x1], axis=-1)
            return x * cos + x_flip * sin
        B, S, _ = x.shape

        def proj(W):
            y = jnp.einsum('bsd,ed->bse', x, W)
            return y.reshape(B, S, NUM_HEADS, D_K).transpose(0, 2, 1, 3)
        Q, K, V = (proj(W_Q), proj(W_K), proj(W_V))
        cos, sin = _rope_tables(S, D_K)
        Q = _apply_rope(Q, cos, sin)
        K = _apply_rope(K, cos, sin)
        scores = jnp.einsum('bhsd,bhtd->bhst', Q, K) / jnp.sqrt(jnp.float32(D_K))
        causal = jnp.tril(jnp.ones((S, S), dtype=bool))
        scores = jnp.where(causal[None, None], scores, -jnp.inf)
        attn = jax.nn.softmax(scores, axis=-1)
        out = jnp.einsum('bhst,bhtd->bhsd', attn, V)
        out = out.transpose(0, 2, 1, 3).reshape(B, S, D_MODEL)
        return jnp.einsum('bsd,ed->bse', out, W_O)

    def _L0_ffn_ref(x, ln_w, Wg, bg, W1a, b1a, W1b, b1b, W2, b2):
        import jax, jax.numpy as jnp
        import numpy as np
        E = 8
        K = 2
        B, S, D = x.shape
        eps = jnp.finfo(x.dtype).eps
        xn = x * jax.lax.rsqrt(jnp.mean(x * x, axis=-1, keepdims=True) + eps) * ln_w
        logits = xn @ Wg + bg
        vals, idx = jax.lax.top_k(logits, K)
        topk_w = jax.nn.softmax(vals, axis=-1)
        we = jnp.sum(jax.nn.one_hot(idx, E, dtype=x.dtype) * topk_w[..., None], axis=-2)
        T = B * S
        xf = xn.reshape(T, D)
        wef = we.reshape(T, E).T

        def step(acc, params):
            W1a_e, b1a_e, W1b_e, b1b_e, W2_e, b2_e, w_e = params
            a = xf @ W1a_e + b1a_e
            b = xf @ W1b_e + b1b_e
            y = jax.nn.silu(a) * b @ W2_e + b2_e
            return (acc + w_e[:, None] * y, None)
        out0 = jnp.zeros_like(xf)
        out, _ = jax.lax.scan(step, out0, (W1a, b1a, W1b, b1b, W2, b2, wef))
        return out.reshape(B, S, D)
    x = L0_attn_x
    mod = (_silu(L0_c) @ L0_wmod).reshape(L0_c.shape[0], 6, 1, -1)
    sa, ca, ga, sb, cb, gb = (mod[:, 0], mod[:, 1], mod[:, 2], mod[:, 3], mod[:, 4], mod[:, 5])
    ga = (2 * (ga >= 0) - 1) * jnp.maximum(jnp.abs(ga), 0.25)
    gb = (2 * (gb >= 0) - 1) * jnp.maximum(jnp.abs(gb), 0.25)
    h = _layernorm(x, axis=-1) * (1 + ca) + sa
    x = x + ga * _L0_attn_ref(h, L0_attn_W_Q, L0_attn_W_K, L0_attn_W_V, L0_attn_W_O)
    h = _layernorm(x, axis=-1) * (1 + cb) + sb
    x = x + gb * _L0_ffn_ref(h, L0_ffn_ln_w, L0_ffn_Wg, L0_ffn_bg, L0_ffn_W1a, L0_ffn_b1a, L0_ffn_W1b, L0_ffn_b1b, L0_ffn_W2, L0_ffn_b2)
    return x

_drawn_inputs = setup_inputs


def setup_inputs(seed=0):
    import zlib

    import numpy as np

    out = dict(_drawn_inputs(seed))
    spreads = {'L0_ffn_ln_w': (1.0, 0.2),
     'L0_ffn_bg': (0.0, 0.318),
     'L0_ffn_b1a': (0.0, 0.663),
     'L0_ffn_b1b': (0.0, 0.689),
     'L0_ffn_b2': (0.0, 0.438)}
    factors = {'L0_attn_W_Q': 8.0, 'L0_attn_W_K': 8.0, 'L0_attn_W_V': 3.501, 'L0_attn_W_O': 3.563}
    for name, (base, spread) in spreads.items():
        noise = np.random.default_rng([zlib.crc32(name.encode()), seed]).standard_normal(out[name].shape)
        drawn = base * np.exp(spread * noise) if base else spread * noise
        out[name] = jnp.asarray(drawn.astype(out[name].dtype))
    for name, factor in factors.items():
        out[name] = (out[name] * factor).astype(out[name].dtype)
    return out
```

```python
from contextlib import ExitStack

import numpy as np

import concourse.bass as bass
from concourse import mybir

F32 = mybir.dt.float32
F16 = mybir.dt.float16
BF16 = mybir.dt.bfloat16
I32 = mybir.dt.int32
U32 = mybir.dt.uint32
ALU = mybir.AluOpType
ACT = mybir.ActivationFunctionType
AX = mybir.AxisListType

P = 128
B, S, D = 16, 256, 128
H, DK = 16, 8
E, K, F = 8, 2, 512
NS = S // P
HG = 4
SLOT = P // HG
FB = F // P
TS = 256
NT = (B * S * K + E * (TS - 1)) // TS
REGION = B * S + TS
ROWS = E * REGION + TS
ROWW = D + 4
W_IDX, W_WGT = D, D + 1
NOUT = B * S * K
CHUNK = F // NS
SM_SCALE = float(1.0 / np.sqrt(np.float32(DK)))
EPS_LN = 1e-5
EPS_RMS = float(np.finfo(np.float32).eps)
MASKED = -1e30
C_COS, C_SIN, C_E, C_BASE, C_TOK, C_POW, C_J = 0, 8, 16, 24, 32, 36, 40
NC32 = C_J + NT + 1


class Steps:

    def __init__(self, sem, names):
        self.sem, self.names = sem, names.split()

    def after(self, n, name):
        return times(n, len(self.names), self.names.index(name) + 1)


def times(n, k, c=0):
    m, r, unroll = n
    return m * (unroll * k) + (r * k + c)


def plus(n, by):
    m, r, unroll = n
    return m + (r + by) // unroll, (r + by) % unroll, unroll


def due(count):
    return not isinstance(count, int) or count > 0


def build(nc, x_in, wq, wk, wv, wo, ln_w, wg, bg, w1a, b1a, w1b, b1b, w2, b2, c_in, wmod, const32,
          const16, constb, dummy_in, out):
    ctx = ExitStack()
    with ctx:
        def sb(name, shape, dt=F32):
            return ctx.enter_context(nc.sbuf_tensor(name, shape, dt))

        def sem(name):
            return ctx.enter_context(nc.semaphore(name))

        def steps(name, names):
            return Steps(sem(name), names)

        mod_rows = nc.dram_tensor("mod_rows", [B, 4 * D], F32).ap()
        rows = nc.dram_tensor("expert_rows", [ROWS, ROWW], F32).ap()
        outs = nc.dram_tensor("expert_outs", [NOUT, D], F32).ap()

        c32 = sb("c32", [P, NC32])
        c16 = sb("c16", [P, 3, P], F16)
        cb = sb("cb", [P, 2, P], BF16)
        ident32 = sb("ident32", [P, P])
        ident16, before16, ones16 = c16[:, 0, :], c16[:, 1, :], c16[:, 2, :]
        mask_q, mask_k = cb[:, 0, :], cb[:, 1, :]
        wraw = sb("wraw", [P, 4, D])
        wmod_sb = sb("wmod_sb", [P, 6 * D])
        c_sb = sb("c_sb", [B, D])
        silu_c = sb("silu_c", [P, B])
        mod_sb = sb("mod_sb", [B, 4 * D])
        mod_t = sb("mod_t", [P, B])
        scale_in = sb("scale_in", [P, B])
        shift_in = sb("shift_in", [P, B])
        w_hi = sb("w_hi", [P, 4, D], F16)
        w_lo = sb("w_lo", [P, 4, D], F16)
        wg_sb = sb("wg_sb", [P, E])
        bg_sb = sb("bg_sb", [P, E])
        lnw_sb = sb("lnw_sb", [P, D])
        b1_rows = sb("b1_rows", [E * FB, 2, P])
        b1_sb = sb("b1_sb", [P, 2, E * FB])
        b2_sb = sb("b2_sb", [P, E, D])
        we_hi = sb("we_hi", [P, 3, E * F], F16)
        we_lo = sb("we_lo", [P, 3, E * F], F16)
        dummy_sb = sb("dummy_sb", [P, NS, ROWW])
        x_sb = sb("x_sb", [P, B * NS, D])
        wstage = sb("wstage", [P, 2, 3, CHUNK])
        st0 = sb("st0", [P, NS, 6])
        mv0 = sb("mv0", [P, NS, 2])
        ve0 = sb("ve0", [P, NS])
        rstd0 = sb("rstd0", [P, NS])
        xhat0 = sb("xhat0", [P, NS, D])
        ht32 = sb("ht32", [P, S])
        ht_hi = sb("ht_hi", [P, S], F16)
        ht_lo = sb("ht_lo", [P, S], F16)
        turn_c = sb("turn_c", [P, NS, 2 * H, DK])
        turn_s = sb("turn_s", [P, NS, 2 * H, DK])
        turned = sb("turned", [P, NS, 2 * H, DK])
        v_sb = sb("v_sb", [P, 2, NS, D])
        qk_tok = sb("qk_tok", [P, 2, NS, 2 * H, SLOT], F16)
        qk_t = sb("qk_t", [P, 2, 2 * HG, S], F16)
        k_pad = sb("k_pad", [P, 2, H, S], F16)
        nmax = sb("nmax", [P, H, 3])
        q_max = sb("q_max", [P, 2, HG, S], F16)
        v_aug = sb("v_aug", [P, 2, NS, H, SLOT])
        probs = sb("probs", [P, 4, S + P])
        o_t = sb("o_t", [P, 2, HG, S])
        mod_b = sb("mod_b", [P, 2, 4 * D])
        rsum = sb("rsum", [P, NS, H])
        o_n = sb("o_n", [P, NS, D])
        on_hi = sb("on_hi", [P, S], F16)
        on_lo = sb("on_lo", [P, S], F16)
        gated = sb("gated", [P, NS, D])
        st3 = sb("st3", [P, NS, 6])
        mv3 = sb("mv3", [P, NS, 2])
        ve3 = sb("ve3", [P, NS])
        rstd3 = sb("rstd3", [P, NS])
        xhat3 = sb("xhat3", [P, NS, D])
        h_s = sb("h_s", [P, NS, D])
        h_m = sb("h_m", [P, NS, D])
        square = sb("square", [P, NS, D])
        ssum = sb("ssum", [P, NS])
        ms = sb("ms", [P, NS])
        rms = sb("rms", [P, NS])
        xn = sb("xn", [P, NS, D])
        xn_t = sb("xn_t", [P, S])
        logits = sb("logits", [P, NS, E])
        top = sb("top", [P, NS, 8])
        top_i = sb("top_i", [P, NS, 8], U32)
        top_f = sb("top_f", [P, NS, K])
        chosen = sb("chosen", [P, NS, K, E])
        member = sb("member", [P, NS, E], F16)
        gap = sb("gap", [P, NS])
        egap = sb("egap", [P, NS])
        den = sb("den", [P, NS])
        rank = sb("rank", [P, NS, E])
        filled = sb("filled", [P, E])
        at_e = sb("at_e", [P, NS, K, E])
        pos_f = sb("pos_f", [P, NS, K])
        pos_i = sb("pos_i", [P, NS, K], I32)
        tok = sb("tok", [P, K, NS])
        send = sb("send", [P, K, NS, ROWW])
        tab = sb("tab", [P, 8, E])
        tab_i = sb("tab_i", [P, 2, E], I32)
        cmp_j = sb("cmp_j", [P, NT + 1, E])
        tj = sb("tj", [P, 5, NT + 1])
        tile_e = sb("tile_e", [P, NT + 1], I32)
        tile_row = sb("tile_row", [P, NT + 1], I32)
        g_in = sb("g_in", [P, 4, NS, ROWW])
        xt = sb("xt", [P, 2, 2, TS], F16)
        silu_a = sb("silu_a", [P, FB, TS])
        h32 = sb("h32", [P, FB, TS])
        hh = sb("hh", [P, 2, FB, TS], F16)
        hl = sb("hl", [P, 2, FB, TS], F16)
        yb = sb("yb", [P, 2, NS, D])
        y_sb = sb("y_sb", [P, 4, NS, D])
        gb_sb = k_pad[:, 0].rearrange("p h t -> p (h t)").bitcast(F32).rearrange("p (b d) -> p b d", d=D)
        free = we_lo[:].rearrange("p n f -> p (n f)").bitcast(F32)

        def last(start, blocks):
            return free[:, start * NS * D:(start + blocks) * NS * D]

        y_in = last(0, 8).rearrange("p (r s k d) -> p r s k d", s=NS, k=K, d=D)
        ysum = last(8, 2).rearrange("p (r s d) -> p r s d", s=NS, d=D)
        ygate = last(10, 2).rearrange("p (r s d) -> p r s d", s=NS, d=D)
        res = last(12, 4).rearrange("p (r s d) -> p r s d", s=NS, d=D)

        banks = [ctx.enter_context(nc.psum_tensor(f"bank{i}", [P, 512], F32)) for i in range(8)]
        row_bank, col_bank = banks[0:2], banks[2:4]
        o_bank, chain_a, chain_b, tail_bank = banks[4:8]
        chain_a16, chain_b16 = chain_a[:].bitcast(F16), chain_b[:].bitcast(F16)

        consts_in = sem("consts_in")
        x_in0, x_in1 = sem("x_in0"), sem("x_in1")
        moe_consts_in = sem("moe_consts_in")
        dummies_out = sem("dummies_out")
        mod_out, gb_in = sem("mod_out"), sem("gb_in")
        init_vec, init_pool = sem("init_vec"), sem("init_pool")
        setup_pe = steps("setup_pe", "c_t w_t mod_t")
        setup_act = steps("setup_act", "silu b1 w_hi")
        setup_vec = steps("setup_vec", "w_lo scale shift copied abs_a abs_b sign_a sign_b sgn_a sgn_b gate_a gate_b plus1")
        wstage_in = [sem("wstage_in0"), sem("wstage_in1")]
        mod_in = [sem("mod_in0"), sem("mod_in1")]
        pad_in = [[sem(f"pad_in{h}{p}") for p in range(2)] for h in range(2)]
        pe0 = steps("pe0", "x_t proj0 proj1 t0 t1")
        vec0 = steps("vec0", "stats0 stats1 aggr0 aggr1 var xhat0 xhat1 cos0 sin0a sin0b hi0 cos1 sin1a sin1b hi1 w_hi w_lo")
        act0 = steps("act0", "h32 h_hi v0 khi0 v1 khi1 ev0 ev1")
        pool0 = steps("pool0", "rstd zero_m h_lo turn0 qlo0 klo0 turn1 qlo1 klo1")
        rows_ready, max_ready = sem("rows_ready"), sem("max_ready")
        vec1 = steps("vec1", "m0a m1a m0b m1b")
        pe1 = steps("pe1", "ta tb")
        act1 = steps("act1", "v_aug eva evb")
        cols_ready, probs_ready, probs_used, group_saved = sem("cols_ready"), sem("probs_ready"), sem("probs_used"), sem("group_saved")
        pe3 = steps("pe3", "o0 o1 on_t wo xn_t logits ranks")
        vec3 = steps("vec3", "rs0 on0 rs1 on1 on_lo gated stats0 stats1 aggr0 aggr1 var xhat0 xhat1 ms xn0 xn1 logits max0 max1 idx0 idx1 idxf chosen member gap den w1 w2 rank filled at pos_f pos_i copy tok tok_on")
        act3 = steps("act3", "on_hi sq0 sq1 xn_t egap xn_hi")
        pool3 = steps("pool3", "resid rstd scaled shifted rms xn_lo")
        sent = sem("sent")
        table = sem("table")
        padded = sem("padded")
        g_arrived = [sem(f"g_arrived{r}") for r in range(4)]
        pe_x = sem("pe_x")
        act_x = sem("act_x")
        pe_ab, act_silu, vec_h, act_hh, vec_hl = sem("pe_ab"), sem("act_silu"), sem("vec_h"), sem("act_hh"), sem("vec_hl")
        pe_y, vec_y, act_y = sem("pe_y"), sem("vec_y"), sem("act_y")
        y_sent = [sem(f"y_sent{r}") for r in range(4)]
        y_back = [sem(f"y_back{r}") for r in range(4)]
        pool_sum, vec_gate, vec_res = sem("pool_sum"), sem("vec_gate"), sem("vec_res")
        out_done = [sem(f"out_done{r}") for r in range(4)]

        TABLE_STEPS = 18
        N_CONST = 14
        N_MOE_CONST = 3

        def number(n):
            return n // 2, n % 2, 2

        def pipeline(eng, iteration):
            def one(i):
                iteration(number(i), 1 <= i <= B, 0 <= i < B, -1 <= i < B - 1, i < B - 2)
            for i in range(-2, 3):
                one(i)
            with eng.Fori(1, 6) as m:
                iteration((m, 1, 2), True, True, True, True)
                iteration((m + 1, 0, 2), True, True, True, True)
            for i in range(13, B + 1):
                one(i)

        def in_fours(eng, first, end, body):
            start = max(4, (first + 3) // 4 * 4)
            for n in range(first, start):
                body((n // 4, n % 4, 4))
            with eng.Fori(start // 4, end // 4) as m:
                for r in range(4):
                    body((m, r, 4))
            for n in range(end // 4 * 4, end):
                body((n // 4, n % 4, 4))

        x_view = x_in.rearrange("b (s p) d -> p (b s) d", p=P)
        w1a_v = w1a.rearrange("e d (h f) -> e h d f", h=NS)
        w1b_v = w1b.rearrange("e d (h f) -> e h d f", h=NS)
        w2_v = w2.rearrange("e (h c f) d -> e h f c d", h=NS, f=P)

        block = ctx.enter_context(nc.Block())

        @block.sync
        def _(sp):
            sp.dma_start(c_sb[:], c_in).then_inc(consts_in, 16)
            sp.dma_start(ident32[:], const32[:, NC32:NC32 + P]).then_inc(consts_in, 16)
            sp.dma_start(wmod_sb[:], wmod).then_inc(consts_in, 16)
            sp.dma_start(c32[:], const32[:, 0:NC32]).then_inc(consts_in, 16)
            sp.dma_start(x_sb[:, 0:4, :], x_view[:, 0:4, :]).then_inc(x_in0, 16)
            for n, w in enumerate((wq, wk, wv, wo)):
                sp.dma_start(wraw[:, n, :], w).then_inc(consts_in, 16)
            sp.dma_start(c16[:], const16).then_inc(consts_in, 16)
            sp.dma_start(cb[:], constb).then_inc(consts_in, 16)
            sp.dma_start(wg_sb[:], wg).then_inc(consts_in, 16)
            sp.dma_start(x_sb[:, 4:, :], x_view[:, 4:, :]).then_inc(x_in1, 16)
            sp.wait_ge(mod_out, 16)

            def iteration(i, s3, s2, s1, s0):
                if s0:
                    b = plus(i, 2)
                    m, par, _ = b
                    if due(vec0.after(plus(b, -2), "w_lo")):
                        sp.wait_ge(vec0.sem, vec0.after(plus(b, -2), "w_lo"))
                    sp.dma_start(wstage[:, par, 0, :], w1a_v[m, par]).then_inc(wstage_in[par], 16)
                    sp.dma_start(wstage[:, par, 1, :], w1b_v[m, par]).then_inc(wstage_in[par], 16)
                    sp.dma_start(wstage[:, par, 2, :].rearrange("p (c d) -> p c d", d=D), w2_v[m, par]).then_inc(wstage_in[par], 16)
                if s2:
                    m, par, _ = i
                    if due(pool3.after(plus(i, -2), "shifted")):
                        sp.wait_ge(pool3.sem, pool3.after(plus(i, -2), "shifted"))
                    sp.dma_start(mod_b[:, par, :], mod_rows[bass.ds(times(i, 1), 1), :].broadcast_to([P, 4 * D])).then_inc(mod_in[par], 16)
                if s0:
                    b = plus(i, 2)
                    par = b[1]
                    sp.wait_ge(act0.sem, act0.after(b, "ev1"))
                    for half in range(2):
                        if due(times(plus(b, -2), H, 8 * (half + 1))):
                            sp.wait_ge(cols_ready, times(plus(b, -2), H, 8 * (half + 1)))
                        for g in range(HG):
                            at = slice(SLOT * g, SLOT * g + SLOT)
                            heads = k_pad[at, par, :, :].rearrange("p (j g) t -> p j g t", g=HG)[:, 2 * half:2 * half + 2, g, :]
                            sp.dma_start(heads, qk_t[at, par, HG + 2 * half:HG + 2 * half + 2, :]).then_inc(pad_in[half][par], 16)

            pipeline(sp, iteration)

            sp.wait_ge(cols_ready, B * H)
            sp.dma_start(gb_sb, mod_rows[:, 3 * D:].unsqueeze(0).broadcast_to([P, B, D])).then_inc(gb_in, 16)
            sp.wait_ge(table, TABLE_STEPS)
            for e in range(E):
                v = sp.value_load(tab_i[0:1, 0, e:e + 1], min_val=0, max_val=ROWS - TS)
                sp.dma_start(rows[bass.ds(v, TS), :].rearrange("(s p) w -> p s w", p=P), dummy_sb[:]).then_inc(padded, 16)
            sp.wait_ge(padded, 16 * E)
            sp.wait_ge(sent, 64 * B)
            sp.wait_ge(dummies_out, 16)

            def load(j):
                r = j[1]
                if due(times((j[0], 0, 1), 32)):
                    sp.wait_ge(y_sent[r], times((j[0], 0, 1), 32))
                v = sp.value_load(tile_row[0:1, bass.ds(times(j, 1), 1)], min_val=0, max_val=ROWS - TS)
                sp.dma_start(g_in[:, r, :, :], rows[bass.ds(v, TS), :].rearrange("(s p) w -> p s w", p=P)).then_inc(g_arrived[r], 16)

            in_fours(sp, 0, NT, load)

            for r in range(4):
                sp.wait_ge(y_sent[r], 32 * ((NT - r + 3) // 4))
            back = outs.rearrange("(b s p k) d -> b p s k d", s=NS, p=P, k=K)

            def finish(n):
                m, r, _ = n
                if due(times(plus(n, -4), 1, 1)):
                    sp.wait_ge(pool_sum, times(plus(n, -4), 1, 1))
                sp.dma_start(y_in[:, r], back[times(n, 1)]).then_inc(y_back[r], 16)

            in_fours(sp, 0, B, finish)
            for r in range(4):
                sp.wait_ge(out_done[r], 16 * (B // 4))

        @block.gpsimd
        def _(pool):
            nc.gpsimd.memset(k_pad[:, 0], 0.0).then_inc(init_pool, 1)
            nc.gpsimd.memset(k_pad[:, 1], 0.0).then_inc(init_pool, 1)
            nc.gpsimd.memset(v_aug[:], 0.0).then_inc(init_pool, 1)
            pool.wait_ge(init_pool, 3)
            nc.gpsimd.memset(v_aug[:, :, :, :, DK:DK + 1], 1.0).then_inc(init_pool, 1)
            nc.gpsimd.memset(send[:], 0.0).then_inc(init_pool, 1)
            pool.wait_ge(consts_in, 16 * N_CONST)
            pool.wait_ge(init_vec, 2)
            power = c32[:, C_POW:C_POW + NS]

            def iteration(i, s3, s2, s1, s0):
                b0, b3 = plus(i, 2), plus(i, -1)
                if s0:
                    par = b0[1]
                    pool.wait_ge(vec0.sem, vec0.after(b0, "var"))
                    nc.gpsimd.tensor_tensor(rstd0[:], ve0[:], power, ALU.pow).then_inc(pool0.sem, 1)
                    if due(pe1.after(plus(b0, -2), "tb")):
                        pool.wait_ge(pe1.sem, pe1.after(plus(b0, -2), "tb"))
                    pool.nop(nofuse=True)
                    nc.gpsimd.memset(qk_tok[:, par, :, 0:H, 3 * DK:3 * DK + 1], 0.0).then_inc(pool0.sem, 1)
                    pool.wait_ge(act0.sem, act0.after(b0, "h_hi"))
                    nc.gpsimd.tensor_tensor(ht_lo[:], ht32[:], ht_hi[:], ALU.subtract).then_inc(pool0.sem, 1)
                if s3:
                    par = b3[1]
                    pool.wait_ge(vec3.sem, vec3.after(b3, "gated"))
                    xs = x_sb[:, bass.ds(times(b3, NS), NS), :]
                    nc.gpsimd.tensor_tensor(xs, xs, gated[:], ALU.add).then_inc(pool3.sem, 1)
                if s0:
                    low_half(pool, b0, 0)
                if s3:
                    pool.wait_ge(vec3.sem, vec3.after(b3, "var"))
                    nc.gpsimd.tensor_tensor(rstd3[:], ve3[:], power, ALU.pow).then_inc(pool3.sem, 1)
                if s0:
                    low_half(pool, b0, 1)
                if s3:
                    pool.wait_ge(vec3.sem, vec3.after(b3, "xhat1"))
                    nc.gpsimd.tensor_tensor(h_s[:], xhat3[:], mod_b[:, par, 2 * D:3 * D].unsqueeze(1).broadcast_to([P, NS, D]), ALU.mult).then_inc(pool3.sem, 1)
                    pool.wait_ge(pool3.sem, pool3.after(b3, "scaled"))
                    nc.gpsimd.tensor_tensor(h_m[:], h_s[:], mod_b[:, par, D:2 * D].unsqueeze(1).broadcast_to([P, NS, D]), ALU.add).then_inc(pool3.sem, 1)
                    pool.wait_ge(vec3.sem, vec3.after(b3, "ms"))
                    nc.gpsimd.tensor_tensor(rms[:], ms[:], power, ALU.pow).then_inc(pool3.sem, 1)
                    pool.wait_ge(act3.sem, act3.after(b3, "xn_hi"))
                    words = send[:, 0, :, 0:D].bitcast(F16)
                    nc.gpsimd.tensor_tensor(words[:, :, D:2 * D], xn[:], words[:, :, 0:D], ALU.subtract).then_inc(pool3.sem, 1)
                    pool.wait_ge(vec3.sem, vec3.after(b3, "tok"))
                    pool.nop(nofuse=True)
                    for s in range(NS):
                        for k in range(K):
                            pool.indirect_dma_start(out=rows, out_offset=bass.IndirectOffsetOnAxis(ap=pos_i[:, s, k:k + 1], axis=0),
                                                    in_=send[:, k, s, :], in_offset=None).then_inc(sent, 16)

            def low_half(pool, b, s):
                par = b[1]
                pool.wait_ge(vec0.sem, vec0.after(b, f"sin{s}b"))
                nc.gpsimd.tensor_tensor(turned[:, s], turn_c[:, s], turn_s[:, s], ALU.add).then_inc(pool0.sem, 1)
                slots = qk_tok[:, par, s].rearrange("p h (c w) -> p h c w", w=DK)
                pool.wait_ge(vec0.sem, vec0.after(b, f"hi{s}"))
                nc.gpsimd.tensor_tensor(slots[:, 0:H, 1, :], turned[:, s, 0:H], slots[:, 0:H, 0, :], ALU.subtract).then_inc(pool0.sem, 1)
                pool.wait_ge(act0.sem, act0.after(b, f"khi{s}"))
                nc.gpsimd.tensor_tensor(slots[:, H:, 2, :], turned[:, s, H:], slots[:, H:, 0, :], ALU.subtract).then_inc(pool0.sem, 1)

            pipeline(pool, iteration)

            def scatter(j):
                r = j[1]
                pool.wait_ge(act_y, times(j, NS, NS))
                pool.nop(nofuse=True)
                for s in range(NS):
                    pool.indirect_dma_start(out=outs, out_offset=bass.IndirectOffsetOnAxis(ap=g_in[:, r, s, W_IDX:W_IDX + 1].bitcast(I32), axis=0),
                                            in_=y_sb[:, r, s, :], in_offset=None, bounds_check=NOUT - 1, oob_is_err=False).then_inc(y_sent[r], 16)

            in_fours(pool, 0, NT, scatter)

            def finish(n):
                m, r, _ = n
                pool.wait_ge(y_back[r], times((m, 0, 1), 16, 16))
                if due(times(plus(n, -2), 1, 1)):
                    pool.wait_ge(vec_gate, times(plus(n, -2), 1, 1))
                nc.gpsimd.tensor_tensor(ysum[:, r % 2], y_in[:, r, :, 0, :], y_in[:, r, :, 1, :], ALU.add).then_inc(pool_sum, 1)

            in_fours(pool, 0, B, finish)

        @block.scalar
        def _(act):
            act.dma_start(dummy_sb[:], dummy_in.rearrange("(s p) w -> p s w", p=P)).then_inc(consts_in, 16)
            for n, b1 in enumerate((b1a, b1b)):
                act.dma_start(b1_rows[:, n, :], b1.rearrange("e (c f) -> (e c) f", f=P)).then_inc(consts_in, 16)
            act.dma_start(lnw_sb[:], ln_w.unsqueeze(0).broadcast_to([P, D])).then_inc(moe_consts_in, 16)
            act.dma_start(bg_sb[:], bg.unsqueeze(0).broadcast_to([P, E])).then_inc(moe_consts_in, 16)
            act.dma_start(b2_sb[:], b2.unsqueeze(0).broadcast_to([P, E, D])).then_inc(moe_consts_in, 16)
            act.wait_ge(setup_pe.sem, 1)
            nc.scalar.activation(silu_c[:], banks[0][:, 0:B], ACT.Silu).then_inc(setup_act.sem, 1)
            nc.scalar.activation(b1_sb[:], banks[0][:, E * FB:3 * E * FB].rearrange("p (n c) -> p n c", n=2), ACT.Copy).then_inc(setup_act.sem, 1)
            nc.scalar.preload_act_table(ACT.Exp)
            act.wait_ge(setup_pe.sem, 2)
            nc.scalar.activation(w_hi[:], banks[2][:].rearrange("p (n d) -> p n d", d=D), ACT.Copy).then_inc(setup_act.sem, 1)
            act.wait_ge(setup_vec.sem, len(setup_vec.names))
            act.dma_start(mod_rows, mod_sb[:]).then_inc(mod_out, 16)
            act.wait_ge(consts_in, 16 * N_CONST)
            act.dma_start(rows[E * REGION:, :].rearrange("(s p) w -> p s w", p=P), dummy_sb[:]).then_inc(dummies_out, 16)
            act.wait_ge(init_pool, 4)

            def iteration(i, s3, s2, s1, s0):
                b0, b1, b3 = plus(i, 2), plus(i, 1), plus(i, -1)
                par0 = b0[1]
                for k in range(H):
                    if s2:
                        n = times(i, H, k)
                        act.wait_ge(cols_ready, times(i, H, k + 1))
                        if due(times(i, H, k - 3)):
                            act.wait_ge(probs_used, times(i, H, k - 3))
                        nc.scalar.activation(probs[:, k % 4], col_bank[k % 2][:, 0:S + P], ACT.Exp, scale=SM_SCALE).then_inc(probs_ready, 1)
                        if k % HG == 0 and k:
                            save_group(i, k // HG - 1)
                    if k == 3 and s0:
                        act.wait_ge(pe0.sem, pe0.after(b0, "x_t"))
                        at = bass.ds(times(b0, 1), 1)
                        nc.scalar.activation(ht32[:], chain_a[:, 0:S], ACT.Identity, scale=scale_in[:, at], bias=shift_in[:, at]).then_inc(act0.sem, 1)
                        nc.scalar.activation(ht_hi[:], chain_a[:, 0:S], ACT.Identity, scale=scale_in[:, at], bias=shift_in[:, at]).then_inc(act0.sem, 1)
                    if k == 1 and s1:
                        act.wait_ge(act0.sem, act0.after(b1, "v1"))
                        par = b1[1]
                        nc.scalar.activation(v_aug[:, par, :, :, 0:DK], v_sb[:, par].rearrange("p s (h w) -> p s h w", w=DK), ACT.Copy).then_inc(act1.sem, 1)
                    if k == 2 and s2:
                        save_queries(i, 1)
                    if k in (6, 8) and s0:
                        s = (k - 6) // 2
                        act.wait_ge(pe0.sem, pe0.after(b0, f"proj{s}"))
                        proj = (chain_b, chain_a)[s]
                        nc.scalar.activation(v_sb[:, par0, s, :], proj[:, 2 * D:3 * D], ACT.Copy).then_inc(act0.sem, 1)
                        act.wait_ge(pool0.sem, pool0.after(b0, f"turn{s}"))
                        slots = qk_tok[:, par0, s].rearrange("p h (c w) -> p h c w", w=DK)
                        nc.scalar.activation(slots[:, H:, 0:2, :], turned[:, s, H:].unsqueeze(2).broadcast_to([P, H, 2, DK]), ACT.Copy).then_inc(act0.sem, 1)
                    if k == 9 and s1:
                        save_queries(b1, 0)
                    if k in (11, 13) and s0:
                        s = (k - 11) // 2
                        act.wait_ge(pe0.sem, pe0.after(b0, f"t{s}"))
                        half = (chain_a16, chain_b16)[s]
                        nc.scalar.activation(qk_t[:, par0, :, P * s:P * s + P], half.rearrange("p (j t) -> p j t", t=P), ACT.Copy).then_inc(act0.sem, 1)
                    if s3:
                        if k == 4:
                            act.wait_ge(pe3.sem, pe3.after(b3, "on_t"))
                            nc.scalar.activation(on_hi[:], tail_bank[:, 0:S], ACT.Copy).then_inc(act3.sem, 1)
                        if k == 10:
                            act.wait_ge(pool3.sem, pool3.after(b3, "shifted"))
                            for s in range(NS):
                                nc.scalar.activation(square[:, s], h_m[:, s], ACT.Square, accum_out=ssum[:, s:s + 1]).then_inc(act3.sem, 1)
                        if k == 12:
                            act.wait_ge(pe3.sem, pe3.after(b3, "xn_t"))
                            nc.scalar.activation(xn_t[:], tail_bank[:, 0:S], ACT.Copy).then_inc(act3.sem, 1)
                        if k == 14:
                            act.wait_ge(vec3.sem, vec3.after(b3, "gap"))
                            nc.scalar.activation(egap[:], gap[:], ACT.Exp).then_inc(act3.sem, 1)
                            if due(times(b3, 64)):
                                act.wait_ge(sent, times(b3, 64))
                            nc.scalar.activation(send[:, 0, :, 0:D].bitcast(F16)[:, :, 0:D], xn[:], ACT.Copy).then_inc(act3.sem, 1)
                if s2:
                    save_group(i, HG - 1)

            def save_group(b, j):
                act.wait_ge(probs_used, times(b, H, HG * (j + 1)))
                nc.scalar.activation(o_t[:, b[1], j, :], o_bank[:, 0:S], ACT.Copy).then_inc(group_saved, 1)

            def save_queries(b, half):
                act.wait_ge(pe1.sem, pe1.after(b, "t" + "ab"[half]))
                nc.scalar.activation(q_max[:, b[1], 2 * half:2 * half + 2, :], chain_b16[:, 0:2 * S].rearrange("p (j t) -> p j t", t=S), ACT.Copy).then_inc(act1.sem, 1)

            pipeline(act, iteration)

            nc.scalar.preload_act_table(ACT.Silu)
            act.wait_ge(table, TABLE_STEPS)

            def save_x(j):
                act.wait_ge(pe_x, times(j, 1, 1))
                if due(times(plus(j, -2), FB, FB)):
                    act.wait_ge(pe_ab, times(plus(j, -2), FB, FB))
                nc.scalar.activation(xt[:, j[1] % 2], (chain_a16, chain_b16)[j[1] % 2][:, 0:2 * TS].rearrange("p (h t) -> p h t", t=TS), ACT.Copy).then_inc(act_x, 1)

            def high(j, f):
                act.wait_ge(vec_h, times(j, FB, f + 1))
                if due(times(plus(j, -2), 1, 1)):
                    act.wait_ge(pe_y, times(plus(j, -2), 1, 1))
                nc.scalar.activation(hh[:, j[1] % 2, f], h32[:, f], ACT.Copy).then_inc(act_hh, 1)

            def weigh(j):
                r = j[1]
                if due(times((j[0], 0, 1), 32)):
                    act.wait_ge(y_sent[r], times((j[0], 0, 1), 32))
                act.wait_ge(vec_y, times(j, 1, 1))
                for s in range(NS):
                    nc.scalar.activation(y_sb[:, r, s], yb[:, r % 2, s], ACT.Copy, scale=g_in[:, r, s, W_WGT:W_WGT + 1]).then_inc(act_y, 1)

            def tile(j, more=True):
                e = act.value_load(tile_e[0:1, bass.ds(times(j, 1), 1)], min_val=0, max_val=E - 1)
                for f in range(FB):
                    act.wait_ge(pe_ab, times(j, FB, f + 1))
                    if due(times(plus(j, -1), FB, f + 1)):
                        act.wait_ge(vec_h, times(plus(j, -1), FB, f + 1))
                    nc.scalar.activation(silu_a[:, f], banks[f][:, 0:TS], ACT.Silu, bias=b1_sb[:, 0, bass.ds(e * FB + f, 1)]).then_inc(act_silu, 1)
                    if f == 2 and more:
                        save_x(plus(j, 1))
                    if f:
                        high(j, f - 1)
                high(j, FB - 1)

            def tile_and_last(j, more=True):
                tile(j, more)
                weigh(plus(j, -1))

            save_x((0, 0, 4))
            tile((0, 0, 4))
            in_fours(act, 1, NT - 1, tile_and_last)
            tile_and_last(((NT - 1) // 4, (NT - 1) % 4, 4), False)
            weigh(((NT - 1) // 4, (NT - 1) % 4, 4))

            out_v = out.rearrange("b (s p) d -> b p s d", p=P)

            def store(n):
                m, r, _ = n
                act.wait_ge(vec_res, times(n, 1, 1))
                act.dma_start(out_v[times(n, 1)], res[:, r]).then_inc(out_done[r], 16)

            in_fours(act, 0, B, store)

        @block.vector
        def _(vec):
            nc.vector.memset(qk_tok[:], 0.0).then_inc(init_vec, 1)
            vec.wait_ge(init_vec, 1)
            nc.vector.memset(qk_tok[:, :, :, H:, 3 * DK:3 * DK + 1], 1.0).then_inc(init_vec, 1)

            vec.wait_ge(setup_act.sem, 3)
            nc.vector.tensor_tensor(w_lo[:], banks[2][:].rearrange("p (n d) -> p n d", d=D), w_hi[:], ALU.subtract).then_inc(setup_vec.sem, 1)
            vec.wait_ge(setup_pe.sem, 3)
            nc.vector.tensor_scalar(scale_in[:], banks[1][:, B:2 * B], 1.0, None, ALU.add).then_inc(setup_vec.sem, 1)
            nc.vector.tensor_copy(shift_in[:], banks[1][:, 0:B]).then_inc(setup_vec.sem, 1)
            nc.vector.tensor_copy(mod_sb[:], banks[3][0:B, :]).then_inc(setup_vec.sem, 1)
            gate = mod_sb[:].rearrange("p (g d) -> p g d", d=D)
            vec.wait_ge(setup_vec.sem, 4)
            for n, g in ((0, 0), (1, 3)):
                nc.vector.tensor_scalar(square[0:B, n, :], gate[:, g], -1.0, None, ALU.mult).then_inc(setup_vec.sem, 1)
            vec.wait_ge(setup_vec.sem, 6)
            for n, g in ((0, 0), (1, 3)):
                nc.vector.scalar_tensor_tensor(out=gated[0:B, n, :], in0=gate[:, g], scalar=0.25, in1=square[0:B, n, :], op0=ALU.max, op1=ALU.max).then_inc(setup_vec.sem, 1)
            for n, g in ((0, 0), (1, 3)):
                nc.vector.tensor_scalar(h_s[0:B, n, :], gate[:, g], 0.0, 2.0, ALU.is_ge, ALU.mult).then_inc(setup_vec.sem, 1)
            vec.wait_ge(setup_vec.sem, 10)
            for n, g in ((0, 0), (1, 3)):
                nc.vector.scalar_tensor_tensor(out=gate[:, g], in0=h_s[0:B, n, :], scalar=-1.0, in1=gated[0:B, n, :], op0=ALU.add, op1=ALU.mult).then_inc(setup_vec.sem, 1)
            nc.vector.tensor_scalar(gate[:, 2], gate[:, 2], 1.0, None, ALU.add).then_inc(setup_vec.sem, 1)
            vec.wait_ge(consts_in, 16 * N_CONST)
            nc.vector.tensor_copy(filled[:], c32[:, C_BASE:C_BASE + E]).then_inc(init_vec, 1)
            nc.vector.tensor_copy(tok[:].rearrange("p k s -> p (k s)"), c32[:, C_TOK:C_TOK + K * NS]).then_inc(init_vec, 1)
            cos = c32[:, C_COS:C_COS + 8].rearrange("p (s w) -> p s w", w=DK // 2)
            sin = c32[:, C_SIN:C_SIN + 8].rearrange("p (s w) -> p s w", w=DK // 2)

            def split_weights(b):
                m, par, _ = b
                at = bass.ds(times(b, CHUNK), CHUNK)
                vec.wait_ge(wstage_in[par], times((m, 0, 1), 48, 48))
                nc.vector.tensor_copy(we_hi[:, :, at], wstage[:, par]).then_inc(vec0.sem, 1)
                vec.wait_ge(vec0.sem, vec0.after(b, "w_hi"))
                nc.vector.tensor_tensor(we_lo[:, :, at], wstage[:, par], we_hi[:, :, at], ALU.subtract).then_inc(vec0.sem, 1)

            def norm(b, stage, vecs, pools, var, st, mv, ve, rstd, xhat):
                xs = [x_sb[:, bass.ds(times(b, NS, s), 1), :].rearrange("p o d -> p (o d)") for s in range(NS)]
                if stage == 0:
                    for s in range(NS):
                        nc.vector.bn_stats(st[:, s], xs[s]).then_inc(vecs.sem, 1)
                    vec.wait_ge(vecs.sem, vecs.after(b, "stats1"))
                    vec.nop(nofuse=True)
                    for s in range(NS):
                        nc.vector.bn_aggr(mv[:, s], st[:, s]).then_inc(vecs.sem, 1)
                    vec.wait_ge(vecs.sem, vecs.after(b, "aggr1"))
                    nc.vector.tensor_scalar(ve[:], mv[:, :, 1], EPS_LN, None, ALU.add).then_inc(vecs.sem, 1)
                else:
                    vec.wait_ge(pools.sem, pools.after(b, "rstd"))
                    for s in range(NS):
                        nc.vector.tensor_scalar(xhat[:, s], xs[s], mv[:, s, 0:1], rstd[:, s:s + 1], ALU.subtract, ALU.mult).then_inc(vecs.sem, 1)

            def norm0(b, part):
                norm(b, part, vec0, pool0, "var", st0, mv0, ve0, rstd0, xhat0)

            def norm3(b, part):
                norm(b, part, vec3, pool3, "var", st3, mv3, ve3, rstd3, xhat3)

            def turn(b, s):
                qk = (chain_b, chain_a)[s][:, 0:2 * D].rearrange("p (h w) -> p h w", w=DK)
                w = DK // 2
                vec.wait_ge(act0.sem, act0.after(b, f"v{s}"))
                halves = (chain_b, chain_a)[s][:, 0:2 * D].rearrange("p (h w) -> p h w", w=w)
                nc.vector.tensor_tensor(turn_c[:, s].rearrange("p h (u w) -> p (h u) w", w=w), halves,
                                        cos[:, s].unsqueeze(1).broadcast_to([P, 4 * H, w]), ALU.mult).then_inc(vec0.sem, 1)
                sn = sin[:, s].unsqueeze(1).broadcast_to([P, 2 * H, w])
                nc.vector.scalar_tensor_tensor(out=turn_s[:, s, :, 0:w], in0=qk[:, :, w:], scalar=-1.0, in1=sn, op0=ALU.mult, op1=ALU.mult).then_inc(vec0.sem, 1)
                nc.vector.tensor_tensor(turn_s[:, s, :, w:], qk[:, :, 0:w], sn, ALU.mult).then_inc(vec0.sem, 1)

            def high_queries(b, s):
                vec.wait_ge(pool0.sem, pool0.after(b, f"turn{s}"))
                slots = qk_tok[:, b[1], s].rearrange("p h (c w) -> p h c w", w=DK)
                nc.vector.tensor_copy(slots[:, 0:H, 0:3:2, :], turned[:, s, 0:H].unsqueeze(2).broadcast_to([P, H, 2, DK])).then_inc(vec0.sem, 1)

            def max_of(b, k):
                vec.wait_ge(rows_ready, times(b, H, k + 1))
                nc.vector.tensor_reduce(nmax[:, k], row_bank[k % 2][:, 0:3 * P].rearrange("p (c t) -> p c t", t=P), AX.X, ALU.max, negate=True).then_inc(max_ready, 1)

            def place_max(b, half):
                vec.wait_ge(max_ready, times(b, H, 8 * (half + 1)))
                heads = slice(8 * half, 8 * half + 8)
                nc.vector.tensor_copy(qk_tok[:, b[1], 0, heads, 3 * DK], nmax[:, heads, 0]).then_inc(vec1.sem, 1)
                nc.vector.tensor_tensor(qk_tok[:, b[1], 1, heads, 3 * DK], nmax[:, heads, 1], nmax[:, heads, 2], ALU.min).then_inc(vec1.sem, 1)

            def divide(b, s):
                vec.wait_ge(pe3.sem, pe3.after(b, f"o{s}"))
                o = tail_bank[:].rearrange("p (h w) -> p h w", w=SLOT)
                nc.vector.reciprocal(rsum[:, s], o[:, :, DK]).then_inc(vec3.sem, 1)
                vec.wait_ge(vec3.sem, vec3.after(b, f"rs{s}"))
                nc.vector.tensor_tensor(o_n[:, s].rearrange("p (h w) -> p h w", w=DK), o[:, :, 0:DK],
                                        rsum[:, s].unsqueeze(2).broadcast_to([P, H, DK]), ALU.mult).then_inc(vec3.sem, 1)

            def low_out(b):
                vec.wait_ge(act3.sem, act3.after(b, "on_hi"))
                nc.vector.tensor_tensor(on_lo[:], tail_bank[:, 0:S], on_hi[:], ALU.subtract).then_inc(vec3.sem, 1)

            def gate_out(b):
                m, par, _ = b
                vec.wait_ge(pe3.sem, pe3.after(b, "wo"))
                vec.wait_ge(mod_in[par], times((m, 0, 1), 16, 16))
                nc.vector.tensor_tensor(gated[:], tail_bank[:, 0:S].rearrange("p (s d) -> p s d", d=D),
                                        mod_b[:, par, 0:D].unsqueeze(1).broadcast_to([P, NS, D]), ALU.mult).then_inc(vec3.sem, 1)

            def rms_norm(b):
                vec.wait_ge(act3.sem, act3.after(b, "sq1"))
                nc.vector.tensor_scalar(ms[:], ssum[:], 1.0 / D, EPS_RMS, ALU.mult, ALU.add).then_inc(vec3.sem, 1)
                vec.wait_ge(pool3.sem, pool3.after(b, "rms"))
                for s in range(NS):
                    nc.vector.scalar_tensor_tensor(out=xn[:, s], in0=h_m[:, s], scalar=rms[:, s:s + 1], in1=lnw_sb[:], op0=ALU.mult, op1=ALU.mult).then_inc(vec3.sem, 1)

            def route(b):
                vec.wait_ge(pe3.sem, pe3.after(b, "logits"))
                nc.vector.tensor_tensor(logits[:], tail_bank[:, 0:NS * E].rearrange("p (s e) -> p s e", e=E),
                                        bg_sb[:].unsqueeze(1).broadcast_to([P, NS, E]), ALU.add).then_inc(vec3.sem, 1)
                vec.wait_ge(vec3.sem, vec3.after(b, "logits"))
                vec.nop(nofuse=True)
                for s in range(NS):
                    nc.vector.max(top[:, s], logits[:, s]).then_inc(vec3.sem, 1)
                vec.wait_ge(vec3.sem, vec3.after(b, "max1"))
                vec.nop(nofuse=True)
                for s in range(NS):
                    nc.vector.max_index(top_i[:, s], top[:, s], logits[:, s]).then_inc(vec3.sem, 1)
                vec.wait_ge(vec3.sem, vec3.after(b, "idx1"))
                nc.vector.tensor_copy(top_f[:], top_i[:, :, 0:K]).then_inc(vec3.sem, 1)
                vec.wait_ge(vec3.sem, vec3.after(b, "idxf"))
                nc.vector.tensor_tensor(chosen[:], c32[:, C_E:C_E + E].unsqueeze(1).unsqueeze(1).broadcast_to([P, NS, K, E]),
                                        top_f[:].unsqueeze(3).broadcast_to([P, NS, K, E]), ALU.is_equal).then_inc(vec3.sem, 1)
                vec.wait_ge(vec3.sem, vec3.after(b, "chosen"))
                nc.vector.tensor_tensor(member[:], chosen[:, :, 0], chosen[:, :, 1], ALU.add).then_inc(vec3.sem, 1)
                nc.vector.tensor_tensor(gap[:], top[:, :, 1], top[:, :, 0], ALU.subtract).then_inc(vec3.sem, 1)

            def place(b):
                vec.wait_ge(act3.sem, act3.after(b, "egap"))
                nc.vector.tensor_scalar(den[:], egap[:], 1.0, None, ALU.add).then_inc(vec3.sem, 1)
                vec.wait_ge(vec3.sem, vec3.after(b, "den"))
                if due(times(b, 64)):
                    vec.wait_ge(sent, times(b, 64))
                nc.vector.reciprocal(send[:, 0, :, W_WGT], den[:]).then_inc(vec3.sem, 1)
                vec.wait_ge(vec3.sem, vec3.after(b, "w1"))
                nc.vector.tensor_tensor(send[:, 1, :, W_WGT], send[:, 0, :, W_WGT], egap[:], ALU.mult).then_inc(vec3.sem, 1)
                vec.wait_ge(pe3.sem, pe3.after(b, "ranks"))
                nc.vector.tensor_tensor(rank[:], tail_bank[:, 0:NS * E].rearrange("p (s e) -> p s e", e=E),
                                        filled[:].unsqueeze(1).broadcast_to([P, NS, E]), ALU.add).then_inc(vec3.sem, 1)
                vec.wait_ge(vec3.sem, vec3.after(b, "rank"))
                nc.vector.tensor_tensor(filled[:], filled[:], tail_bank[:, NS * E:(NS + 1) * E], ALU.add).then_inc(vec3.sem, 1)
                nc.vector.tensor_tensor(at_e[:], chosen[:], rank[:].unsqueeze(2).broadcast_to([P, NS, K, E]), ALU.mult).then_inc(vec3.sem, 1)
                vec.wait_ge(vec3.sem, vec3.after(b, "at"))
                nc.vector.tensor_reduce(pos_f[:], at_e[:], AX.X, ALU.add).then_inc(vec3.sem, 1)
                vec.wait_ge(vec3.sem, vec3.after(b, "pos_f"))
                nc.vector.tensor_copy(pos_i[:], pos_f[:]).then_inc(vec3.sem, 1)
                vec.wait_ge(pool3.sem, pool3.after(b, "xn_lo"))
                nc.vector.tensor_copy(send[:, 1, :, 0:D], send[:, 0, :, 0:D]).then_inc(vec3.sem, 1)
                nc.vector.tensor_copy(send[:, :, :, W_IDX].bitcast(I32), tok[:]).then_inc(vec3.sem, 1)
                vec.wait_ge(vec3.sem, vec3.after(b, "tok"))
                nc.vector.tensor_scalar(tok[:], tok[:], float(S * K), None, ALU.add).then_inc(vec3.sem, 1)

            def iteration(i, s3, s2, s1, s0):
                b0, b1, b3 = plus(i, 2), plus(i, 1), plus(i, -1)
                if s0:
                    if isinstance(i[0], int) and times(i, 1) == -2:
                        vec.wait_ge(x_in0, 16)
                    if isinstance(i[0], int) and times(i, 1) == 0:
                        vec.wait_ge(x_in1, 16)
                    norm0(b0, 0)
                for k in range(H):
                    if k == 0 and s3:
                        divide(b3, 0)
                    if k == 1 and s0:
                        norm0(b0, 1)
                    if s1:
                        max_of(b1, k)
                    if k == 8 and s1:
                        place_max(b1, 0)
                    if s0:
                        if k in (6, 8):
                            turn(b0, (k - 6) // 2)
                        if k in (7, 9):
                            high_queries(b0, (k - 7) // 2)
                    if s3:
                        if k == 2:
                            divide(b3, 1)
                        if k == 4:
                            low_out(b3)
                        if k == 6:
                            gate_out(b3)
                        if k == 7:
                            vec.wait_ge(pool3.sem, pool3.after(b3, "resid"))
                            norm3(b3, 0)
                        if k == 8:
                            norm3(b3, 1)
                        if k == 10:
                            rms_norm(b3)
                        if k == 13:
                            route(b3)
                        if k == 15:
                            place(b3)
                if s1:
                    place_max(b1, 1)
                if s0:
                    split_weights(b0)

            vec.wait_ge(moe_consts_in, 16 * N_MOE_CONST)
            pipeline(vec, iteration)

            base, iota_j = c32[:, C_BASE:C_BASE + E], c32[:, C_J:C_J + NT + 1]
            vec.wait_ge(vec3.sem, vec3.after(number(B - 1), "tok_on"))
            nc.vector.tensor_copy(tab_i[:, 0], filled[:]).then_inc(table, 1)
            vec.wait_ge(table, 1)
            nc.vector.scalar_tensor_tensor(out=tab[:, 0], in0=filled[:], scalar=float(TS - 1), in1=base, op0=ALU.add, op1=ALU.subtract).then_inc(table, 1)
            vec.wait_ge(table, 2)
            nc.vector.tensor_copy(tab_i[:, 1], tab[:, 0]).then_inc(table, 1)
            vec.wait_ge(table, 3)
            nc.vector.tensor_scalar(tab_i[:, 1], tab_i[:, 1], TS.bit_length() - 1, None, ALU.logical_shift_right).then_inc(table, 1)
            vec.wait_ge(table, 4)
            nc.vector.tensor_copy(tab[:, 1], tab_i[:, 1]).then_inc(table, 1)
            vec.wait_ge(table, 5)
            nc.vector.memset(tab[:, 2], 0.0).then_inc(table, 1)
            vec.wait_ge(table, 6)
            nc.vector.tensor_tensor_scan(tab[:, 3], tab[:, 1], tab[:, 2], 0.0, ALU.add, ALU.add).then_inc(table, 1)
            ends = tab[:, 3].unsqueeze(1).broadcast_to([P, NT + 1, E])
            vec.wait_ge(table, 7)
            nc.vector.tensor_tensor(cmp_j[:], iota_j.unsqueeze(2).broadcast_to([P, NT + 1, E]), ends, ALU.is_ge).then_inc(table, 1)
            vec.wait_ge(table, 8)
            nc.vector.tensor_reduce(tj[:, 0], cmp_j[:], AX.X, ALU.add).then_inc(table, 1)
            vec.wait_ge(table, 9)
            nc.vector.tensor_tensor(cmp_j[:], cmp_j[:], tab[:, 1].unsqueeze(1).broadcast_to([P, NT + 1, E]), ALU.mult).then_inc(table, 1)
            vec.wait_ge(table, 10)
            nc.vector.tensor_reduce(tj[:, 1], cmp_j[:], AX.X, ALU.add).then_inc(table, 1)
            vec.wait_ge(table, 11)
            nc.vector.tensor_tensor(tj[:, 2], iota_j, tj[:, 1], ALU.subtract).then_inc(table, 1)
            vec.wait_ge(table, 12)
            nc.vector.tensor_scalar(tj[:, 3], tj[:, 0], float(REGION), None, ALU.mult).then_inc(table, 1)
            vec.wait_ge(table, 13)
            nc.vector.scalar_tensor_tensor(out=tj[:, 4], in0=tj[:, 2], scalar=float(TS), in1=tj[:, 3], op0=ALU.mult, op1=ALU.add).then_inc(table, 1)
            vec.wait_ge(table, 14)
            nc.vector.tensor_scalar(tj[:, 4], tj[:, 4], float(E * REGION), None, ALU.min).then_inc(table, 1)
            vec.wait_ge(table, 15)
            nc.vector.tensor_copy(tile_row[:], tj[:, 4]).then_inc(table, 1)
            vec.wait_ge(table, 16)
            nc.vector.tensor_scalar(tj[:, 0], tj[:, 0], float(E - 1), None, ALU.min).then_inc(table, 1)
            vec.wait_ge(table, 17)
            nc.vector.tensor_copy(tile_e[:], tj[:, 0]).then_inc(table, 1)
            vec.wait_ge(table, TABLE_STEPS)
            vec.wait_ge(vec0.sem, vec0.after(number(B - 1), "w_lo"))

            def low(j, f):
                vec.wait_ge(act_hh, times(j, FB, f + 1))
                nc.vector.tensor_tensor(hl[:, j[1] % 2, f], h32[:, f], hh[:, j[1] % 2, f], ALU.subtract).then_inc(vec_hl, 1)

            def tile(j):
                e = vec.value_load(tile_e[0:1, bass.ds(times(j, 1), 1)], min_val=0, max_val=E - 1)
                for f in range(FB):
                    vec.wait_ge(act_silu, times(j, FB, f + 1))
                    nc.vector.scalar_tensor_tensor(out=h32[:, f], in0=banks[f][:, TS:2 * TS], scalar=b1_sb[:, 1, bass.ds(e * FB + f, 1)],
                                                   in1=silu_a[:, f], op0=ALU.add, op1=ALU.mult).then_inc(vec_h, 1)
                    if f:
                        low(j, f - 1)
                low(j, FB - 1)

            def bias_out(j):
                e = vec.value_load(tile_e[0:1, bass.ds(times(j, 1), 1)], min_val=0, max_val=E - 1)
                vec.wait_ge(pe_y, times(j, 1, 1))
                if due(times(plus(j, -2), NS, NS)):
                    vec.wait_ge(act_y, times(plus(j, -2), NS, NS))
                y = (o_bank, tail_bank)[j[1] % 2]
                nc.vector.tensor_tensor(yb[:, j[1] % 2], y[:, 0:NS * D].rearrange("p (s d) -> p s d", d=D),
                                        b2_sb[:, bass.ds(e, 1), :].broadcast_to([P, NS, D]), ALU.add).then_inc(vec_y, 1)

            def tile_and_last(j):
                tile(j)
                bias_out(plus(j, -1))

            tile((0, 0, 4))
            in_fours(vec, 1, NT, tile_and_last)
            bias_out(((NT - 1) // 4, (NT - 1) % 4, 4))

            vec.wait_ge(gb_in, 16)

            def finish(n):
                m, r, _ = n
                vec.wait_ge(pool_sum, times(n, 1, 1))
                nc.vector.tensor_tensor(ygate[:, r % 2], ysum[:, r % 2], gb_sb[:, bass.ds(times(n, 1), 1), :].broadcast_to([P, NS, D]), ALU.mult).then_inc(vec_gate, 1)
                vec.wait_ge(vec_gate, times(n, 1, 1))
                if due(times((m, 0, 1), 16)):
                    vec.wait_ge(out_done[r], times((m, 0, 1), 16))
                nc.vector.tensor_tensor(res[:, r], ygate[:, r % 2], x_sb[:, bass.ds(times(n, NS), NS), :], ALU.add).then_inc(vec_res, 1)

            in_fours(vec, 0, B, finish)

        @block.tensor
        def _(pe):
            mm = nc.tensor.matmul

            def halves(o, l_hi, l_lo, r_hi, r_lo, start=True, stop=True):
                mm(o, l_hi, r_hi, start=start, stop=False, skip_group_check=True)
                mm(o, l_hi, r_lo, start=False, stop=False, skip_group_check=True)
                return mm(o, l_lo, r_hi, start=False, stop=stop, skip_group_check=True)

            pe.wait_ge(consts_in, 16 * N_CONST)
            for n in range(2):
                at = slice(E * FB * (n + 1), E * FB * (n + 2))
                nc.tensor.transpose(banks[0][:, at], b1_rows[:, n, :], ident32[0:E * FB, 0:E * FB])
            nc.tensor.transpose(banks[0][:, 0:B], c_sb[:], ident32[0:B, 0:B]).then_inc(setup_pe.sem, 1)
            for n in range(4):
                t = nc.tensor.transpose(banks[2][:, D * n:D * n + D], wraw[:, n, :], ident32[:])
            t.then_inc(setup_pe.sem, 1)
            pe.wait_ge(setup_act.sem, 1)
            for n in range(2):
                mm(banks[1][:, B * n:B * n + B], wmod_sb[:, D * n:D * n + D], silu_c[:], start=(n == 0), stop=True, skip_group_check=True)
            mm(banks[3][0:B, :], silu_c[:], wmod_sb[:, 2 * D:6 * D], start=True, stop=True).then_inc(setup_pe.sem, 1)
            pe.wait_ge(setup_vec.sem, 4)
            pe.wait_ge(init_vec, 4)
            pe.wait_ge(init_pool, 5)

            def project(b, s):
                at = slice(P * s, P * s + P)
                o = (chain_b, chain_a)[s][:, 0:3 * D]
                halves(o, ht_hi[:, at], ht_lo[:, at], w_hi[:, 0:3, :].rearrange("p n d -> p (n d)"), w_lo[:, 0:3, :].rearrange("p n d -> p (n d)")).then_inc(pe0.sem, 1)

            def turn_tile(b, s):
                o = (chain_a16, chain_b16)[s]
                tok_q = qk_tok[:, b[1], s].rearrange("p (j g) w -> p j (g w)", g=HG)
                for j in range(2 * HG):
                    t = nc.tensor.transpose(o[:, P * j:P * j + P], tok_q[:, j, :], ident16)
                t.then_inc(pe0.sem, 1)

            def turn_max(b, half):
                for j in range(2):
                    for s in range(NS):
                        q = qk_tok[:, b[1], s].rearrange("p (j g) w -> p j (g w)", g=HG)[:, 2 * half + j, :]
                        t = nc.tensor.transpose(chain_b16[:, S * j + P * s:S * j + P * s + P], q, ident16)
                t.then_inc(pe1.sem, 1)

            def masks(o, mask):
                diagonal = o[:, 0:4 * P].rearrange("p (c t) -> p c t", t=2 * P)[:, :, 0:P]
                return mm(diagonal, ident16, mask.unsqueeze(1).broadcast_to([P, 2, P]), start=False, stop=True, skip_group_check=True)

            def scores_by_query(b, k):
                j, par = k // HG, b[1]
                if k % 8 == 0:
                    pe.wait_ge(pad_in[k // 8][par], times((b[0], 0, 1), 64, 64))
                if due(times(b, H, k - 1)):
                    pe.wait_ge(max_ready, times(b, H, k - 1))
                o = row_bank[k % 2]
                mm(o[:, 0:P], qk_t[:, par, j, 0:P], k_pad[:, par, k, 0:P], start=True, stop=False, skip_group_check=True)
                mm(o[:, P:3 * P], qk_t[:, par, j, P:], k_pad[:, par, k, :], start=False, stop=False, skip_group_check=True)
                masks(o, mask_q).then_inc(rows_ready, 1)

            def scores_by_key(b, k):
                j, par = k // HG, b[1]
                if k % 8 == 0:
                    pe.wait_ge(act1.sem, act1.after(b, "ev" + "ab"[k // 8]))
                if due(times(b, H, k - 1)):
                    pe.wait_ge(probs_ready, times(b, H, k - 1))
                o = col_bank[k % 2]
                mm(o[:, 0:S], k_pad[:, par, k, 0:P], q_max[:, par, j, :], start=True, stop=False, skip_group_check=True)
                mm(o[:, S:S + P], k_pad[:, par, k, P:], q_max[:, par, j, P:], start=False, stop=False, skip_group_check=True)
                masks(o, mask_k).then_inc(cols_ready, 1)

            def values(b, k):
                g, par = k % HG, b[1]
                if g == 0:
                    if due(times(b, HG, k // HG)):
                        pe.wait_ge(group_saved, times(b, HG, k // HG))
                pe.wait_ge(probs_ready, times(b, H, k + 1))
                at = slice(SLOT * g, SLOT * g + SLOT)
                mm(o_bank[at, 0:S], v_aug[:, par, 0, k, :], probs[:, k % 4, 0:S], start=True, stop=False, skip_group_check=True)
                mm(o_bank[at, P:S], v_aug[:, par, 1, k, :], probs[:, k % 4, S:], start=False, stop=True, skip_group_check=True).then_inc(probs_used, 1)

            def out_rows(b, s):
                if s == 0:
                    pe.wait_ge(group_saved, times(b, HG, HG))
                    if due(vec3.after(plus(b, -1), "filled")):
                        pe.wait_ge(vec3.sem, vec3.after(plus(b, -1), "filled"))
                else:
                    pe.wait_ge(vec3.sem, vec3.after(b, "on0"))
                for j in range(HG):
                    t = nc.tensor.transpose(tail_bank[:, P * j:P * j + P], o_t[:, b[1], j, P * s:P * s + P], ident32[:])
                t.then_inc(pe3.sem, 1)

            def ranks(b):
                pe.wait_ge(vec3.sem, vec3.after(b, "member"))
                two = member[:].rearrange("p s e -> p (s e)")
                mm(tail_bank[:, 0:2 * E], before16, two, start=True, stop=False, skip_group_check=True)
                mm(tail_bank[:, E:2 * E], ones16, member[:, 0], start=False, stop=False, skip_group_check=True)
                mm(tail_bank[:, 2 * E:3 * E], ones16, member[:, 0], start=False, stop=False, skip_group_check=True)
                mm(tail_bank[:, 2 * E:3 * E], ones16, member[:, 1], start=False, stop=True, skip_group_check=True).then_inc(pe3.sem, 1)

            def iteration(i, s3, s2, s1, s0):
                b0, b1, b3 = plus(i, 2), plus(i, 1), plus(i, -1)
                for k in range(H):
                    if s1:
                        scores_by_query(b1, k)
                    if s2:
                        scores_by_key(i, k)
                        if k:
                            values(i, k - 1)
                    if k == 2 and s2:
                        pe.wait_ge(vec1.sem, vec1.after(i, "m1b"))
                        if s1:
                            pe.wait_ge(act0.sem, act0.after(b1, "ev1"))
                        turn_max(i, 1)
                    if k == 9 and s1:
                        if s0:
                            pe.wait_ge(vec0.sem, vec0.after(b0, "sin0b"))
                        elif s2:
                            pe.wait_ge(act1.sem, act1.after(i, "evb"))
                        pe.wait_ge(vec1.sem, vec1.after(b1, "m1a"))
                        turn_max(b1, 0)
                    if s0:
                        if k == 3:
                            pe.wait_ge(vec0.sem, vec0.after(b0, "xhat1"))
                            if due(act0.after(plus(b0, -1), "ev0")):
                                pe.wait_ge(act0.sem, act0.after(plus(b0, -1), "ev0"))
                            for s in range(NS):
                                t = nc.tensor.transpose(chain_a[:, P * s:P * s + P], xhat0[:, s], ident32[:])
                            t.then_inc(pe0.sem, 1)
                        if k == 5:
                            pe.wait_ge(pool0.sem, pool0.after(b0, "h_lo"))
                            if due(act0.after(plus(b0, -1), "ev1")):
                                pe.wait_ge(act0.sem, act0.after(plus(b0, -1), "ev1"))
                            if s2:
                                pe.wait_ge(act1.sem, act1.after(i, "evb"))
                            project(b0, 0)
                        if k == 7:
                            project(b0, 1)
                        if k == 11:
                            pe.wait_ge(vec0.sem, vec0.after(b0, "sin1b"))
                            pe.wait_ge(pool0.sem, pool0.after(b0, "klo0"))
                            turn_tile(b0, 0)
                        if k == 13:
                            pe.wait_ge(pool0.sem, pool0.after(b0, "klo1"))
                            if s1:
                                pe.wait_ge(act1.sem, act1.after(b1, "eva"))
                            turn_tile(b0, 1)
                    if s3:
                        if k == 0:
                            out_rows(b3, 0)
                        if k == 2:
                            out_rows(b3, 1)
                        if k == 4:
                            pe.wait_ge(vec3.sem, vec3.after(b3, "on1"))
                            for s in range(NS):
                                t = nc.tensor.transpose(tail_bank[:, P * s:P * s + P], o_n[:, s], ident32[:])
                            t.then_inc(pe3.sem, 1)
                        if k == 6:
                            pe.wait_ge(vec3.sem, vec3.after(b3, "on_lo"))
                            for s in range(NS):
                                at = slice(P * s, P * s + P)
                                t = halves(tail_bank[:, at], on_hi[:, at], on_lo[:, at], w_hi[:, 3], w_lo[:, 3], start=(s == 0))
                            t.then_inc(pe3.sem, 1)
                        if k == 12:
                            pe.wait_ge(vec3.sem, vec3.after(b3, "xn1"))
                            for s in range(NS):
                                t = nc.tensor.transpose(tail_bank[:, P * s:P * s + P], xn[:, s], ident32[:])
                            t.then_inc(pe3.sem, 1)
                        if k == 13:
                            pe.wait_ge(act3.sem, act3.after(b3, "xn_t"))
                            for s in range(NS):
                                t = mm(tail_bank[:, E * s:E * s + E], xn_t[:, P * s:P * s + P], wg_sb[:], start=(s == 0), stop=True, skip_group_check=True)
                            t.then_inc(pe3.sem, 1)
                        if k == 15:
                            ranks(b3)
                if s2:
                    values(i, H - 1)

            pipeline(pe, iteration)

            pe.wait_ge(table, TABLE_STEPS)

            def turn_rows(j):
                r = j[1]
                pe.wait_ge(g_arrived[r], times((j[0], 0, 1), 16, 16))
                if due(times(plus(j, -2), 1, 1)):
                    pe.wait_ge(act_x, times(plus(j, -2), 1, 1))
                o = (chain_a16, chain_b16)[r % 2]
                for h in range(2):
                    for s in range(NS):
                        words = g_in[:, r, s, 0:D].bitcast(F16)
                        t = nc.tensor.transpose(o[:, TS * h + P * s:TS * h + P * s + P], words[:, D * h:D * h + D], ident16)
                t.then_inc(pe_x, 1)

            def hidden(j):
                e = pe.value_load(tile_e[0:1, bass.ds(times(j, 1), 1)], min_val=0, max_val=E - 1)
                x_hi, x_lo = xt[:, j[1] % 2, 0, :], xt[:, j[1] % 2, 1, :]
                pe.wait_ge(act_x, times(j, 1, 1))
                for f in range(FB):
                    if due(times(plus(j, -1), FB, f + 1)):
                        pe.wait_ge(vec_h, times(plus(j, -1), FB, f + 1))
                    at = bass.ds(e * F + f * P, P)
                    for n in range(2):
                        o = banks[f][:, TS * n:TS * n + TS]
                        mm(o, we_hi[:, n, at], x_hi, start=(n == 0), stop=False, skip_group_check=True)
                        mm(o, we_hi[:, n, at], x_lo, start=False, stop=False, skip_group_check=True)
                        t = mm(o, we_lo[:, n, at], x_hi, start=False, stop=True, skip_group_check=True)
                    t.then_inc(pe_ab, 1)

            def project_out(j):
                par = j[1] % 2
                e = pe.value_load(tile_e[0:1, bass.ds(times(j, 1), 1)], min_val=0, max_val=E - 1)
                pe.wait_ge(vec_hl, times(j, FB, FB))
                if due(times(plus(j, -2), 1, 1)):
                    pe.wait_ge(vec_y, times(plus(j, -2), 1, 1))
                y = (o_bank, tail_bank)[par]
                for s in range(NS):
                    o = y[:, D * s:D * s + D]
                    tok_s = slice(P * s, P * s + P)
                    for f in range(FB):
                        at = bass.ds(e * F + f * P, P)
                        mm(o, hh[:, par, f, tok_s], we_hi[:, 2, at], start=(s == 0 and f == 0), stop=False, skip_group_check=True)
                        mm(o, hh[:, par, f, tok_s], we_lo[:, 2, at], start=False, stop=False, skip_group_check=True)
                        t = mm(o, hl[:, par, f, tok_s], we_hi[:, 2, at], start=False, stop=(f == FB - 1), skip_group_check=True)
                t.then_inc(pe_y, 1)

            turn_rows((0, 0, 4))
            hidden((0, 0, 4))
            turn_rows((0, 1, 4))

            def tile_and_last(j, more=True):
                hidden(j)
                if more:
                    turn_rows(plus(j, 1))
                project_out(plus(j, -1))

            in_fours(pe, 1, NT - 1, tile_and_last)
            tile_and_last(((NT - 1) // 4, (NT - 1) % 4, 4), False)
            project_out(((NT - 1) // 4, (NT - 1) % 4, 4))


def constants():
    f = np.float32
    theta = (f(1.0) / f(10000.0) ** (np.arange(0, DK, 2, dtype=f) / f(DK))).astype(f)
    angle = np.outer(np.arange(S, dtype=f), theta).astype(f).reshape(NS, P, DK // 2).transpose(1, 0, 2).reshape(P, -1)
    p = np.arange(P)
    c = np.zeros((P, NC32 + P), f)
    c[:, C_COS:C_COS + 8] = np.cos(angle)
    c[:, C_SIN:C_SIN + 8] = np.sin(angle)
    c[:, C_E:C_E + E] = np.arange(E)
    c[:, C_BASE:C_BASE + E] = np.arange(E) * REGION
    for k in range(K):
        for s in range(NS):
            c[:, C_TOK + k * NS + s] = K * (s * P + p) + k
    c[:, C_POW:C_POW + 4] = -0.5
    c[:, C_J:C_J + NT + 1] = np.arange(NT + 1)
    c[:, NC32:] = np.eye(P)
    c16 = np.stack([np.eye(P), p[:, None] < p[None, :], np.ones((P, P))], 1).astype(np.float16)
    after = p[None, :] > p[:, None]
    masks = np.stack([np.where(after, MASKED, 0.0), np.where(after.T, MASKED, 0.0)], 1)
    dummy = np.zeros((TS, ROWW), f)
    dummy[:, W_IDX] = (NOUT + np.arange(TS)).astype(np.int32).view(f)
    return c, c16, masks, dummy


_INS = ['L0_attn_x', 'L0_attn_W_Q', 'L0_attn_W_K', 'L0_attn_W_V', 'L0_attn_W_O', 'L0_ffn_ln_w', 'L0_ffn_Wg', 'L0_ffn_bg',
        'L0_ffn_W1a', 'L0_ffn_b1a', 'L0_ffn_W1b', 'L0_ffn_b1b', 'L0_ffn_W2', 'L0_ffn_b2', 'L0_c', 'L0_wmod']


def kernel(**inputs):
    import ml_dtypes
    import concourse.bacc as _bacc
    from concourse import mybir as _mybir
    from concourse.bass_utils import run_bass_kernel_spmd as _run

    nc = _bacc.Bacc("TRN2", target_bir_lowering=False, num_devices=1)
    c, c16, masks, dummy = constants()
    arrays, args = {}, []
    named = [(name, np.ascontiguousarray(inputs[name])) for name in _INS]
    named += [("const32", c), ("const16", c16), ("constb", masks.astype(ml_dtypes.bfloat16)), ("dummy", dummy)]
    for name, a in named:
        arrays[f"in_{name}_dram"] = a
        args.append(nc.dram_tensor(f"in_{name}_dram", a.shape, _mybir.dt.from_np(a.dtype), kind="ExternalInput").ap())
    o = nc.dram_tensor("out_0_dram", (B, S, D), F32, kind="ExternalOutput").ap()
    build(nc, *args, o)
    r = _run(nc, [arrays], core_ids=[0])
    return r.results[0]["out_0_dram"]
```

```python
from contextlib import ExitStack

import numpy as np

import concourse.bass as bass
from concourse import mybir

F32 = mybir.dt.float32
F16 = mybir.dt.float16
BF16 = mybir.dt.bfloat16
I32 = mybir.dt.int32
U32 = mybir.dt.uint32
ALU = mybir.AluOpType
ACT = mybir.ActivationFunctionType
AX = mybir.AxisListType

P = 128
B, S, D = 16, 256, 128
H, DK = 16, 8
E, K, F = 8, 2, 512
NS = S // P
HG = 4
SLOT = P // HG
FB = F // P
TS = 256
NT = (B * S * K + E * (TS - 1)) // TS
REGION = B * S + TS
ROWS = E * REGION + TS
ROWW = D + 4
W_IDX, W_WGT = D, D + 1
NOUT = B * S * K
CHUNK = F // NS
SM_SCALE = float(1.0 / np.sqrt(np.float32(DK)))
EPS_LN = 1e-5
EPS_RMS = float(np.finfo(np.float32).eps)
MASKED = -1e30
C_COS, C_SIN, C_E, C_BASE, C_TOK, C_POW, C_J = 0, 8, 16, 24, 32, 36, 40
NC32 = C_J + NT + 1


class Steps:

    def __init__(self, sem, names):
        self.sem, self.names = sem, names.split()

    def after(self, n, name):
        return times(n, len(self.names), self.names.index(name) + 1)


def times(n, k, c=0):
    m, r, unroll = n
    return m * (unroll * k) + (r * k + c)


def plus(n, by):
    m, r, unroll = n
    return m + (r + by) // unroll, (r + by) % unroll, unroll


def due(count):
    return not isinstance(count, int) or count > 0


def build(nc, x_in, wq, wk, wv, wo, ln_w, wg, bg, w1a, b1a, w1b, b1b, w2, b2, c_in, wmod, const32,
          const16, constb, dummy_in, out):
    ctx = ExitStack()
    with ctx:
        def sb(name, shape, dt=F32):
            return ctx.enter_context(nc.sbuf_tensor(name, shape, dt))

        def sem(name):
            return ctx.enter_context(nc.semaphore(name))

        def steps(name, names):
            return Steps(sem(name), names)

        mod_rows = nc.dram_tensor("mod_rows", [B, 4 * D], F32).ap()
        rows = nc.dram_tensor("expert_rows", [ROWS, ROWW], F32).ap()
        outs = nc.dram_tensor("expert_outs", [NOUT, D], F32).ap()

        c32 = sb("c32", [P, NC32])
        c16 = sb("c16", [P, 3, P], F16)
        cb = sb("cb", [P, 2, P], BF16)
        ident32 = sb("ident32", [P, P])
        ident16, before16, ones16 = c16[:, 0, :], c16[:, 1, :], c16[:, 2, :]
        mask_q, mask_k = cb[:, 0, :], cb[:, 1, :]
        wraw = sb("wraw", [P, 4, D])
        wmod_sb = sb("wmod_sb", [P, 6 * D])
        c_sb = sb("c_sb", [B, D])
        silu_c = sb("silu_c", [P, B])
        mod_sb = sb("mod_sb", [B, 4 * D])
        mod_t = sb("mod_t", [P, B])
        scale_in = sb("scale_in", [P, B])
        shift_in = sb("shift_in", [P, B])
        w_hi = sb("w_hi", [P, 4, D], F16)
        w_lo = sb("w_lo", [P, 4, D], F16)
        wg_sb = sb("wg_sb", [P, E])
        bg_sb = sb("bg_sb", [P, E])
        lnw_sb = sb("lnw_sb", [P, D])
        b1_rows = sb("b1_rows", [E * FB, 2, P])
        b1_sb = sb("b1_sb", [P, 2, E * FB])
        b2_sb = sb("b2_sb", [P, E, D])
        we_hi = sb("we_hi", [P, 3, E * F], F16)
        we_lo = sb("we_lo", [P, 3, E * F], F16)
        dummy_sb = sb("dummy_sb", [P, NS, ROWW])
        x_sb = sb("x_sb", [P, B * NS, D])
        wstage = sb("wstage", [P, 2, 3, CHUNK])
        st0 = sb("st0", [P, NS, 6])
        mv0 = sb("mv0", [P, NS, 2])
        ve0 = sb("ve0", [P, NS])
        rstd0 = sb("rstd0", [P, NS])
        xhat0 = sb("xhat0", [P, NS, D])
        ht32 = sb("ht32", [P, S])
        ht_hi = sb("ht_hi", [P, S], F16)
        ht_lo = sb("ht_lo", [P, S], F16)
        turn_c = sb("turn_c", [P, NS, 2 * H, DK])
        turn_s = sb("turn_s", [P, NS, 2 * H, DK])
        turned = sb("turned", [P, NS, 2 * H, DK])
        v_sb = sb("v_sb", [P, 2, NS, D])
        qk_tok = sb("qk_tok", [P, 2, NS, 2 * H, SLOT], F16)
        qk_t = sb("qk_t", [P, 2, 2 * HG, S], F16)
        k_pad = sb("k_pad", [P, 2, H, S], F16)
        nmax = sb("nmax", [P, H, 3])
        q_max = sb("q_max", [P, 2, HG, S], F16)
        v_aug = sb("v_aug", [P, 2, NS, H, SLOT])
        probs = sb("probs", [P, 4, S + P])
        o_t = sb("o_t", [P, 2, HG, S])
        mod_b = sb("mod_b", [P, 2, 4 * D])
        rsum = sb("rsum", [P, NS, H])
        o_n = sb("o_n", [P, NS, D])
        on_hi = sb("on_hi", [P, S], F16)
        on_lo = sb("on_lo", [P, S], F16)
        gated = sb("gated", [P, NS, D])
        st3 = sb("st3", [P, NS, 6])
        mv3 = sb("mv3", [P, NS, 2])
        ve3 = sb("ve3", [P, NS])
        rstd3 = sb("rstd3", [P, NS])
        xhat3 = sb("xhat3", [P, NS, D])
        h_s = sb("h_s", [P, NS, D])
        h_m = sb("h_m", [P, NS, D])
        square = sb("square", [P, NS, D])
        ssum = sb("ssum", [P, NS])
        ms = sb("ms", [P, NS])
        rms = sb("rms", [P, NS])
        xn = sb("xn", [P, NS, D])
        xn_t = sb("xn_t", [P, S])
        logits = sb("logits", [P, NS, E])
        top = sb("top", [P, NS, 8])
        top_i = sb("top_i", [P, NS, 8], U32)
        top_f = sb("top_f", [P, NS, K])
        chosen = sb("chosen", [P, NS, K, E])
        member = sb("member", [P, NS, E], F16)
        gap = sb("gap", [P, NS])
        egap = sb("egap", [P, NS])
        den = sb("den", [P, NS])
        rank = sb("rank", [P, NS, E])
        filled = sb("filled", [P, E])
        at_e = sb("at_e", [P, NS, K, E])
        pos_f = sb("pos_f", [P, NS, K])
        pos_i = sb("pos_i", [P, 2, NS, K], I32)
        tok = sb("tok", [P, K, NS])
        send = sb("send", [P, 2, K, NS, ROWW])
        tab = sb("tab", [P, 8, E])
        tab_i = sb("tab_i", [P, 2, E], I32)
        cmp_j = sb("cmp_j", [P, NT + 1, E])
        tj = sb("tj", [P, 5, NT + 1])
        tile_e = sb("tile_e", [P, NT + 1], I32)
        tile_row = sb("tile_row", [P, NT + 1], I32)
        g_in = sb("g_in", [P, 4, NS, ROWW])
        number_of = sb("number_of", [P, 4, NS], I32)
        weight_of = sb("weight_of", [P, 4, NS])
        xt = sb("xt", [P, 2, 2, TS], F16)
        silu_a = sb("silu_a", [P, FB, TS])
        h32 = sb("h32", [P, FB, TS])
        hh = sb("hh", [P, 2, FB, TS], F16)
        hl = sb("hl", [P, 2, FB, TS], F16)
        yb = sb("yb", [P, 2, NS, D])
        y_sb = sb("y_sb", [P, 4, NS, D])
        gb_sb = k_pad[:, 0].rearrange("p h t -> p (h t)").bitcast(F32).rearrange("p (b d) -> p b d", d=D)
        free = we_lo[:].rearrange("p n f -> p (n f)").bitcast(F32)

        def last(start, blocks):
            return free[:, start * NS * D:(start + blocks) * NS * D]

        y_in = last(0, 8).rearrange("p (r s k d) -> p r s k d", s=NS, k=K, d=D)
        ysum = last(8, 2).rearrange("p (r s d) -> p r s d", s=NS, d=D)
        ygate = last(10, 2).rearrange("p (r s d) -> p r s d", s=NS, d=D)
        res = last(12, 4).rearrange("p (r s d) -> p r s d", s=NS, d=D)

        banks = [ctx.enter_context(nc.psum_tensor(f"bank{i}", [P, 512], F32)) for i in range(8)]
        row_bank, col_bank = banks[0:2], banks[2:4]
        o_bank, chain_a, chain_b, tail_bank = banks[4:8]
        chain_a16, chain_b16 = chain_a[:].bitcast(F16), chain_b[:].bitcast(F16)

        consts_in = sem("consts_in")
        x_in0, x_in1 = sem("x_in0"), sem("x_in1")
        moe_consts_in = sem("moe_consts_in")
        dummies_out = sem("dummies_out")
        mod_out, gb_in = sem("mod_out"), sem("gb_in")
        init_vec, init_pool = sem("init_vec"), sem("init_pool")
        setup_pe = steps("setup_pe", "c_t w_t mod_t")
        setup_act = steps("setup_act", "silu b1 w_hi")
        setup_vec = steps("setup_vec", "w_lo scale shift copied abs_a abs_b sign_a sign_b sgn_a sgn_b gate_a gate_b plus1")
        wstage_in = [sem("wstage_in0"), sem("wstage_in1")]
        mod_in = [sem("mod_in0"), sem("mod_in1")]
        pad_in = [[[sem(f"pad_in{h}{p}{g}") for g in range(HG)] for p in range(2)] for h in range(2)]
        pe0 = steps("pe0", "x_t proj0 proj1 t0 t1")
        vecn = steps("vecn", "stats0 stats1 aggr0 aggr1 var xhat0 xhat1")
        pooln = steps("pooln", "rstd")
        vec0 = steps("vec0", "cos0 sin0a sin0b cos1 sin1a sin1b hi0 hi1")
        act0 = steps("act0", "h32 h_hi v0 v1 khi0 khi1 w_hi ev0 ev1")
        pool0 = steps("pool0", "h_lo zero_m turn0 turn1 qlo0 klo0 qlo1 klo1 w_lo")
        rows_ready, max_ready = sem("rows_ready"), sem("max_ready")
        vec1 = steps("vec1", "m0a m1a m0b m1b")
        pe1 = steps("pe1", "ta tb")
        act1 = steps("act1", "v_aug eva evb")
        cols_ready, probs_ready, probs_used, group_saved = sem("cols_ready"), sem("probs_ready"), sem("probs_used"), sem("group_saved")
        pe3a = steps("pe3a", "o0 o1 on_t wo")
        vec3a = steps("vec3a", "rs0 on0 rs1 on1 on_lo gated")
        act3a = steps("act3a", "on_hi")
        pool3a = steps("pool3a", "resid")
        pe3b = steps("pe3b", "xn_t logits")
        vec3b = steps("vec3b", "stats0 stats1 aggr0 aggr1 var xhat0 xhat1 ms xn0 xn1 logits max0 max1 idx0 idx1 idxf chosen member gap")
        act3b = steps("act3b", "sq0 sq1 xn_t xn_hi egap")
        pool3b = steps("pool3b", "rstd scaled shifted rms xn_lo")
        pe_rank = steps("pe_rank", "ranks")
        vec_place = steps("vec_place", "rank filled den w1 at w2 pos_f pos_i copy tok tok_on")
        sent = [sem("sent0"), sem("sent1")]
        table = sem("table")
        padded = sem("padded")
        g_arrived = [sem(f"g_arrived{r}") for r in range(4)]
        named = steps("named", "number weight")
        pe_x = sem("pe_x")
        act_x = sem("act_x")
        pe_ab, act_silu, vec_h, act_hh, vec_hl = sem("pe_ab"), sem("act_silu"), sem("vec_h"), sem("act_hh"), sem("vec_hl")
        pe_y, vec_y, act_y = sem("pe_y"), sem("vec_y"), sem("act_y")
        y_sent = [sem(f"y_sent{r}") for r in range(4)]
        y_back = [sem(f"y_back{r}") for r in range(4)]
        pool_sum, vec_gate, vec_res = sem("pool_sum"), sem("vec_gate"), sem("vec_res")
        out_done = [sem(f"out_done{r}") for r in range(4)]

        TABLE_STEPS = 18
        N_CONST = 14
        N_MOE_CONST = 3

        def number(n):
            return n // 2, n % 2, 2

        def pipeline(eng, iteration):
            def one(i):
                iteration(number(i), *(0 <= i + n < B for n in (-3, -2, -1, 0, 1, 2, 3)))
            for i in range(-3, 5):
                one(i)
            with eng.Fori(2, (B - 3) // 2) as m:
                iteration((m, 1, 2), *[True] * 7)
                iteration((m + 1, 0, 2), *[True] * 7)
            for i in range(B - 3, B + 3):
                one(i)

        def tile_number(n):
            return n // 4, n % 4, 4

        def experts_of(eng):
            regs = [eng.alloc_register(f"expert{r}") for r in range(4)]
            before = [eng.alloc_register(f"expert_before{r}") for r in range(2)]

            def read(j):
                m, r, _ = j
                if r == 0:
                    for n in range(2):
                        eng.reg_mov(before[n], regs[2 + n] if due(times(j, 1)) else 0)
                    eng.load(regs, tile_e[0:1, bass.ds(4 * m, 4)])
                known = before + regs
                return [eng.snap(known[2 + r - n], min_val=0, max_val=E - 1) for n in range(3)]
            return read

        def in_fours(eng, first, end, body):
            start = max(4, (first + 3) // 4 * 4)
            for n in range(first, start):
                body((n // 4, n % 4, 4))
            with eng.Fori(start // 4, end // 4) as m:
                for r in range(4):
                    body((m, r, 4))
            for n in range(end // 4 * 4, end):
                body((n // 4, n % 4, 4))

        x_view = x_in.rearrange("b (s p) d -> p (b s) d", p=P)
        w1a_v = w1a.rearrange("e d (h f) -> e h d f", h=NS)
        w1b_v = w1b.rearrange("e d (h f) -> e h d f", h=NS)
        w2_v = w2.rearrange("e (h c f) d -> e h f c d", h=NS, f=P)

        block = ctx.enter_context(nc.Block())

        @block.sync
        def _(sp):
            sp.dma_start(c_sb[:], c_in).then_inc(consts_in, 16)
            sp.dma_start(ident32[:], const32[:, NC32:NC32 + P]).then_inc(consts_in, 16)
            sp.dma_start(wmod_sb[:], wmod).then_inc(consts_in, 16)
            sp.dma_start(c32[:], const32[:, 0:NC32]).then_inc(consts_in, 16)
            sp.dma_start(x_sb[:, 0:4, :], x_view[:, 0:4, :]).then_inc(x_in0, 16)
            for n, w in enumerate((wq, wk, wv, wo)):
                sp.dma_start(wraw[:, n, :], w).then_inc(consts_in, 16)
            sp.dma_start(c16[:], const16).then_inc(consts_in, 16)
            sp.dma_start(cb[:], constb).then_inc(consts_in, 16)
            sp.dma_start(wg_sb[:], wg).then_inc(consts_in, 16)
            sp.dma_start(x_sb[:, 4:, :], x_view[:, 4:, :]).then_inc(x_in1, 16)
            sp.wait_ge(mod_out, 16)

            def iteration(i, placing, routing, closing, s2, s1, s0, norm):
                if s0:
                    b = plus(i, 2)
                    m, par, _ = b
                    if due(pool0.after(plus(b, -2), "w_lo")):
                        sp.wait_ge(pool0.sem, pool0.after(plus(b, -2), "w_lo"))
                    sp.dma_start(wstage[:, par, 0, :], w1a_v[m, par]).then_inc(wstage_in[par], 16)
                    sp.dma_start(wstage[:, par, 1, :], w1b_v[m, par]).then_inc(wstage_in[par], 16)
                    sp.dma_start(wstage[:, par, 2, :].rearrange("p (c d) -> p c d", d=D), w2_v[m, par]).then_inc(wstage_in[par], 16)
                if s2:
                    m, par, _ = i
                    if due(pool3b.after(plus(i, -2), "shifted")):
                        sp.wait_ge(pool3b.sem, pool3b.after(plus(i, -2), "shifted"))
                    sp.dma_start(mod_b[:, par, :], mod_rows[bass.ds(times(i, 1), 1), :].broadcast_to([P, 4 * D])).then_inc(mod_in[par], 16)
                if s0:
                    b = plus(i, 2)
                    par = b[1]
                    sp.wait_ge(act0.sem, act0.after(b, "ev1"))
                    for half in range(2):
                        if due(times(plus(b, -2), H, 8 * (half + 1))):
                            sp.wait_ge(cols_ready, times(plus(b, -2), H, 8 * (half + 1)))
                        for g in range(HG):
                            at = slice(SLOT * g, SLOT * g + SLOT)
                            heads = k_pad[at, par, :, :].rearrange("p (j g) t -> p j g t", g=HG)[:, 2 * half:2 * half + 2, g, :]
                            sp.dma_start(heads, qk_t[at, par, HG + 2 * half:HG + 2 * half + 2, :]).then_inc(pad_in[half][par][g], 16)

            pipeline(sp, iteration)

            sp.wait_ge(cols_ready, B * H)
            sp.dma_start(gb_sb, mod_rows[:, 3 * D:].unsqueeze(0).broadcast_to([P, B, D])).then_inc(gb_in, 16)
            sp.wait_ge(table, TABLE_STEPS)
            for e in range(E):
                v = sp.value_load(tab_i[0:1, 0, e:e + 1], min_val=0, max_val=ROWS - TS)
                sp.dma_start(rows[bass.ds(v, TS), :].rearrange("(s p) w -> p s w", p=P), dummy_sb[:]).then_inc(padded, 16)
            sp.wait_ge(padded, 16 * E)
            sp.wait_ge(sent[0], 64 * B // 2)
            sp.wait_ge(sent[1], 64 * B // 2)
            sp.wait_ge(dummies_out, 16)

            def load(j):
                r = j[1]
                if due(times(plus(j, -4), 1, 1)):
                    sp.wait_ge(pe_x, times(plus(j, -4), 1, 1))
                    sp.nop(nofuse=True)
                    sp.wait_ge(named.sem, named.after(plus(j, -4), "weight"))
                    sp.nop(nofuse=True)
                v = sp.value_load(tile_row[0:1, bass.ds(times(j, 1), 1)], min_val=0, max_val=ROWS - TS)
                sp.dma_start(g_in[:, r, :, :], rows[bass.ds(v, TS), :].rearrange("(s p) w -> p s w", p=P)).then_inc(g_arrived[r], 16)

            in_fours(sp, 0, NT, load)

            for r in range(4):
                sp.wait_ge(y_sent[r], 32 * ((NT - r + 3) // 4))
            back = outs.rearrange("(b s p k) d -> b p s k d", s=NS, p=P, k=K)

            def finish(n):
                m, r, _ = n
                if due(times(plus(n, -4), 1, 1)):
                    sp.wait_ge(pool_sum, times(plus(n, -4), 1, 1))
                sp.dma_start(y_in[:, r], back[times(n, 1)]).then_inc(y_back[r], 16)

            in_fours(sp, 0, B, finish)
            for r in range(4):
                sp.wait_ge(out_done[r], 16 * (B // 4))

        @block.gpsimd
        def _(pool):
            nc.gpsimd.memset(k_pad[:, 0], 0.0).then_inc(init_pool, 1)
            nc.gpsimd.memset(k_pad[:, 1], 0.0).then_inc(init_pool, 1)
            nc.gpsimd.memset(v_aug[:], 0.0).then_inc(init_pool, 1)
            pool.wait_ge(init_pool, 3)
            nc.gpsimd.memset(v_aug[:, :, :, :, DK:DK + 1], 1.0).then_inc(init_pool, 1)
            nc.gpsimd.memset(send[:], 0.0).then_inc(init_pool, 1)
            pool.wait_ge(consts_in, 16 * N_CONST)
            pool.wait_ge(init_vec, 2)
            power = c32[:, C_POW:C_POW + NS]

            def send_rows(b, n):
                s, k = n // K, n % K
                pool.wait_ge(vec_place.sem, vec_place.after(b, "tok"))
                pool.nop(nofuse=True)
                pool.indirect_dma_start(out=rows, out_offset=bass.IndirectOffsetOnAxis(ap=pos_i[:, b[1], s, k:k + 1], axis=0),
                                        in_=send[:, b[1], k, s, :], in_offset=None).then_inc(sent[b[1]], 16)

            def iteration(i, placing, routing, closing, s2, s1, s0, norm):
                bn, b0, ba, bb, bs = plus(i, 3), plus(i, 2), plus(i, -1), plus(i, -2), plus(i, -3)
                if s0:
                    pool.wait_ge(act0.sem, act0.after(b0, "h_hi"))
                    nc.gpsimd.tensor_tensor(ht_lo[:], ht32[:], ht_hi[:], ALU.subtract).then_inc(pool0.sem, 1)
                    if due(pe1.after(plus(b0, -2), "tb")):
                        pool.wait_ge(pe1.sem, pe1.after(plus(b0, -2), "tb"))
                    pool.nop(nofuse=True)
                    nc.gpsimd.memset(qk_tok[:, b0[1], :, 0:H, 3 * DK:3 * DK + 1], 0.0).then_inc(pool0.sem, 1)
                if routing:
                    par = bb[1]
                    pool.wait_ge(vec3b.sem, vec3b.after(bb, "var"))
                    nc.gpsimd.tensor_tensor(rstd3[:], ve3[:], power, ALU.pow).then_inc(pool3b.sem, 1)
                    pool.wait_ge(vec3b.sem, vec3b.after(bb, "xhat1"))
                    nc.gpsimd.tensor_tensor(h_s[:], xhat3[:], mod_b[:, par, 2 * D:3 * D].unsqueeze(1).broadcast_to([P, NS, D]), ALU.mult).then_inc(pool3b.sem, 1)
                    pool.wait_ge(pool3b.sem, pool3b.after(bb, "scaled"))
                    nc.gpsimd.tensor_tensor(h_m[:], h_s[:], mod_b[:, par, D:2 * D].unsqueeze(1).broadcast_to([P, NS, D]), ALU.add).then_inc(pool3b.sem, 1)
                if s0:
                    add_turned(b0, 0)
                    add_turned(b0, 1)
                if routing:
                    pool.wait_ge(vec3b.sem, vec3b.after(bb, "ms"))
                    nc.gpsimd.tensor_tensor(rms[:], ms[:], power, ALU.pow).then_inc(pool3b.sem, 1)
                if s0:
                    low_parts(b0, 0)
                    low_parts(b0, 1)
                if placing:
                    send_rows(bs, 0)
                if closing:
                    pool.wait_ge(vec3a.sem, vec3a.after(ba, "gated"))
                    xs = x_sb[:, bass.ds(times(ba, NS), NS), :]
                    nc.gpsimd.tensor_tensor(xs, xs, gated[:], ALU.add).then_inc(pool3a.sem, 1)
                if placing:
                    send_rows(bs, 1)
                if norm:
                    pool.wait_ge(vecn.sem, vecn.after(bn, "var"))
                    nc.gpsimd.tensor_tensor(rstd0[:], ve0[:], power, ALU.pow).then_inc(pooln.sem, 1)
                if placing:
                    send_rows(bs, 2)
                if routing:
                    pool.wait_ge(act3b.sem, act3b.after(bb, "xn_hi"))
                    words = send[:, bb[1], 0, :, 0:D].bitcast(F16)
                    nc.gpsimd.tensor_tensor(words[:, :, D:2 * D], xn[:], words[:, :, 0:D], ALU.subtract).then_inc(pool3b.sem, 1)
                if placing:
                    send_rows(bs, 3)
                if s0:
                    at = bass.ds(times(b0, CHUNK), CHUNK)
                    pool.wait_ge(act0.sem, act0.after(b0, "w_hi"))
                    nc.gpsimd.tensor_tensor(we_lo[:, :, at], wstage[:, b0[1]], we_hi[:, :, at], ALU.subtract).then_inc(pool0.sem, 1)

            def add_turned(b, s):
                pool.wait_ge(vec0.sem, vec0.after(b, f"sin{s}b"))
                nc.gpsimd.tensor_tensor(turned[:, s], turn_c[:, s], turn_s[:, s], ALU.add).then_inc(pool0.sem, 1)

            def low_parts(b, s):
                slots = qk_tok[:, b[1], s].rearrange("p h (c w) -> p h c w", w=DK)
                pool.wait_ge(vec0.sem, vec0.after(b, f"hi{s}"))
                nc.gpsimd.tensor_tensor(slots[:, 0:H, 1, :], turned[:, s, 0:H], slots[:, 0:H, 0, :], ALU.subtract).then_inc(pool0.sem, 1)
                pool.wait_ge(act0.sem, act0.after(b, f"khi{s}"))
                nc.gpsimd.tensor_tensor(slots[:, H:, 2, :], turned[:, s, H:], slots[:, H:, 0, :], ALU.subtract).then_inc(pool0.sem, 1)

            pipeline(pool, iteration)

            def name_rows(j):
                m, r, _ = j
                pool.wait_ge(g_arrived[r], times((m, 0, 1), 16, 16))
                if due(times((m, 0, 1), 32)):
                    pool.wait_ge(y_sent[r], times((m, 0, 1), 32))
                pool.nop(nofuse=True)
                nc.gpsimd.tensor_copy(number_of[:, r], g_in[:, r, :, W_IDX].bitcast(I32)).then_inc(named.sem, 1)
                nc.gpsimd.tensor_copy(weight_of[:, r], g_in[:, r, :, W_WGT]).then_inc(named.sem, 1)

            def scatter(j, more=True):
                r = j[1]
                if more:
                    name_rows(plus(j, 2))
                pool.wait_ge(act_y, times(j, NS, NS))
                pool.nop(nofuse=True)
                for s in range(NS):
                    pool.indirect_dma_start(out=outs, out_offset=bass.IndirectOffsetOnAxis(ap=number_of[:, r, s:s + 1], axis=0),
                                            in_=y_sb[:, r, s, :], in_offset=None, bounds_check=NOUT - 1, oob_is_err=False).then_inc(y_sent[r], 16)

            name_rows(tile_number(0))
            name_rows(tile_number(1))
            in_fours(pool, 0, NT - 2, scatter)
            scatter(tile_number(NT - 2), False)
            scatter(tile_number(NT - 1), False)

            def finish(n):
                m, r, _ = n
                pool.wait_ge(y_back[r], times((m, 0, 1), 16, 16))
                if due(times(plus(n, -2), 1, 1)):
                    pool.wait_ge(vec_gate, times(plus(n, -2), 1, 1))
                nc.gpsimd.tensor_tensor(ysum[:, r % 2], y_in[:, r, :, 0, :], y_in[:, r, :, 1, :], ALU.add).then_inc(pool_sum, 1)

            in_fours(pool, 0, B, finish)

        @block.scalar
        def _(act):
            act.dma_start(dummy_sb[:], dummy_in.rearrange("(s p) w -> p s w", p=P)).then_inc(consts_in, 16)
            for n, b1 in enumerate((b1a, b1b)):
                act.dma_start(b1_rows[:, n, :], b1.rearrange("e (c f) -> (e c) f", f=P)).then_inc(consts_in, 16)
            act.dma_start(lnw_sb[:], ln_w.unsqueeze(0).broadcast_to([P, D])).then_inc(moe_consts_in, 16)
            act.dma_start(bg_sb[:], bg.unsqueeze(0).broadcast_to([P, E])).then_inc(moe_consts_in, 16)
            act.dma_start(b2_sb[:], b2.unsqueeze(0).broadcast_to([P, E, D])).then_inc(moe_consts_in, 16)
            act.wait_ge(setup_pe.sem, 1)
            nc.scalar.activation(silu_c[:], banks[0][:, 0:B], ACT.Silu).then_inc(setup_act.sem, 1)
            nc.scalar.activation(b1_sb[:], banks[0][:, E * FB:3 * E * FB].rearrange("p (n c) -> p n c", n=2), ACT.Copy).then_inc(setup_act.sem, 1)
            nc.scalar.preload_act_table(ACT.Exp)
            act.wait_ge(setup_pe.sem, 2)
            nc.scalar.activation(w_hi[:], banks[2][:].rearrange("p (n d) -> p n d", d=D), ACT.Copy).then_inc(setup_act.sem, 1)
            act.wait_ge(setup_vec.sem, len(setup_vec.names))
            act.dma_start(mod_rows, mod_sb[:]).then_inc(mod_out, 16)
            act.wait_ge(consts_in, 16 * N_CONST)
            act.dma_start(rows[E * REGION:, :].rearrange("(s p) w -> p s w", p=P), dummy_sb[:]).then_inc(dummies_out, 16)
            act.wait_ge(init_pool, 4)

            def iteration(i, placing, routing, closing, s2, s1, s0, norm):
                b0, b1, ba, bb = plus(i, 2), plus(i, 1), plus(i, -1), plus(i, -2)
                for k in range(H):
                    if s2:
                        act.wait_ge(cols_ready, times(i, H, k + 1))
                        if due(times(i, H, k - 3)):
                            act.wait_ge(probs_used, times(i, H, k - 3))
                        nc.scalar.activation(probs[:, k % 4], col_bank[k % 2][:, 0:S + P], ACT.Exp, scale=SM_SCALE).then_inc(probs_ready, 1)
                        if k % HG == 0 and k:
                            save_group(i, k // HG - 1)
                        if k == 1:
                            save_queries(i, 1)
                    if s1:
                        if k == 2:
                            act.wait_ge(act0.sem, act0.after(b1, "v1"))
                            nc.scalar.activation(v_aug[:, b1[1], :, :, 0:DK], v_sb[:, b1[1]].rearrange("p s (h w) -> p s h w", w=DK), ACT.Copy).then_inc(act1.sem, 1)
                        if k == 9:
                            save_queries(b1, 0)
                    if s0:
                        if k == 0:
                            act.wait_ge(pe0.sem, pe0.after(b0, "x_t"))
                            at = bass.ds(times(b0, 1), 1)
                            nc.scalar.activation(ht32[:], chain_a[:, 0:S], ACT.Identity, scale=scale_in[:, at], bias=shift_in[:, at]).then_inc(act0.sem, 1)
                            nc.scalar.activation(ht_hi[:], chain_a[:, 0:S], ACT.Identity, scale=scale_in[:, at], bias=shift_in[:, at]).then_inc(act0.sem, 1)
                        if k in (3, 4):
                            t = k - 3
                            act.wait_ge(pe0.sem, pe0.after(b0, f"proj{t}"))
                            nc.scalar.activation(v_sb[:, b0[1], t, :], (chain_b, chain_a)[t][:, 2 * D:3 * D], ACT.Copy).then_inc(act0.sem, 1)
                        if k in (7, 8):
                            t = k - 7
                            act.wait_ge(pool0.sem, pool0.after(b0, f"turn{t}"))
                            slots = qk_tok[:, b0[1], t].rearrange("p h (c w) -> p h c w", w=DK)
                            nc.scalar.activation(slots[:, H:, 0:2, :], turned[:, t, H:].unsqueeze(2).broadcast_to([P, H, 2, DK]), ACT.Copy).then_inc(act0.sem, 1)
                        if k == 9:
                            act.wait_ge(wstage_in[b0[1]], times((b0[0], 0, 1), 48, 48))
                            nc.scalar.activation(we_hi[:, :, bass.ds(times(b0, CHUNK), CHUNK)], wstage[:, b0[1]], ACT.Copy).then_inc(act0.sem, 1)
                        if k in (10, 12):
                            t = (k - 10) // 2
                            act.wait_ge(pe0.sem, pe0.after(b0, f"t{t}"))
                            half = (chain_a16, chain_b16)[t]
                            nc.scalar.activation(qk_t[:, b0[1], :, P * t:P * t + P], half.rearrange("p (j t) -> p j t", t=P), ACT.Copy).then_inc(act0.sem, 1)
                    if closing and k == 6:
                        act.wait_ge(pe3a.sem, pe3a.after(ba, "on_t"))
                        nc.scalar.activation(on_hi[:], tail_bank[:, 0:S], ACT.Copy).then_inc(act3a.sem, 1)
                    if routing:
                        if k == 6:
                            act.wait_ge(pool3b.sem, pool3b.after(bb, "shifted"))
                            for t in range(NS):
                                nc.scalar.activation(square[:, t], h_m[:, t], ACT.Square, accum_out=ssum[:, t:t + 1]).then_inc(act3b.sem, 1)
                        if k == 11:
                            act.wait_ge(pe3b.sem, pe3b.after(bb, "xn_t"))
                            nc.scalar.activation(xn_t[:], tail_bank[:, 0:S], ACT.Copy).then_inc(act3b.sem, 1)
                            if due(times((bb[0], 0, 1), 64)):
                                act.wait_ge(sent[bb[1]], times((bb[0], 0, 1), 64))
                            nc.scalar.activation(send[:, bb[1], 0, :, 0:D].bitcast(F16)[:, :, 0:D], xn[:], ACT.Copy).then_inc(act3b.sem, 1)
                        if k == 15:
                            act.wait_ge(vec3b.sem, vec3b.after(bb, "gap"))
                            nc.scalar.activation(egap[:], gap[:], ACT.Exp).then_inc(act3b.sem, 1)
                if s2:
                    save_group(i, HG - 1)

            def save_group(b, j):
                act.wait_ge(probs_used, times(b, H, HG * (j + 1)))
                nc.scalar.activation(o_t[:, b[1], j, :], o_bank[:, 0:S], ACT.Copy).then_inc(group_saved, 1)

            def save_queries(b, half):
                act.wait_ge(pe1.sem, pe1.after(b, "t" + "ab"[half]))
                nc.scalar.activation(q_max[:, b[1], 2 * half:2 * half + 2, :], chain_b16[:, 0:2 * S].rearrange("p (j t) -> p j t", t=S), ACT.Copy).then_inc(act1.sem, 1)

            pipeline(act, iteration)

            nc.scalar.preload_act_table(ACT.Silu)
            act.wait_ge(table, TABLE_STEPS)

            def save_x(j):
                act.wait_ge(pe_x, times(j, 1, 1))
                if due(times(plus(j, -2), FB, FB)):
                    act.wait_ge(pe_ab, times(plus(j, -2), FB, FB))
                nc.scalar.activation(xt[:, j[1] % 2], (chain_a16, chain_b16)[j[1] % 2][:, 0:2 * TS].rearrange("p (h t) -> p h t", t=TS), ACT.Copy).then_inc(act_x, 1)

            def high(j, f):
                act.wait_ge(vec_h, times(j, FB, f + 1))
                if due(times(plus(j, -2), 1, 1)):
                    act.wait_ge(pe_y, times(plus(j, -2), 1, 1))
                nc.scalar.activation(hh[:, j[1] % 2, f], h32[:, f], ACT.Copy).then_inc(act_hh, 1)

            def weigh(j):
                r = j[1]
                if due(times((j[0], 0, 1), 32)):
                    act.wait_ge(y_sent[r], times((j[0], 0, 1), 32))
                act.wait_ge(vec_y, times(j, 1, 1))
                act.wait_ge(named.sem, named.after(j, "weight"))
                for s in range(NS):
                    nc.scalar.activation(y_sb[:, r, s], yb[:, r % 2, s], ACT.Copy, scale=weight_of[:, r, s:s + 1]).then_inc(act_y, 1)

            experts = experts_of(act)

            def tile(j, more=True, finished=True):
                e = experts(j)[0]
                for f in range(FB):
                    act.wait_ge(pe_ab, times(j, FB, f + 1))
                    if due(times(plus(j, -1), FB, f + 1)):
                        act.wait_ge(vec_h, times(plus(j, -1), FB, f + 1))
                    nc.scalar.activation(silu_a[:, f], banks[f][:, 0:TS], ACT.Silu, bias=b1_sb[:, 0, bass.ds(e * FB + f, 1)]).then_inc(act_silu, 1)
                    if f == 1 and more:
                        save_x(plus(j, 1))
                    if f == 2 and finished:
                        weigh(plus(j, -2))
                    if f:
                        high(j, f - 1)
                high(j, FB - 1)

            save_x(tile_number(0))
            tile(tile_number(0), finished=False)
            tile(tile_number(1), finished=False)
            in_fours(act, 2, NT - 1, tile)
            tile(tile_number(NT - 1), more=False)
            weigh(tile_number(NT - 2))
            weigh(tile_number(NT - 1))

            out_v = out.rearrange("b (s p) d -> b p s d", p=P)

            def store(n):
                m, r, _ = n
                act.wait_ge(vec_res, times(n, 1, 1))
                act.dma_start(out_v[times(n, 1)], res[:, r]).then_inc(out_done[r], 16)

            in_fours(act, 0, B, store)

        @block.vector
        def _(vec):
            nc.vector.memset(qk_tok[:], 0.0).then_inc(init_vec, 1)
            vec.wait_ge(init_vec, 1)
            nc.vector.memset(qk_tok[:, :, :, H:, 3 * DK:3 * DK + 1], 1.0).then_inc(init_vec, 1)

            vec.wait_ge(setup_act.sem, 3)
            nc.vector.tensor_tensor(w_lo[:], banks[2][:].rearrange("p (n d) -> p n d", d=D), w_hi[:], ALU.subtract).then_inc(setup_vec.sem, 1)
            vec.wait_ge(setup_pe.sem, 3)
            nc.vector.tensor_scalar(scale_in[:], banks[1][:, B:2 * B], 1.0, None, ALU.add).then_inc(setup_vec.sem, 1)
            nc.vector.tensor_copy(shift_in[:], banks[1][:, 0:B]).then_inc(setup_vec.sem, 1)
            nc.vector.tensor_copy(mod_sb[:], banks[3][0:B, :]).then_inc(setup_vec.sem, 1)
            gate = mod_sb[:].rearrange("p (g d) -> p g d", d=D)
            vec.wait_ge(setup_vec.sem, 4)
            for n, g in ((0, 0), (1, 3)):
                nc.vector.tensor_scalar(square[0:B, n, :], gate[:, g], -1.0, None, ALU.mult).then_inc(setup_vec.sem, 1)
            vec.wait_ge(setup_vec.sem, 6)
            for n, g in ((0, 0), (1, 3)):
                nc.vector.scalar_tensor_tensor(out=gated[0:B, n, :], in0=gate[:, g], scalar=0.25, in1=square[0:B, n, :], op0=ALU.max, op1=ALU.max).then_inc(setup_vec.sem, 1)
            for n, g in ((0, 0), (1, 3)):
                nc.vector.tensor_scalar(h_s[0:B, n, :], gate[:, g], 0.0, 2.0, ALU.is_ge, ALU.mult).then_inc(setup_vec.sem, 1)
            vec.wait_ge(setup_vec.sem, 10)
            for n, g in ((0, 0), (1, 3)):
                nc.vector.scalar_tensor_tensor(out=gate[:, g], in0=h_s[0:B, n, :], scalar=-1.0, in1=gated[0:B, n, :], op0=ALU.add, op1=ALU.mult).then_inc(setup_vec.sem, 1)
            nc.vector.tensor_scalar(gate[:, 2], gate[:, 2], 1.0, None, ALU.add).then_inc(setup_vec.sem, 1)
            vec.wait_ge(consts_in, 16 * N_CONST)
            nc.vector.tensor_copy(filled[:], c32[:, C_BASE:C_BASE + E]).then_inc(init_vec, 1)
            nc.vector.tensor_copy(tok[:].rearrange("p k s -> p (k s)"), c32[:, C_TOK:C_TOK + K * NS]).then_inc(init_vec, 1)
            cos = c32[:, C_COS:C_COS + 8].rearrange("p (s w) -> p s w", w=DK // 2)
            sin = c32[:, C_SIN:C_SIN + 8].rearrange("p (s w) -> p s w", w=DK // 2)

            def moments(b, vecs, st, mv, ve):
                for s in range(NS):
                    nc.vector.bn_stats(st[:, s], x_sb[:, bass.ds(times(b, NS, s), 1), :].rearrange("p o d -> p (o d)")).then_inc(vecs.sem, 1)
                vec.wait_ge(vecs.sem, vecs.after(b, "stats1"))
                vec.nop(nofuse=True)
                for s in range(NS):
                    nc.vector.bn_aggr(mv[:, s], st[:, s]).then_inc(vecs.sem, 1)
                vec.wait_ge(vecs.sem, vecs.after(b, "aggr1"))
                nc.vector.tensor_scalar(ve[:], mv[:, :, 1], EPS_LN, None, ALU.add).then_inc(vecs.sem, 1)

            def normed(b, vecs, pools, mv, rstd, xhat):
                vec.wait_ge(pools.sem, pools.after(b, "rstd"))
                for s in range(NS):
                    nc.vector.tensor_scalar(xhat[:, s], x_sb[:, bass.ds(times(b, NS, s), 1), :].rearrange("p o d -> p (o d)"),
                                            mv[:, s, 0:1], rstd[:, s:s + 1], ALU.subtract, ALU.mult).then_inc(vecs.sem, 1)

            def turn(b, s):
                qk = (chain_b, chain_a)[s][:, 0:2 * D].rearrange("p (h w) -> p h w", w=DK)
                w = DK // 2
                vec.wait_ge(act0.sem, act0.after(b, f"v{s}"))
                halves = (chain_b, chain_a)[s][:, 0:2 * D].rearrange("p (h w) -> p h w", w=w)
                nc.vector.tensor_tensor(turn_c[:, s].rearrange("p h (u w) -> p (h u) w", w=w), halves,
                                        cos[:, s].unsqueeze(1).broadcast_to([P, 4 * H, w]), ALU.mult).then_inc(vec0.sem, 1)
                sn = sin[:, s].unsqueeze(1).broadcast_to([P, 2 * H, w])
                nc.vector.scalar_tensor_tensor(out=turn_s[:, s, :, 0:w], in0=qk[:, :, w:], scalar=-1.0, in1=sn, op0=ALU.mult, op1=ALU.mult).then_inc(vec0.sem, 1)
                nc.vector.tensor_tensor(turn_s[:, s, :, w:], qk[:, :, 0:w], sn, ALU.mult).then_inc(vec0.sem, 1)

            def high_queries(b, s):
                vec.wait_ge(pool0.sem, pool0.after(b, f"turn{s}"))
                slots = qk_tok[:, b[1], s].rearrange("p h (c w) -> p h c w", w=DK)
                nc.vector.tensor_copy(slots[:, 0:H, 0:3:2, :], turned[:, s, 0:H].unsqueeze(2).broadcast_to([P, H, 2, DK])).then_inc(vec0.sem, 1)

            def max_of(b, k):
                vec.wait_ge(rows_ready, times(b, H, k + 1))
                nc.vector.tensor_reduce(nmax[:, k], row_bank[k % 2][:, 0:3 * P].rearrange("p (c t) -> p c t", t=P), AX.X, ALU.max, negate=True).then_inc(max_ready, 1)

            def place_max(b, half):
                vec.wait_ge(max_ready, times(b, H, 8 * (half + 1)))
                heads = slice(8 * half, 8 * half + 8)
                nc.vector.tensor_copy(qk_tok[:, b[1], 0, heads, 3 * DK], nmax[:, heads, 0]).then_inc(vec1.sem, 1)
                nc.vector.tensor_tensor(qk_tok[:, b[1], 1, heads, 3 * DK], nmax[:, heads, 1], nmax[:, heads, 2], ALU.min).then_inc(vec1.sem, 1)

            def divide(b, s):
                vec.wait_ge(pe3a.sem, pe3a.after(b, f"o{s}"))
                o = tail_bank[:].rearrange("p (h w) -> p h w", w=SLOT)
                nc.vector.reciprocal(rsum[:, s], o[:, :, DK]).then_inc(vec3a.sem, 1)
                vec.wait_ge(vec3a.sem, vec3a.after(b, f"rs{s}"))
                nc.vector.tensor_tensor(o_n[:, s].rearrange("p (h w) -> p h w", w=DK), o[:, :, 0:DK],
                                        rsum[:, s].unsqueeze(2).broadcast_to([P, H, DK]), ALU.mult).then_inc(vec3a.sem, 1)

            def low_out(b):
                vec.wait_ge(act3a.sem, act3a.after(b, "on_hi"))
                nc.vector.tensor_tensor(on_lo[:], tail_bank[:, 0:S], on_hi[:], ALU.subtract).then_inc(vec3a.sem, 1)

            def gate_out(b):
                m, par, _ = b
                vec.wait_ge(pe3a.sem, pe3a.after(b, "wo"))
                vec.wait_ge(mod_in[par], times((m, 0, 1), 16, 16))
                nc.vector.tensor_tensor(gated[:], tail_bank[:, 0:S].rearrange("p (s d) -> p s d", d=D),
                                        mod_b[:, par, 0:D].unsqueeze(1).broadcast_to([P, NS, D]), ALU.mult).then_inc(vec3a.sem, 1)

            def mean_square(b):
                vec.wait_ge(act3b.sem, act3b.after(b, "sq1"))
                nc.vector.tensor_scalar(ms[:], ssum[:], 1.0 / D, EPS_RMS, ALU.mult, ALU.add).then_inc(vec3b.sem, 1)

            def scale_norm(b):
                vec.wait_ge(pool3b.sem, pool3b.after(b, "rms"))
                for s in range(NS):
                    nc.vector.scalar_tensor_tensor(out=xn[:, s], in0=h_m[:, s], scalar=rms[:, s:s + 1], in1=lnw_sb[:], op0=ALU.mult, op1=ALU.mult).then_inc(vec3b.sem, 1)

            def route(b, part):
                if part == 0:
                    vec.wait_ge(pe3b.sem, pe3b.after(b, "logits"))
                    nc.vector.tensor_tensor(logits[:], tail_bank[:, 0:NS * E].rearrange("p (s e) -> p s e", e=E),
                                            bg_sb[:].unsqueeze(1).broadcast_to([P, NS, E]), ALU.add).then_inc(vec3b.sem, 1)
                if part == 1:
                    vec.wait_ge(vec3b.sem, vec3b.after(b, "logits"))
                    vec.nop(nofuse=True)
                    for s in range(NS):
                        nc.vector.max(top[:, s], logits[:, s]).then_inc(vec3b.sem, 1)
                    vec.wait_ge(vec3b.sem, vec3b.after(b, "max1"))
                    vec.nop(nofuse=True)
                    for s in range(NS):
                        nc.vector.max_index(top_i[:, s], top[:, s], logits[:, s]).then_inc(vec3b.sem, 1)
                if part == 2:
                    vec.wait_ge(vec3b.sem, vec3b.after(b, "idx1"))
                    nc.vector.tensor_copy(top_f[:], top_i[:, :, 0:K]).then_inc(vec3b.sem, 1)
                    vec.wait_ge(vec3b.sem, vec3b.after(b, "idxf"))
                    nc.vector.tensor_tensor(chosen[:], c32[:, C_E:C_E + E].unsqueeze(1).unsqueeze(1).broadcast_to([P, NS, K, E]),
                                            top_f[:].unsqueeze(3).broadcast_to([P, NS, K, E]), ALU.is_equal).then_inc(vec3b.sem, 1)
                    vec.wait_ge(vec3b.sem, vec3b.after(b, "chosen"))
                    nc.vector.tensor_tensor(member[:], chosen[:, :, 0], chosen[:, :, 1], ALU.add).then_inc(vec3b.sem, 1)
                    nc.vector.tensor_tensor(gap[:], top[:, :, 1], top[:, :, 0], ALU.subtract).then_inc(vec3b.sem, 1)

            def place(b, k):
                to_send = send[:, b[1]]
                if k == 0:
                    vec.wait_ge(pe_rank.sem, pe_rank.after(b, "ranks"))
                    nc.vector.tensor_tensor(rank[:], tail_bank[:, 0:NS * E].rearrange("p (s e) -> p s e", e=E),
                                            filled[:].unsqueeze(1).broadcast_to([P, NS, E]), ALU.add).then_inc(vec_place.sem, 1)
                    vec.wait_ge(vec_place.sem, vec_place.after(b, "rank"))
                    nc.vector.tensor_tensor(filled[:], filled[:], tail_bank[:, NS * E:(NS + 1) * E], ALU.add).then_inc(vec_place.sem, 1)
                if k == 1:
                    vec.wait_ge(act3b.sem, act3b.after(b, "egap"))
                    nc.vector.tensor_scalar(den[:], egap[:], 1.0, None, ALU.add).then_inc(vec_place.sem, 1)
                if k == 3:
                    vec.wait_ge(vec_place.sem, vec_place.after(b, "den"))
                    if due(times((b[0], 0, 1), 64)):
                        vec.wait_ge(sent[b[1]], times((b[0], 0, 1), 64))
                    nc.vector.reciprocal(to_send[:, 0, :, W_WGT], den[:]).then_inc(vec_place.sem, 1)
                    nc.vector.tensor_tensor(at_e[:], chosen[:], rank[:].unsqueeze(2).broadcast_to([P, NS, K, E]), ALU.mult).then_inc(vec_place.sem, 1)
                if k == 4:
                    vec.wait_ge(vec_place.sem, vec_place.after(b, "at"))
                    nc.vector.tensor_tensor(to_send[:, 1, :, W_WGT], to_send[:, 0, :, W_WGT], egap[:], ALU.mult).then_inc(vec_place.sem, 1)
                    nc.vector.tensor_reduce(pos_f[:], at_e[:], AX.X, ALU.add).then_inc(vec_place.sem, 1)
                if k == 8:
                    vec.wait_ge(vec_place.sem, vec_place.after(b, "pos_f"))
                    nc.vector.tensor_copy(pos_i[:, b[1]], pos_f[:]).then_inc(vec_place.sem, 1)
                    vec.wait_ge(pool3b.sem, pool3b.after(b, "xn_lo"))
                    nc.vector.tensor_copy(to_send[:, 1, :, 0:D], to_send[:, 0, :, 0:D]).then_inc(vec_place.sem, 1)
                    nc.vector.tensor_copy(to_send[:, :, :, W_IDX].bitcast(I32), tok[:]).then_inc(vec_place.sem, 1)
                if k == 9:
                    vec.wait_ge(vec_place.sem, vec_place.after(b, "tok"))
                    nc.vector.tensor_scalar(tok[:], tok[:], float(S * K), None, ALU.add).then_inc(vec_place.sem, 1)

            def iteration(i, placing, routing, closing, s2, s1, s0, norm):
                bn, b0, b1, ba, bb, bs = plus(i, 3), plus(i, 2), plus(i, 1), plus(i, -1), plus(i, -2), plus(i, -3)
                for k in range(H):
                    if s1:
                        max_of(b1, k)
                        if k == 7:
                            place_max(b1, 0)
                    if placing:
                        place(bs, k)
                    if s0:
                        if k in (5, 6):
                            turn(b0, k - 5)
                        if k in (7, 8):
                            high_queries(b0, k - 7)
                    if closing:
                        if k == 2:
                            divide(ba, 0)
                        if k == 4:
                            divide(ba, 1)
                        if k == 7:
                            low_out(ba)
                        if k == 9:
                            gate_out(ba)
                    if norm:
                        if k == 11:
                            if isinstance(bn[0], int) and times(bn, 1) == 0:
                                vec.wait_ge(x_in0, 16)
                            if isinstance(bn[0], int) and times(bn, 1) == 2:
                                vec.wait_ge(x_in1, 16)
                            moments(bn, vecn, st0, mv0, ve0)
                        if k == 13:
                            normed(bn, vecn, pooln, mv0, rstd0, xhat0)
                    if routing:
                        if k == 0:
                            vec.wait_ge(pool3a.sem, pool3a.after(bb, "resid"))
                            moments(bb, vec3b, st3, mv3, ve3)
                        if k == 3:
                            normed(bb, vec3b, pool3b, mv3, rstd3, xhat3)
                        if k == 7:
                            mean_square(bb)
                        if k == 9:
                            scale_norm(bb)
                        if k >= 13:
                            route(bb, k - 13)
                if s1:
                    place_max(b1, 1)

            vec.wait_ge(moe_consts_in, 16 * N_MOE_CONST)
            pipeline(vec, iteration)

            base, iota_j = c32[:, C_BASE:C_BASE + E], c32[:, C_J:C_J + NT + 1]
            vec.wait_ge(vec_place.sem, vec_place.after(number(B - 1), "tok_on"))
            nc.vector.tensor_copy(tab_i[:, 0], filled[:]).then_inc(table, 1)
            vec.wait_ge(table, 1)
            nc.vector.scalar_tensor_tensor(out=tab[:, 0], in0=filled[:], scalar=float(TS - 1), in1=base, op0=ALU.add, op1=ALU.subtract).then_inc(table, 1)
            vec.wait_ge(table, 2)
            nc.vector.tensor_copy(tab_i[:, 1], tab[:, 0]).then_inc(table, 1)
            vec.wait_ge(table, 3)
            nc.vector.tensor_scalar(tab_i[:, 1], tab_i[:, 1], TS.bit_length() - 1, None, ALU.logical_shift_right).then_inc(table, 1)
            vec.wait_ge(table, 4)
            nc.vector.tensor_copy(tab[:, 1], tab_i[:, 1]).then_inc(table, 1)
            vec.wait_ge(table, 5)
            nc.vector.memset(tab[:, 2], 0.0).then_inc(table, 1)
            vec.wait_ge(table, 6)
            nc.vector.tensor_tensor_scan(tab[:, 3], tab[:, 1], tab[:, 2], 0.0, ALU.add, ALU.add).then_inc(table, 1)
            ends = tab[:, 3].unsqueeze(1).broadcast_to([P, NT + 1, E])
            vec.wait_ge(table, 7)
            nc.vector.tensor_tensor(cmp_j[:], iota_j.unsqueeze(2).broadcast_to([P, NT + 1, E]), ends, ALU.is_ge).then_inc(table, 1)
            vec.wait_ge(table, 8)
            nc.vector.tensor_reduce(tj[:, 0], cmp_j[:], AX.X, ALU.add).then_inc(table, 1)
            vec.wait_ge(table, 9)
            nc.vector.tensor_tensor(cmp_j[:], cmp_j[:], tab[:, 1].unsqueeze(1).broadcast_to([P, NT + 1, E]), ALU.mult).then_inc(table, 1)
            vec.wait_ge(table, 10)
            nc.vector.tensor_reduce(tj[:, 1], cmp_j[:], AX.X, ALU.add).then_inc(table, 1)
            vec.wait_ge(table, 11)
            nc.vector.tensor_tensor(tj[:, 2], iota_j, tj[:, 1], ALU.subtract).then_inc(table, 1)
            vec.wait_ge(table, 12)
            nc.vector.tensor_scalar(tj[:, 3], tj[:, 0], float(REGION), None, ALU.mult).then_inc(table, 1)
            vec.wait_ge(table, 13)
            nc.vector.scalar_tensor_tensor(out=tj[:, 4], in0=tj[:, 2], scalar=float(TS), in1=tj[:, 3], op0=ALU.mult, op1=ALU.add).then_inc(table, 1)
            vec.wait_ge(table, 14)
            nc.vector.tensor_scalar(tj[:, 4], tj[:, 4], float(E * REGION), None, ALU.min).then_inc(table, 1)
            vec.wait_ge(table, 15)
            nc.vector.tensor_copy(tile_row[:], tj[:, 4]).then_inc(table, 1)
            vec.wait_ge(table, 16)
            nc.vector.tensor_scalar(tj[:, 0], tj[:, 0], float(E - 1), None, ALU.min).then_inc(table, 1)
            vec.wait_ge(table, 17)
            nc.vector.tensor_copy(tile_e[:], tj[:, 0]).then_inc(table, 1)
            vec.wait_ge(table, TABLE_STEPS)

            def low(j, f):
                vec.wait_ge(act_hh, times(j, FB, f + 1))
                nc.vector.tensor_tensor(hl[:, j[1] % 2, f], h32[:, f], hh[:, j[1] % 2, f], ALU.subtract).then_inc(vec_hl, 1)

            experts = experts_of(vec)

            def tile(j, finished=True):
                e, last, before_last = experts(j)
                if finished:
                    bias_out(plus(j, -2), before_last)
                for f in range(FB):
                    vec.wait_ge(act_silu, times(j, FB, f + 1))
                    if due(times(plus(j, -1), FB, f + 1)):
                        vec.wait_ge(vec_hl, times(plus(j, -1), FB, f + 1))
                    nc.vector.scalar_tensor_tensor(out=h32[:, f], in0=banks[f][:, TS:2 * TS], scalar=b1_sb[:, 1, bass.ds(e * FB + f, 1)],
                                                   in1=silu_a[:, f], op0=ALU.add, op1=ALU.mult).then_inc(vec_h, 1)
                    if f >= 2:
                        low(j, f - 2)
                low(j, FB - 2)
                low(j, FB - 1)
                return e, last

            def bias_out(j, e):
                vec.wait_ge(pe_y, times(j, 1, 1))
                if due(times(plus(j, -2), NS, NS)):
                    vec.wait_ge(act_y, times(plus(j, -2), NS, NS))
                y = (o_bank, tail_bank)[j[1] % 2]
                nc.vector.tensor_tensor(yb[:, j[1] % 2], y[:, 0:NS * D].rearrange("p (s d) -> p s d", d=D),
                                        b2_sb[:, bass.ds(e, 1), :].broadcast_to([P, NS, D]), ALU.add).then_inc(vec_y, 1)

            tile(tile_number(0), finished=False)
            tile(tile_number(1), finished=False)
            in_fours(vec, 2, NT - 1, tile)
            e, last = tile(tile_number(NT - 1))
            bias_out(tile_number(NT - 2), last)
            bias_out(tile_number(NT - 1), e)

            vec.wait_ge(gb_in, 16)

            def finish(n):
                m, r, _ = n
                vec.wait_ge(pool_sum, times(n, 1, 1))
                nc.vector.tensor_tensor(ygate[:, r % 2], ysum[:, r % 2], gb_sb[:, bass.ds(times(n, 1), 1), :].broadcast_to([P, NS, D]), ALU.mult).then_inc(vec_gate, 1)
                vec.wait_ge(vec_gate, times(n, 1, 1))
                if due(times((m, 0, 1), 16)):
                    vec.wait_ge(out_done[r], times((m, 0, 1), 16))
                nc.vector.tensor_tensor(res[:, r], ygate[:, r % 2], x_sb[:, bass.ds(times(n, NS), NS), :], ALU.add).then_inc(vec_res, 1)

            in_fours(vec, 0, B, finish)

        @block.tensor
        def _(pe):
            mm = nc.tensor.matmul

            def halves(o, l_hi, l_lo, r_hi, r_lo, start=True, stop=True):
                mm(o, l_hi, r_hi, start=start, stop=False, skip_group_check=True)
                mm(o, l_hi, r_lo, start=False, stop=False, skip_group_check=True)
                return mm(o, l_lo, r_hi, start=False, stop=stop, skip_group_check=True)

            pe.wait_ge(consts_in, 16 * N_CONST)
            for n in range(2):
                at = slice(E * FB * (n + 1), E * FB * (n + 2))
                nc.tensor.transpose(banks[0][:, at], b1_rows[:, n, :], ident32[0:E * FB, 0:E * FB])
            nc.tensor.transpose(banks[0][:, 0:B], c_sb[:], ident32[0:B, 0:B]).then_inc(setup_pe.sem, 1)
            for n in range(4):
                t = nc.tensor.transpose(banks[2][:, D * n:D * n + D], wraw[:, n, :], ident32[:])
            t.then_inc(setup_pe.sem, 1)
            pe.wait_ge(setup_act.sem, 1)
            for n in range(2):
                mm(banks[1][:, B * n:B * n + B], wmod_sb[:, D * n:D * n + D], silu_c[:], start=(n == 0), stop=True, skip_group_check=True)
            mm(banks[3][0:B, :], silu_c[:], wmod_sb[:, 2 * D:6 * D], start=True, stop=True).then_inc(setup_pe.sem, 1)
            pe.wait_ge(setup_vec.sem, 4)
            pe.wait_ge(init_vec, 4)
            pe.wait_ge(init_pool, 5)

            def project(b, s):
                at = slice(P * s, P * s + P)
                o = (chain_b, chain_a)[s][:, 0:3 * D]
                halves(o, ht_hi[:, at], ht_lo[:, at], w_hi[:, 0:3, :].rearrange("p n d -> p (n d)"), w_lo[:, 0:3, :].rearrange("p n d -> p (n d)")).then_inc(pe0.sem, 1)

            def turn_tile(b, s):
                o = (chain_a16, chain_b16)[s]
                tok_q = qk_tok[:, b[1], s].rearrange("p (j g) w -> p j (g w)", g=HG)
                for j in range(2 * HG):
                    t = nc.tensor.transpose(o[:, P * j:P * j + P], tok_q[:, j, :], ident16)
                t.then_inc(pe0.sem, 1)

            def turn_max(b, half):
                for j in range(2):
                    for s in range(NS):
                        q = qk_tok[:, b[1], s].rearrange("p (j g) w -> p j (g w)", g=HG)[:, 2 * half + j, :]
                        t = nc.tensor.transpose(chain_b16[:, S * j + P * s:S * j + P * s + P], q, ident16)
                t.then_inc(pe1.sem, 1)

            def masks(o, mask):
                diagonal = o[:, 0:4 * P].rearrange("p (c t) -> p c t", t=2 * P)[:, :, 0:P]
                return mm(diagonal, ident16, mask.unsqueeze(1).broadcast_to([P, 2, P]), start=False, stop=True, skip_group_check=True)

            def scores_by_query(b, k):
                j, par = k // HG, b[1]
                if k % 8 < HG:
                    pe.wait_ge(pad_in[k // 8][par][k % HG], times((b[0], 0, 1), 16, 16))
                if due(times(b, H, k - 1)):
                    pe.wait_ge(max_ready, times(b, H, k - 1))
                o = row_bank[k % 2]
                mm(o[:, 0:P], qk_t[:, par, j, 0:P], k_pad[:, par, k, 0:P], start=True, stop=False, skip_group_check=True)
                mm(o[:, P:3 * P], qk_t[:, par, j, P:], k_pad[:, par, k, :], start=False, stop=False, skip_group_check=True)
                masks(o, mask_q).then_inc(rows_ready, 1)

            def scores_by_key(b, k):
                j, par = k // HG, b[1]
                if k % 8 == 0:
                    pe.wait_ge(act1.sem, act1.after(b, "ev" + "ab"[k // 8]))
                if due(times(b, H, k - 1)):
                    pe.wait_ge(probs_ready, times(b, H, k - 1))
                o = col_bank[k % 2]
                mm(o[:, 0:S], k_pad[:, par, k, 0:P], q_max[:, par, j, :], start=True, stop=False, skip_group_check=True)
                mm(o[:, S:S + P], k_pad[:, par, k, P:], q_max[:, par, j, P:], start=False, stop=False, skip_group_check=True)
                masks(o, mask_k).then_inc(cols_ready, 1)

            def values(b, k):
                g, par = k % HG, b[1]
                if g == 0:
                    if due(times(b, HG, k // HG)):
                        pe.wait_ge(group_saved, times(b, HG, k // HG))
                pe.wait_ge(probs_ready, times(b, H, k + 1))
                at = slice(SLOT * g, SLOT * g + SLOT)
                mm(o_bank[at, 0:S], v_aug[:, par, 0, k, :], probs[:, k % 4, 0:S], start=True, stop=False, skip_group_check=True)
                mm(o_bank[at, P:S], v_aug[:, par, 1, k, :], probs[:, k % 4, S:], start=False, stop=True, skip_group_check=True).then_inc(probs_used, 1)

            def out_rows(b, s):
                if s == 0:
                    pe.wait_ge(group_saved, times(b, HG, HG))
                    if due(vec_place.after(plus(b, -2), "filled")):
                        pe.wait_ge(vec_place.sem, vec_place.after(plus(b, -2), "filled"))
                else:
                    pe.wait_ge(vec3a.sem, vec3a.after(b, "on0"))
                for j in range(HG):
                    t = nc.tensor.transpose(tail_bank[:, P * j:P * j + P], o_t[:, b[1], j, P * s:P * s + P], ident32[:])
                t.then_inc(pe3a.sem, 1)

            def ranks(b):
                pe.wait_ge(vec3b.sem, vec3b.after(b, "member"))
                two = member[:].rearrange("p s e -> p (s e)")
                mm(tail_bank[:, 0:2 * E], before16, two, start=True, stop=False, skip_group_check=True)
                mm(tail_bank[:, E:2 * E], ones16, member[:, 0], start=False, stop=False, skip_group_check=True)
                mm(tail_bank[:, 2 * E:3 * E], ones16, member[:, 0], start=False, stop=False, skip_group_check=True)
                mm(tail_bank[:, 2 * E:3 * E], ones16, member[:, 1], start=False, stop=True, skip_group_check=True).then_inc(pe_rank.sem, 1)

            def iteration(i, placing, routing, closing, s2, s1, s0, norm):
                b0, b1, ba, bb, bs = plus(i, 2), plus(i, 1), plus(i, -1), plus(i, -2), plus(i, -3)
                for k in range(H):
                    if s1:
                        scores_by_query(b1, k)
                    if s2:
                        scores_by_key(i, k)
                        if k:
                            values(i, k - 1)
                    if k == 0 and placing:
                        ranks(bs)
                    if k == 1 and s2:
                        pe.wait_ge(vec1.sem, vec1.after(i, "m1b"))
                        if s1:
                            pe.wait_ge(act0.sem, act0.after(b1, "ev1"))
                        turn_max(i, 1)
                    if k == 9 and s1:
                        if s0:
                            pe.wait_ge(vec0.sem, vec0.after(b0, "sin0b"))
                        elif s2:
                            pe.wait_ge(act1.sem, act1.after(i, "evb"))
                        pe.wait_ge(vec1.sem, vec1.after(b1, "m1a"))
                        turn_max(b1, 0)
                    if s0:
                        if k == 0:
                            pe.wait_ge(vecn.sem, vecn.after(b0, "xhat1"))
                            if due(act0.after(plus(b0, -1), "ev0")):
                                pe.wait_ge(act0.sem, act0.after(plus(b0, -1), "ev0"))
                            for s in range(NS):
                                t = nc.tensor.transpose(chain_a[:, P * s:P * s + P], xhat0[:, s], ident32[:])
                            t.then_inc(pe0.sem, 1)
                        if k == 3:
                            pe.wait_ge(pool0.sem, pool0.after(b0, "h_lo"))
                            if due(act0.after(plus(b0, -1), "ev1")):
                                pe.wait_ge(act0.sem, act0.after(plus(b0, -1), "ev1"))
                            if s2:
                                pe.wait_ge(act1.sem, act1.after(i, "evb"))
                            project(b0, 0)
                        if k == 4:
                            project(b0, 1)
                        if k == 10:
                            pe.wait_ge(vec0.sem, vec0.after(b0, "sin1b"))
                            pe.wait_ge(pool0.sem, pool0.after(b0, "klo0"))
                            turn_tile(b0, 0)
                        if k == 12:
                            pe.wait_ge(pool0.sem, pool0.after(b0, "klo1"))
                            if s1:
                                pe.wait_ge(act1.sem, act1.after(b1, "eva"))
                            turn_tile(b0, 1)
                    if closing:
                        if k == 2:
                            out_rows(ba, 0)
                        if k == 4:
                            out_rows(ba, 1)
                        if k == 6:
                            pe.wait_ge(vec3a.sem, vec3a.after(ba, "on1"))
                            for s in range(NS):
                                t = nc.tensor.transpose(tail_bank[:, P * s:P * s + P], o_n[:, s], ident32[:])
                            t.then_inc(pe3a.sem, 1)
                        if k == 9:
                            pe.wait_ge(vec3a.sem, vec3a.after(ba, "on_lo"))
                            for s in range(NS):
                                at = slice(P * s, P * s + P)
                                t = halves(tail_bank[:, at], on_hi[:, at], on_lo[:, at], w_hi[:, 3], w_lo[:, 3], start=(s == 0))
                            t.then_inc(pe3a.sem, 1)
                    if routing:
                        if k == 11:
                            if closing:
                                pe.wait_ge(vec3a.sem, vec3a.after(ba, "gated"))
                            pe.wait_ge(vec3b.sem, vec3b.after(bb, "xn1"))
                            for s in range(NS):
                                t = nc.tensor.transpose(tail_bank[:, P * s:P * s + P], xn[:, s], ident32[:])
                            t.then_inc(pe3b.sem, 1)
                        if k == 13:
                            pe.wait_ge(act3b.sem, act3b.after(bb, "xn_t"))
                            for s in range(NS):
                                t = mm(tail_bank[:, E * s:E * s + E], xn_t[:, P * s:P * s + P], wg_sb[:], start=(s == 0), stop=True, skip_group_check=True)
                            t.then_inc(pe3b.sem, 1)
                if s2:
                    values(i, H - 1)

            pipeline(pe, iteration)

            pe.wait_ge(table, TABLE_STEPS)

            def turn_rows(j):
                r = j[1]
                pe.wait_ge(g_arrived[r], times((j[0], 0, 1), 16, 16))
                if due(times(plus(j, -2), 1, 1)):
                    pe.wait_ge(act_x, times(plus(j, -2), 1, 1))
                o = (chain_a16, chain_b16)[r % 2]
                for h in range(2):
                    for s in range(NS):
                        words = g_in[:, r, s, 0:D].bitcast(F16)
                        t = nc.tensor.transpose(o[:, TS * h + P * s:TS * h + P * s + P], words[:, D * h:D * h + D], ident16)
                t.then_inc(pe_x, 1)

            experts = experts_of(pe)

            def hidden(j, more=True):
                e, last, _ = experts(j)
                x_hi, x_lo = xt[:, j[1] % 2, 0, :], xt[:, j[1] % 2, 1, :]
                pe.wait_ge(act_x, times(j, 1, 1))
                for f in range(FB):
                    if due(times(plus(j, -1), FB, f + 1)):
                        pe.wait_ge(vec_h, times(plus(j, -1), FB, f + 1))
                    at = bass.ds(e * F + f * P, P)
                    for n in range(2):
                        o = banks[f][:, TS * n:TS * n + TS]
                        mm(o, we_hi[:, n, at], x_hi, start=(n == 0), stop=False, skip_group_check=True)
                        mm(o, we_hi[:, n, at], x_lo, start=False, stop=False, skip_group_check=True)
                        t = mm(o, we_lo[:, n, at], x_hi, start=False, stop=True, skip_group_check=True)
                    t.then_inc(pe_ab, 1)
                    if f == 1 and more:
                        turn_rows(plus(j, 1))
                return e, last

            def project_out(j, e):
                par = j[1] % 2
                pe.wait_ge(vec_hl, times(j, FB, FB))
                if due(times(plus(j, -2), 1, 1)):
                    pe.wait_ge(vec_y, times(plus(j, -2), 1, 1))
                y = (o_bank, tail_bank)[par]
                for f in range(FB):
                    at = bass.ds(e * F + f * P, P)
                    for s in range(NS):
                        o = y[:, D * s:D * s + D]
                        tok_s = slice(P * s, P * s + P)
                        mm(o, hh[:, par, f, tok_s], we_hi[:, 2, at], start=(s == 0 and f == 0), stop=False, skip_group_check=True)
                        mm(o, hh[:, par, f, tok_s], we_lo[:, 2, at], start=False, stop=False, skip_group_check=True)
                        t = mm(o, hl[:, par, f, tok_s], we_hi[:, 2, at], start=False, stop=(f == FB - 1), skip_group_check=True)
                t.then_inc(pe_y, 1)

            def tile_and_last(j, more=True):
                e, last = hidden(j, more)
                project_out(plus(j, -1), last)
                return e

            turn_rows(tile_number(0))
            hidden(tile_number(0))
            in_fours(pe, 1, NT - 1, tile_and_last)
            project_out(tile_number(NT - 1), tile_and_last(tile_number(NT - 1), False))


def constants():
    f = np.float32
    theta = (f(1.0) / f(10000.0) ** (np.arange(0, DK, 2, dtype=f) / f(DK))).astype(f)
    angle = np.outer(np.arange(S, dtype=f), theta).astype(f).reshape(NS, P, DK // 2).transpose(1, 0, 2).reshape(P, -1)
    p = np.arange(P)
    c = np.zeros((P, NC32 + P), f)
    c[:, C_COS:C_COS + 8] = np.cos(angle)
    c[:, C_SIN:C_SIN + 8] = np.sin(angle)
    c[:, C_E:C_E + E] = np.arange(E)
    c[:, C_BASE:C_BASE + E] = np.arange(E) * REGION
    for k in range(K):
        for s in range(NS):
            c[:, C_TOK + k * NS + s] = K * (s * P + p) + k
    c[:, C_POW:C_POW + 4] = -0.5
    c[:, C_J:C_J + NT + 1] = np.arange(NT + 1)
    c[:, NC32:] = np.eye(P)
    c16 = np.stack([np.eye(P), p[:, None] < p[None, :], np.ones((P, P))], 1).astype(np.float16)
    after = p[None, :] > p[:, None]
    masks = np.stack([np.where(after, MASKED, 0.0), np.where(after.T, MASKED, 0.0)], 1)
    dummy = np.zeros((TS, ROWW), f)
    dummy[:, W_IDX] = (NOUT + np.arange(TS)).astype(np.int32).view(f)
    return c, c16, masks, dummy


_INS = ['L0_attn_x', 'L0_attn_W_Q', 'L0_attn_W_K', 'L0_attn_W_V', 'L0_attn_W_O', 'L0_ffn_ln_w', 'L0_ffn_Wg', 'L0_ffn_bg',
        'L0_ffn_W1a', 'L0_ffn_b1a', 'L0_ffn_W1b', 'L0_ffn_b1b', 'L0_ffn_W2', 'L0_ffn_b2', 'L0_c', 'L0_wmod']


def kernel(**inputs):
    import ml_dtypes
    import concourse.bacc as _bacc
    from concourse import mybir as _mybir
    from concourse.bass_utils import run_bass_kernel_spmd as _run

    nc = _bacc.Bacc("TRN2", target_bir_lowering=False, num_devices=1)
    c, c16, masks, dummy = constants()
    arrays, args = {}, []
    named = [(name, np.ascontiguousarray(inputs[name])) for name in _INS]
    named += [("const32", c), ("const16", c16), ("constb", masks.astype(ml_dtypes.bfloat16)), ("dummy", dummy)]
    for name, a in named:
        arrays[f"in_{name}_dram"] = a
        args.append(nc.dram_tensor(f"in_{name}_dram", a.shape, _mybir.dt.from_np(a.dtype), kind="ExternalInput").ap())
    o = nc.dram_tensor("out_0_dram", (B, S, D), F32, kind="ExternalOutput").ap()
    build(nc, *args, o)
    r = _run(nc, [arrays], core_ids=[0])
    return r.results[0]["out_0_dram"]
```

```python
from contextlib import ExitStack

import numpy as np

import concourse.bass as bass
from concourse import mybir

F32 = mybir.dt.float32
F16 = mybir.dt.float16
BF16 = mybir.dt.bfloat16
I32 = mybir.dt.int32
U32 = mybir.dt.uint32
ALU = mybir.AluOpType
ACT = mybir.ActivationFunctionType
AX = mybir.AxisListType

P = 128
B, S, D = 16, 256, 128
H, DK = 16, 8
E, K, F = 8, 2, 512
NS = S // P
HG = 4
SLOT = P // HG
FB = F // P
TS = 256
NT = (B * S * K + E * (TS - 1)) // TS
REGION = B * S + TS
ROWS = E * REGION + TS
ROWW = D + 4
W_IDX, W_WGT = D, D + 1
NOUT = B * S * K
CHUNK = F // NS
SM_SCALE = float(1.0 / np.sqrt(np.float32(DK)))
EPS_LN = 1e-5
EPS_RMS = float(np.finfo(np.float32).eps)
MASKED = -1e30
C_COS, C_SIN, C_E, C_BASE, C_TOK, C_POW, C_J = 0, 8, 16, 24, 32, 36, 40
NC32 = C_J + NT + 1


class Steps:

    def __init__(self, sem, names):
        self.sem, self.names = sem, names.split()

    def after(self, n, name):
        return times(n, len(self.names), self.names.index(name) + 1)


def times(n, k, c=0):
    m, r, unroll = n
    return m * (unroll * k) + (r * k + c)


def plus(n, by):
    m, r, unroll = n
    return m + (r + by) // unroll, (r + by) % unroll, unroll


def due(count):
    return not isinstance(count, int) or count > 0


def build(nc, x_in, wq, wk, wv, wo, ln_w, wg, bg, w1a, b1a, w1b, b1b, w2, b2, c_in, wmod, const32,
          const16, constb, dummy_in, out):
    ctx = ExitStack()
    with ctx:
        def sb(name, shape, dt=F32):
            return ctx.enter_context(nc.sbuf_tensor(name, shape, dt))

        def sem(name):
            return ctx.enter_context(nc.semaphore(name))

        def steps(name, names):
            return Steps(sem(name), names)

        mod_rows = nc.dram_tensor("mod_rows", [B, 4 * D], F32).ap()
        rows = nc.dram_tensor("expert_rows", [ROWS, ROWW], F32).ap()
        outs = nc.dram_tensor("expert_outs", [NOUT, D], F32).ap()

        c32 = sb("c32", [P, NC32])
        c16 = sb("c16", [P, 3, P], F16)
        cb = sb("cb", [P, 2, P], BF16)
        ident32 = sb("ident32", [P, P])
        ident16, before16, ones16 = c16[:, 0, :], c16[:, 1, :], c16[:, 2, :]
        mask_q, mask_k = cb[:, 0, :], cb[:, 1, :]
        wraw = sb("wraw", [P, 4, D])
        wmod_sb = sb("wmod_sb", [P, 6 * D])
        c_sb = sb("c_sb", [B, D])
        silu_c = sb("silu_c", [P, B])
        mod_sb = sb("mod_sb", [B, 4 * D])
        mod_t = sb("mod_t", [P, B])
        scale_in = sb("scale_in", [P, B])
        shift_in = sb("shift_in", [P, B])
        w_hi = sb("w_hi", [P, 4, D], F16)
        w_lo = sb("w_lo", [P, 4, D], F16)
        wg_sb = sb("wg_sb", [P, E])
        bg_sb = sb("bg_sb", [P, E])
        lnw_sb = sb("lnw_sb", [P, D])
        b1_rows = sb("b1_rows", [E * FB, 2, P])
        b1_sb = sb("b1_sb", [P, 2, E * FB])
        b2_sb = sb("b2_sb", [P, E, D])
        we_hi = sb("we_hi", [P, 3, E * F], F16)
        we_lo = sb("we_lo", [P, 3, E * F], F16)
        dummy_sb = sb("dummy_sb", [P, NS, ROWW])
        x_sb = sb("x_sb", [P, B * NS, D])
        wstage = sb("wstage", [P, 2, 3, CHUNK])
        st0 = sb("st0", [P, NS, 6])
        mv0 = sb("mv0", [P, NS, 2])
        ve0 = sb("ve0", [P, NS])
        rstd0 = sb("rstd0", [P, NS])
        xhat0 = sb("xhat0", [P, NS, D])
        ht32 = sb("ht32", [P, S])
        ht_hi = sb("ht_hi", [P, S], F16)
        ht_lo = sb("ht_lo", [P, S], F16)
        turn_c = sb("turn_c", [P, NS, 2 * H, DK])
        turn_s = sb("turn_s", [P, NS, 2 * H, DK])
        turned = sb("turned", [P, NS, 2 * H, DK])
        v_sb = sb("v_sb", [P, 2, NS, D])
        qk_tok = sb("qk_tok", [P, 2, NS, 2 * H, SLOT], F16)
        qk_t = sb("qk_t", [P, 2, 2 * HG, S], F16)
        k_pad = sb("k_pad", [P, 2, H, S], F16)
        nmax = sb("nmax", [P, H, 3])
        q_max = sb("q_max", [P, 2, HG, S], F16)
        v_aug = sb("v_aug", [P, 2, NS, H, SLOT])
        probs = sb("probs", [P, 4, S + P])
        o_t = sb("o_t", [P, 2, HG, S])
        mod_b = sb("mod_b", [P, 2, 4 * D])
        rsum = sb("rsum", [P, NS, H])
        o_n = sb("o_n", [P, NS, D])
        on_hi = sb("on_hi", [P, S], F16)
        on_lo = sb("on_lo", [P, S], F16)
        gated = sb("gated", [P, NS, D])
        st3 = sb("st3", [P, NS, 6])
        mv3 = sb("mv3", [P, NS, 2])
        ve3 = sb("ve3", [P, NS])
        rstd3 = sb("rstd3", [P, NS])
        xhat3 = sb("xhat3", [P, NS, D])
        h_s = sb("h_s", [P, NS, D])
        h_m = sb("h_m", [P, NS, D])
        square = sb("square", [P, NS, D])
        ssum = sb("ssum", [P, NS])
        ms = sb("ms", [P, NS])
        rms = sb("rms", [P, NS])
        xn = sb("xn", [P, NS, D])
        xn_t = sb("xn_t", [P, S])
        logits = sb("logits", [P, NS, E])
        top = sb("top", [P, NS, 8])
        top_i = sb("top_i", [P, NS, 8], U32)
        top_f = sb("top_f", [P, NS, K])
        chosen = sb("chosen", [P, NS, K, E])
        member = sb("member", [P, NS, E], F16)
        gap = sb("gap", [P, NS])
        egap = sb("egap", [P, NS])
        den = sb("den", [P, NS])
        rank = sb("rank", [P, NS, E])
        filled = sb("filled", [P, E])
        at_e = sb("at_e", [P, NS, K, E])
        pos_f = sb("pos_f", [P, NS, K])
        pos_i = sb("pos_i", [P, 2, NS, K], I32)
        tok = sb("tok", [P, K, NS])
        send = sb("send", [P, 2, K, NS, ROWW])
        tab = sb("tab", [P, 8, E])
        tab_i = sb("tab_i", [P, 2, E], I32)
        cmp_j = sb("cmp_j", [P, NT + 1, E])
        tj = sb("tj", [P, 5, NT + 1])
        tile_e = sb("tile_e", [P, NT + 1], I32)
        tile_row = sb("tile_row", [P, NT + 1], I32)
        g_in = sb("g_in", [P, 4, NS, ROWW])
        number_of = sb("number_of", [P, 4, NS], I32)
        weight_of = sb("weight_of", [P, 4, NS])
        xt = sb("xt", [P, 2, 2, TS], F16)
        silu_a = sb("silu_a", [P, FB, TS])
        h32 = sb("h32", [P, FB, TS])
        hh = sb("hh", [P, 2, FB, TS], F16)
        hl = sb("hl", [P, 2, FB, TS], F16)
        yb = sb("yb", [P, 2, NS, D])
        y_sb = sb("y_sb", [P, 4, NS, D])
        gb_sb = k_pad[:, 0].rearrange("p h t -> p (h t)").bitcast(F32).rearrange("p (b d) -> p b d", d=D)
        free = we_lo[:].rearrange("p n f -> p (n f)").bitcast(F32)

        def last(start, blocks):
            return free[:, start * NS * D:(start + blocks) * NS * D]

        y_in = last(0, 8).rearrange("p (r s k d) -> p r s k d", s=NS, k=K, d=D)
        ysum = last(8, 4).rearrange("p (r s d) -> p r s d", s=NS, d=D)
        ygate = last(12, 4).rearrange("p (r s d) -> p r s d", s=NS, d=D)
        res = last(16, 4).rearrange("p (r s d) -> p r s d", s=NS, d=D)

        banks = [ctx.enter_context(nc.psum_tensor(f"bank{i}", [P, 512], F32)) for i in range(8)]
        row_bank, col_bank = banks[0:2], banks[2:4]
        o_bank, chain_a, chain_b, tail_bank = banks[4:8]
        chain_a16, chain_b16 = chain_a[:].bitcast(F16), chain_b[:].bitcast(F16)

        c_in_sem, w_in_sem, wmod_in_sem, consts_in = sem("c_in"), sem("w_in"), sem("wmod_in"), sem("consts_in")
        b1_in_sem, dummy_in_sem = sem("b1_in"), sem("dummy_in")
        x_in0, x_in1 = sem("x_in0"), sem("x_in1")
        moe_consts_in = sem("moe_consts_in")
        dummies_out = sem("dummies_out")
        mod_out, gb_in = sem("mod_out"), sem("gb_in")
        init_vec, init_pool = sem("init_vec"), sem("init_pool")
        setup_pe = steps("setup_pe", "c_t w_t mod_t b1_t")
        setup_act = steps("setup_act", "silu w_hi b1")
        setup_vec = steps("setup_vec", "scale shift copied w_lo abs_a abs_b sign_a sign_b sgn_a sgn_b gate_a gate_b plus1")
        wstage_in = [sem("wstage_in0"), sem("wstage_in1")]
        mod_in = [sem("mod_in0"), sem("mod_in1")]
        pad_in = [[[sem(f"pad_in{h}{p}{g}") for g in range(HG)] for p in range(2)] for h in range(2)]
        pe0 = steps("pe0", "x_t proj0 proj1 t0 t1")
        vecn = steps("vecn", "stats0 stats1 aggr0 aggr1 var xhat0 xhat1")
        pooln = steps("pooln", "rstd")
        vec0 = steps("vec0", "cos0 sin0a sin0b cos1 sin1a sin1b hi0 hi1")
        act0 = steps("act0", "h32 h_hi v0 v1 khi0 khi1 ev0 ev1_keys ev1 w_hi")
        pool0 = steps("pool0", "h_lo zero_m turn0 turn1 qlo0 klo0 qlo1 klo1 w_lo")
        rows_ready, max_ready = sem("rows_ready"), sem("max_ready")
        vec1 = steps("vec1", "m0a m1a m0b m1b")
        pe1 = steps("pe1", "ta tb")
        act1 = steps("act1", "v_aug eva evb")
        cols_ready, probs_ready, probs_used, group_saved = sem("cols_ready"), sem("probs_ready"), sem("probs_used"), sem("group_saved")
        pe3a = steps("pe3a", "o0 o1 on_t wo")
        vec3a = steps("vec3a", "rs0 on0 rs1 on1 on_lo gated")
        act3a = steps("act3a", "on_hi")
        pool3a = steps("pool3a", "resid")
        pe3b = steps("pe3b", "xn_t logits")
        vec3b = steps("vec3b", "stats0 stats1 aggr0 aggr1 var xhat0 xhat1 ms xn0 xn1 logits max0 max1 idx0 idx1 idxf chosen member gap")
        act3b = steps("act3b", "sq0 sq1 xn_t xn_hi egap")
        act_place = steps("act_place", "copy")
        pool3b = steps("pool3b", "rstd scaled shifted rms xn_lo")
        pe_rank = steps("pe_rank", "ranks")
        vec_place = steps("vec_place", "rank filled den w1 at w2 pos_f pos_i tok tok_on")
        sent = [sem("sent0"), sem("sent1")]
        table = sem("table")
        padded = sem("padded")
        g_arrived = [sem(f"g_arrived{r}") for r in range(4)]
        named = steps("named", "number weight")
        pe_x = sem("pe_x")
        act_x = sem("act_x")
        pe_ab, act_silu, vec_h, act_hh, vec_hl = sem("pe_ab"), sem("act_silu"), sem("vec_h"), sem("act_hh"), sem("vec_hl")
        pe_y, vec_y, act_y = sem("pe_y"), sem("vec_y"), sem("act_y")
        y_sent = [sem(f"y_sent{r}") for r in range(4)]
        y_back = [sem(f"y_back{r}") for r in range(4)]
        pool_sum, vec_gate, vec_res = sem("pool_sum"), sem("vec_gate"), sem("vec_res")
        out_done = [sem(f"out_done{r}") for r in range(4)]

        TABLE_STEPS = 18
        N_CONST = 3
        N_MOE_CONST = 4

        def number(n):
            return n // 2, n % 2, 2

        def pipeline(eng, iteration):
            def one(i):
                iteration(number(i), *(0 <= i + n < B for n in (-3, -2, -1, 0, 1, 2, 3)))
            for i in range(-3, 5):
                one(i)
            with eng.Fori(2, (B - 3) // 2) as m:
                iteration((m, 1, 2), *[True] * 7)
                iteration((m + 1, 0, 2), *[True] * 7)
            for i in range(B - 3, B + 3):
                one(i)

        def is_first(i, n):
            return isinstance(i[0], int) and times(i, 1) == n

        def tile_number(n):
            return n // 4, n % 4, 4

        def experts_of(eng):
            regs = [eng.alloc_register(f"expert{r}") for r in range(4)]
            before = [eng.alloc_register(f"expert_before{r}") for r in range(2)]

            def known(j):
                r = j[1]
                all_known = before + regs
                return [eng.snap(all_known[2 + r - n], min_val=0, max_val=E - 1) for n in range(3)]

            def read_next(j):
                m, r, _ = j
                if r == 3:
                    for n in range(2):
                        eng.reg_mov(before[n], regs[2 + n])
                    eng.load(regs, tile_e[0:1, bass.ds(4 * (m + 1), 4)])

            for n in range(2):
                eng.reg_mov(before[n], 0)
            eng.load(regs, tile_e[0:1, 0:4])
            return known, read_next

        def pad_experts(eng, first):
            ends = [eng.alloc_register(f"end{n}") for n in range(4)]
            eng.load(ends, tab_i[0:1, 0, first:first + 4])
            for end in ends:
                v = eng.snap(end, min_val=0, max_val=ROWS - TS)
                eng.dma_start(rows[bass.ds(v, TS), :].rearrange("(s p) w -> p s w", p=P), dummy_sb[:]).then_inc(padded, 16)

        def in_fours(eng, first, end, body):
            start = max(4, (first + 3) // 4 * 4)
            for n in range(first, start):
                body((n // 4, n % 4, 4))
            eights = (end - start) // 8
            with eng.Fori(0, eights) as q:
                for r in range(8):
                    body((2 * q + (start // 4 + r // 4), r % 4, 4))
            for n in range(start + 8 * eights, end):
                body((n // 4, n % 4, 4))

        x_view = x_in.rearrange("b (s p) d -> p (b s) d", p=P)
        w1a_v = w1a.rearrange("e d (h f) -> e h d f", h=NS)
        w1b_v = w1b.rearrange("e d (h f) -> e h d f", h=NS)
        w2_v = w2.rearrange("e (h c f) d -> e h f c d", h=NS, f=P)

        block = ctx.enter_context(nc.Block())

        @block.sync
        def _(sp):
            sp.dma_start(c_sb[:], c_in).then_inc(c_in_sem, 16)
            sp.dma_start(ident32[:], const32[:, NC32:NC32 + P]).then_inc(c_in_sem, 16)
            sp.dma_start(x_sb[:, 0:4, :], x_view[:, 0:4, :]).then_inc(x_in0, 16)
            for n, w in enumerate((wq, wk, wv, wo)):
                sp.dma_start(wraw[:, n, :], w).then_inc(w_in_sem, 16)
            sp.dma_start(x_sb[:, 4:, :], x_view[:, 4:, :]).then_inc(x_in1, 16)
            sp.dma_start(wg_sb[:], wg).then_inc(moe_consts_in, 16)
            sp.dma_start(lnw_sb[:], ln_w.unsqueeze(0).broadcast_to([P, D])).then_inc(moe_consts_in, 16)
            sp.dma_start(bg_sb[:], bg.unsqueeze(0).broadcast_to([P, E])).then_inc(moe_consts_in, 16)
            sp.dma_start(b2_sb[:], b2.unsqueeze(0).broadcast_to([P, E, D])).then_inc(moe_consts_in, 16)
            for n, b1 in enumerate((b1a, b1b)):
                sp.dma_start(b1_rows[:, n, :], b1.rearrange("e (c f) -> (e c) f", f=P)).then_inc(b1_in_sem, 16)
            sp.dma_start(dummy_sb[:], dummy_in.rearrange("(s p) w -> p s w", p=P)).then_inc(dummy_in_sem, 16)
            sp.wait_ge(init_pool, 2)

            def iteration(i, placing, routing, closing, s2, s1, s0, norm):
                if is_first(i, -1):
                    sp.wait_ge(setup_vec.sem, len(setup_vec.names))
                    sp.dma_start(mod_rows, mod_sb[:]).then_inc(mod_out, 16)
                    sp.wait_ge(dummy_in_sem, 16)
                    sp.dma_start(rows[E * REGION:, :].rearrange("(s p) w -> p s w", p=P), dummy_sb[:]).then_inc(dummies_out, 16)
                if is_first(i, 0):
                    sp.wait_ge(mod_out, 16)
                if s0:
                    b = plus(i, 2)
                    m, par, _ = b
                    if due(pool0.after(plus(b, -2), "w_lo")):
                        sp.wait_ge(pool0.sem, pool0.after(plus(b, -2), "w_lo"))
                    sp.dma_start(wstage[:, par, 0, :], w1a_v[m, par]).then_inc(wstage_in[par], 16)
                    sp.dma_start(wstage[:, par, 1, :], w1b_v[m, par]).then_inc(wstage_in[par], 16)
                    sp.dma_start(wstage[:, par, 2, :].rearrange("p (c d) -> p c d", d=D), w2_v[m, par]).then_inc(wstage_in[par], 16)
                if s2:
                    m, par, _ = i
                    if due(pool3b.after(plus(i, -2), "shifted")):
                        sp.wait_ge(pool3b.sem, pool3b.after(plus(i, -2), "shifted"))
                    sp.dma_start(mod_b[:, par, :], mod_rows[bass.ds(times(i, 1), 1), :].broadcast_to([P, 4 * D])).then_inc(mod_in[par], 16)
                if s0:
                    b = plus(i, 2)
                    par = b[1]
                    sp.wait_ge(act0.sem, act0.after(b, "ev1_keys"))
                    for half in range(2):
                        if due(times(plus(b, -2), H, 8 * (half + 1))):
                            sp.wait_ge(cols_ready, times(plus(b, -2), H, 8 * (half + 1)))
                        for g in range(HG):
                            at = slice(SLOT * g, SLOT * g + SLOT)
                            heads = k_pad[at, par, :, :].rearrange("p (j g) t -> p j g t", g=HG)[:, 2 * half:2 * half + 2, g, :]
                            sp.dma_start(heads, qk_t[at, par, HG + 2 * half:HG + 2 * half + 2, :]).then_inc(pad_in[half][par][g], 16)

            pipeline(sp, iteration)

            sp.wait_ge(cols_ready, B * H)
            sp.dma_start(gb_sb, mod_rows[:, 3 * D:].unsqueeze(0).broadcast_to([P, B, D])).then_inc(gb_in, 16)
            sp.wait_ge(table, 1)
            pad_experts(sp, 0)
            sp.wait_ge(padded, 16 * E)
            sp.wait_ge(sent[0], 64 * B // 2)
            sp.wait_ge(sent[1], 64 * B // 2)
            sp.wait_ge(dummies_out, 16)
            sp.wait_ge(table, TABLE_STEPS)

            def load(j):
                r = j[1]
                if due(times(plus(j, -4), 1, 1)):
                    sp.wait_ge(pe_x, times(plus(j, -4), 1, 1))
                    sp.nop(nofuse=True)
                    sp.wait_ge(named.sem, named.after(plus(j, -4), "weight"))
                    sp.nop(nofuse=True)
                v = sp.value_load(tile_row[0:1, bass.ds(times(j, 1), 1)], min_val=0, max_val=ROWS - TS)
                sp.dma_start(g_in[:, r, :, :], rows[bass.ds(v, TS), :].rearrange("(s p) w -> p s w", p=P)).then_inc(g_arrived[r], 16)

            in_fours(sp, 0, NT, load)

            for r in range(4):
                sp.wait_ge(y_sent[r], 32 * ((NT - r + 3) // 4))
            back = outs.rearrange("(b s p k) d -> b p s k d", s=NS, p=P, k=K)

            def finish(n):
                m, r, _ = n
                if due(times(plus(n, -4), 1, 1)):
                    sp.wait_ge(pool_sum, times(plus(n, -4), 1, 1))
                sp.dma_start(y_in[:, r], back[times(n, 1)]).then_inc(y_back[r], 16)

            in_fours(sp, 0, B, finish)
            for r in range(4):
                sp.wait_ge(out_done[r], 16 * (B // 4))

        @block.gpsimd
        def _(pool):
            for par in range(2):
                nc.gpsimd.memset(k_pad[:, par].rearrange("p h t -> p (h t)").bitcast(F32), 0.0).then_inc(init_pool, 1)
            nc.gpsimd.memset(v_aug[:], 0.0).then_inc(init_pool, 1)
            pool.wait_ge(init_pool, 3)
            nc.gpsimd.memset(v_aug[:, :, :, :, DK:DK + 1], 1.0).then_inc(init_pool, 1)
            nc.gpsimd.memset(send[:], 0.0).then_inc(init_pool, 1)
            pool.wait_ge(consts_in, 16 * N_CONST)
            pool.wait_ge(init_vec, 2)
            power = c32[:, C_POW:C_POW + NS]

            def send_rows(b, n):
                s, k = n // K, n % K
                pool.wait_ge(vec_place.sem, vec_place.after(b, "tok"))
                pool.wait_ge(act_place.sem, act_place.after(b, "copy"))
                pool.nop(nofuse=True)
                pool.indirect_dma_start(out=rows, out_offset=bass.IndirectOffsetOnAxis(ap=pos_i[:, b[1], s, k:k + 1], axis=0),
                                        in_=send[:, b[1], k, s, :], in_offset=None).then_inc(sent[b[1]], 16)

            def iteration(i, placing, routing, closing, s2, s1, s0, norm):
                bn, b0, ba, bb, bs = plus(i, 3), plus(i, 2), plus(i, -1), plus(i, -2), plus(i, -3)
                if s0:
                    pool.wait_ge(act0.sem, act0.after(b0, "h_hi"))
                    nc.gpsimd.tensor_tensor(ht_lo[:], ht32[:], ht_hi[:], ALU.subtract).then_inc(pool0.sem, 1)
                    if due(pe1.after(plus(b0, -2), "tb")):
                        pool.wait_ge(pe1.sem, pe1.after(plus(b0, -2), "tb"))
                    pool.nop(nofuse=True)
                    nc.gpsimd.memset(qk_tok[:, b0[1], :, 0:H, 3 * DK:3 * DK + 1], 0.0).then_inc(pool0.sem, 1)
                if routing:
                    par = bb[1]
                    pool.wait_ge(vec3b.sem, vec3b.after(bb, "var"))
                    nc.gpsimd.tensor_tensor(rstd3[:], ve3[:], power, ALU.pow).then_inc(pool3b.sem, 1)
                    pool.wait_ge(vec3b.sem, vec3b.after(bb, "xhat1"))
                    nc.gpsimd.tensor_tensor(h_s[:], xhat3[:], mod_b[:, par, 2 * D:3 * D].unsqueeze(1).broadcast_to([P, NS, D]), ALU.mult).then_inc(pool3b.sem, 1)
                    pool.wait_ge(pool3b.sem, pool3b.after(bb, "scaled"))
                    nc.gpsimd.tensor_tensor(h_m[:], h_s[:], mod_b[:, par, D:2 * D].unsqueeze(1).broadcast_to([P, NS, D]), ALU.add).then_inc(pool3b.sem, 1)
                if s0:
                    add_turned(b0, 0)
                    add_turned(b0, 1)
                if routing:
                    pool.wait_ge(vec3b.sem, vec3b.after(bb, "ms"))
                    nc.gpsimd.tensor_tensor(rms[:], ms[:], power, ALU.pow).then_inc(pool3b.sem, 1)
                if s0:
                    low_parts(b0, 0)
                    low_parts(b0, 1)
                if norm:
                    pool.wait_ge(vecn.sem, vecn.after(bn, "var"))
                    nc.gpsimd.tensor_tensor(rstd0[:], ve0[:], power, ALU.pow).then_inc(pooln.sem, 1)
                if placing:
                    for n in range(3):
                        send_rows(bs, n)
                if routing:
                    pool.wait_ge(act3b.sem, act3b.after(bb, "xn_hi"))
                    words = send[:, bb[1], 0, :, 0:D].bitcast(F16)
                    nc.gpsimd.tensor_tensor(words[:, :, D:2 * D], xn[:], words[:, :, 0:D], ALU.subtract).then_inc(pool3b.sem, 1)
                if closing:
                    pool.wait_ge(vec3a.sem, vec3a.after(ba, "gated"))
                    xs = x_sb[:, bass.ds(times(ba, NS), NS), :]
                    nc.gpsimd.tensor_tensor(xs, xs, gated[:], ALU.add).then_inc(pool3a.sem, 1)
                if placing:
                    send_rows(bs, 3)
                if s0:
                    at = bass.ds(times(b0, CHUNK), CHUNK)
                    pool.wait_ge(act0.sem, act0.after(b0, "w_hi"))
                    nc.gpsimd.tensor_tensor(we_lo[:, :, at], wstage[:, b0[1]], we_hi[:, :, at], ALU.subtract).then_inc(pool0.sem, 1)

            def add_turned(b, s):
                pool.wait_ge(vec0.sem, vec0.after(b, f"sin{s}b"))
                nc.gpsimd.tensor_tensor(turned[:, s], turn_c[:, s], turn_s[:, s], ALU.add).then_inc(pool0.sem, 1)

            def low_parts(b, s):
                slots = qk_tok[:, b[1], s].rearrange("p h (c w) -> p h c w", w=DK)
                pool.wait_ge(vec0.sem, vec0.after(b, f"hi{s}"))
                nc.gpsimd.tensor_tensor(slots[:, 0:H, 1, :], turned[:, s, 0:H], slots[:, 0:H, 0, :], ALU.subtract).then_inc(pool0.sem, 1)
                pool.wait_ge(act0.sem, act0.after(b, f"khi{s}"))
                nc.gpsimd.tensor_tensor(slots[:, H:, 2, :], turned[:, s, H:], slots[:, H:, 0, :], ALU.subtract).then_inc(pool0.sem, 1)

            pipeline(pool, iteration)

            def name_rows(j):
                m, r, _ = j
                pool.wait_ge(g_arrived[r], times((m, 0, 1), 16, 16))
                if due(times((m, 0, 1), 32)):
                    pool.wait_ge(y_sent[r], times((m, 0, 1), 32))
                pool.nop(nofuse=True)
                nc.gpsimd.tensor_copy(number_of[:, r], g_in[:, r, :, W_IDX].bitcast(I32)).then_inc(named.sem, 1)
                nc.gpsimd.tensor_copy(weight_of[:, r], g_in[:, r, :, W_WGT]).then_inc(named.sem, 1)

            def scatter(j, more=True):
                r = j[1]
                if more:
                    name_rows(plus(j, 2))
                pool.wait_ge(act_y, times(j, NS, NS))
                pool.nop(nofuse=True)
                for s in range(NS):
                    pool.indirect_dma_start(out=outs, out_offset=bass.IndirectOffsetOnAxis(ap=number_of[:, r, s:s + 1], axis=0),
                                            in_=y_sb[:, r, s, :], in_offset=None, bounds_check=NOUT - 1, oob_is_err=False).then_inc(y_sent[r], 16)

            name_rows(tile_number(0))
            name_rows(tile_number(1))
            in_fours(pool, 0, NT - 2, scatter)
            scatter(tile_number(NT - 2), False)
            scatter(tile_number(NT - 1), False)

            def finish(n):
                m, r, _ = n
                pool.wait_ge(y_back[r], times((m, 0, 1), 16, 16))
                if due(times(plus(n, -4), 1, 1)):
                    pool.wait_ge(vec_gate, times(plus(n, -4), 1, 1))
                nc.gpsimd.tensor_tensor(ysum[:, r], y_in[:, r, :, 0, :], y_in[:, r, :, 1, :], ALU.add).then_inc(pool_sum, 1)

            in_fours(pool, 0, B, finish)

        @block.scalar
        def _(act):
            nc.scalar.preload_act_table(ACT.Silu)
            act.dma_start(wmod_sb[:], wmod).then_inc(wmod_in_sem, 16)
            act.dma_start(c32[:], const32[:, 0:NC32]).then_inc(consts_in, 16)
            act.dma_start(c16[:], const16).then_inc(consts_in, 16)
            act.dma_start(cb[:], constb).then_inc(consts_in, 16)
            act.wait_ge(setup_pe.sem, 1)
            nc.scalar.activation(silu_c[:], banks[0][:, 0:B], ACT.Silu).then_inc(setup_act.sem, 1)
            nc.scalar.preload_act_table(ACT.Exp)
            act.wait_ge(setup_pe.sem, 2)
            nc.scalar.activation(w_hi[:], banks[2][:].rearrange("p (n d) -> p n d", d=D), ACT.Copy).then_inc(setup_act.sem, 1)
            act.wait_ge(setup_vec.sem, 2)
            act.wait_ge(init_pool, 4)

            def iteration(i, placing, routing, closing, s2, s1, s0, norm):
                b0, b1, ba, bb, bs = plus(i, 2), plus(i, 1), plus(i, -1), plus(i, -2), plus(i, -3)
                if is_first(i, -1):
                    act.wait_ge(setup_pe.sem, 4)
                    nc.scalar.activation(b1_sb[:], o_bank[:, 0:2 * E * FB].rearrange("p (n c) -> p n c", n=2), ACT.Copy).then_inc(setup_act.sem, 1)
                for k in range(H):
                    if s2:
                        act.wait_ge(cols_ready, times(i, H, k + 1))
                        if due(times(i, H, k - 3)):
                            act.wait_ge(probs_used, times(i, H, k - 3))
                        nc.scalar.activation(probs[:, k % 4], col_bank[k % 2][:, 0:S + P], ACT.Exp, scale=SM_SCALE).then_inc(probs_ready, 1)
                        if k % HG == 1 and k > 1:
                            save_group(i, k // HG - 1)
                    if closing and k == 1:
                        save_group(ba, HG - 1)
                    if s2 and k == 1:
                        save_queries(i, 1)
                    if s1:
                        if k == 2:
                            act.wait_ge(act0.sem, act0.after(b1, "v1"))
                            nc.scalar.activation(v_aug[:, b1[1], :, :, 0:DK], v_sb[:, b1[1]].rearrange("p s (h w) -> p s h w", w=DK), ACT.Copy).then_inc(act1.sem, 1)
                        if k == 9:
                            save_queries(b1, 0)
                    if placing and k == 3:
                        act.wait_ge(pool3b.sem, pool3b.after(bs, "xn_lo"))
                        nc.scalar.activation(send[:, bs[1], 1, :, 0:D].bitcast(F16), send[:, bs[1], 0, :, 0:D].bitcast(F16), ACT.Copy).then_inc(act_place.sem, 1)
                    if closing and k == 10:
                        act.wait_ge(pe3a.sem, pe3a.after(ba, "on_t"))
                        nc.scalar.activation(on_hi[:], tail_bank[:, 0:S], ACT.Copy).then_inc(act3a.sem, 1)
                    if routing:
                        if k == 6:
                            act.wait_ge(pool3b.sem, pool3b.after(bb, "shifted"))
                            for t in range(NS):
                                nc.scalar.activation(square[:, t], h_m[:, t], ACT.Square, accum_out=ssum[:, t:t + 1]).then_inc(act3b.sem, 1)
                        if k == 12:
                            act.wait_ge(pe3b.sem, pe3b.after(bb, "xn_t"))
                            nc.scalar.activation(xn_t[:], chain_a[:, 0:S], ACT.Copy).then_inc(act3b.sem, 1)
                        if k == 13:
                            if due(times((bb[0], 0, 1), 64)):
                                act.wait_ge(sent[bb[1]], times((bb[0], 0, 1), 64))
                            nc.scalar.activation(send[:, bb[1], 0, :, 0:D].bitcast(F16)[:, :, 0:D], xn[:], ACT.Copy).then_inc(act3b.sem, 1)
                        if k == 15:
                            act.wait_ge(vec3b.sem, vec3b.after(bb, "gap"))
                            nc.scalar.activation(egap[:], gap[:], ACT.Exp).then_inc(act3b.sem, 1)
                    if s0:
                        if k == 0:
                            act.wait_ge(pe0.sem, pe0.after(b0, "x_t"))
                            at = bass.ds(times(b0, 1), 1)
                            nc.scalar.activation(ht32[:], chain_a[:, 0:S], ACT.Identity, scale=scale_in[:, at], bias=shift_in[:, at]).then_inc(act0.sem, 1)
                            nc.scalar.activation(ht_hi[:], chain_a[:, 0:S], ACT.Identity, scale=scale_in[:, at], bias=shift_in[:, at]).then_inc(act0.sem, 1)
                        if k in (3, 4):
                            t = (3, 4).index(k)
                            act.wait_ge(pe0.sem, pe0.after(b0, f"proj{t}"))
                            nc.scalar.activation(v_sb[:, b0[1], t, :], (chain_b, chain_a)[t][:, 2 * D:3 * D], ACT.Copy).then_inc(act0.sem, 1)
                        if k in (7, 8):
                            t = (7, 8).index(k)
                            act.wait_ge(pool0.sem, pool0.after(b0, f"turn{t}"))
                            slots = qk_tok[:, b0[1], t].rearrange("p h (c w) -> p h c w", w=DK)
                            nc.scalar.activation(slots[:, H:, 0:2, :], turned[:, t, H:].unsqueeze(2).broadcast_to([P, H, 2, DK]), ACT.Copy).then_inc(act0.sem, 1)
                        if k in (10, 12):
                            t = (10, 12).index(k)
                            act.wait_ge(pe0.sem, pe0.after(b0, f"t{t}"))
                            half = (chain_a16, chain_b16)[t]
                            half = half.rearrange("p (j t) -> p j t", t=P)
                            if t == 0:
                                nc.scalar.activation(qk_t[:, b0[1], :, 0:P], half, ACT.Copy).then_inc(act0.sem, 1)
                            else:
                                nc.scalar.activation(qk_t[:, b0[1], HG:, P:], half[:, HG:], ACT.Copy).then_inc(act0.sem, 1)
                                nc.scalar.activation(qk_t[:, b0[1], 0:HG, P:], half[:, 0:HG], ACT.Copy).then_inc(act0.sem, 1)
                        if k == 14:
                            act.wait_ge(wstage_in[b0[1]], times((b0[0], 0, 1), 48, 48))
                            nc.scalar.activation(we_hi[:, :, bass.ds(times(b0, CHUNK), CHUNK)], wstage[:, b0[1]], ACT.Copy).then_inc(act0.sem, 1)

            def save_group(b, j):
                act.wait_ge(probs_used, times(b, H, HG * (j + 1)))
                nc.scalar.activation(o_t[:, b[1], j, :], o_bank[:, 0:S], ACT.Copy).then_inc(group_saved, 1)

            def save_queries(b, half):
                act.wait_ge(pe1.sem, pe1.after(b, "t" + "ab"[half]))
                nc.scalar.activation(q_max[:, b[1], 2 * half:2 * half + 2, :], chain_b16[:, 0:2 * S].rearrange("p (j t) -> p j t", t=S), ACT.Copy).then_inc(act1.sem, 1)

            pipeline(act, iteration)

            nc.scalar.preload_act_table(ACT.Silu)
            act.wait_ge(table, 1)
            pad_experts(act, 4)
            act.wait_ge(table, TABLE_STEPS)

            def save_x(j):
                act.wait_ge(pe_x, times(j, 1, 1))
                if due(times(plus(j, -2), FB, FB)):
                    act.wait_ge(pe_ab, times(plus(j, -2), FB, FB))
                nc.scalar.activation(xt[:, j[1] % 2], (chain_a16, chain_b16)[j[1] % 2][:, 0:2 * TS].rearrange("p (h t) -> p h t", t=TS), ACT.Copy).then_inc(act_x, 1)

            def high(j, f):
                act.wait_ge(vec_h, times(j, FB, f + 1))
                if due(times(plus(j, -2), 1, 1)):
                    act.wait_ge(pe_y, times(plus(j, -2), 1, 1))
                nc.scalar.activation(hh[:, j[1] % 2, f], h32[:, f], ACT.Copy).then_inc(act_hh, 1)

            def weigh(j):
                r = j[1]
                if due(times((j[0], 0, 1), 32)):
                    act.wait_ge(y_sent[r], times((j[0], 0, 1), 32))
                act.wait_ge(vec_y, times(j, 1, 1))
                act.wait_ge(named.sem, named.after(j, "weight"))
                for s in range(NS):
                    nc.scalar.activation(y_sb[:, r, s], yb[:, r % 2, s], ACT.Copy, scale=weight_of[:, r, s:s + 1]).then_inc(act_y, 1)

            known_experts, read_next_experts = experts_of(act)

            def tile(j, more=True, finished=True):
                e = known_experts(j)[0]
                for f in range(FB):
                    act.wait_ge(pe_ab, times(j, FB, f + 1))
                    if due(times(plus(j, -1), FB, f + 1)):
                        act.wait_ge(vec_h, times(plus(j, -1), FB, f + 1))
                    nc.scalar.activation(silu_a[:, f], banks[f][:, 0:TS], ACT.Silu, bias=b1_sb[:, 0, bass.ds(e * FB + f, 1)]).then_inc(act_silu, 1)
                    if f == 1 and more:
                        save_x(plus(j, 1))
                    if f == 2 and finished:
                        weigh(plus(j, -2))
                    if f == 2:
                        read_next_experts(j)
                    if f:
                        high(j, f - 1)
                high(j, FB - 1)

            save_x(tile_number(0))
            tile(tile_number(0), finished=False)
            tile(tile_number(1), finished=False)
            in_fours(act, 2, NT - 1, tile)
            tile(tile_number(NT - 1), more=False)
            weigh(tile_number(NT - 2))
            weigh(tile_number(NT - 1))

            out_v = out.rearrange("b (s p) d -> b p s d", p=P)

            def store(n):
                m, r, _ = n
                act.wait_ge(vec_res, times(n, 1, 1))
                act.dma_start(out_v[times(n, 1)], res[:, r]).then_inc(out_done[r], 16)

            in_fours(act, 0, B, store)

        @block.vector
        def _(vec):
            nc.vector.memset(qk_tok[:], 0.0).then_inc(init_vec, 1)
            vec.wait_ge(init_vec, 1)
            nc.vector.memset(qk_tok[:, :, :, H:, 3 * DK:3 * DK + 1], 1.0).then_inc(init_vec, 1)

            cos = c32[:, C_COS:C_COS + 8].rearrange("p (s w) -> p s w", w=DK // 2)
            sin = c32[:, C_SIN:C_SIN + 8].rearrange("p (s w) -> p s w", w=DK // 2)

            def statistics(b, vecs, st):
                for s in range(NS):
                    nc.vector.bn_stats(st[:, s], x_sb[:, bass.ds(times(b, NS, s), 1), :].rearrange("p o d -> p (o d)")).then_inc(vecs.sem, 1)

            def moments(b, vecs, st, mv):
                vec.wait_ge(vecs.sem, vecs.after(b, "stats1"))
                vec.nop(nofuse=True)
                for s in range(NS):
                    nc.vector.bn_aggr(mv[:, s], st[:, s]).then_inc(vecs.sem, 1)

            def variance(b, vecs, mv, ve):
                vec.wait_ge(vecs.sem, vecs.after(b, "aggr1"))
                nc.vector.tensor_scalar(ve[:], mv[:, :, 1], EPS_LN, None, ALU.add).then_inc(vecs.sem, 1)

            def normed(b, vecs, pools, mv, rstd, xhat):
                vec.wait_ge(pools.sem, pools.after(b, "rstd"))
                for s in range(NS):
                    nc.vector.tensor_scalar(xhat[:, s], x_sb[:, bass.ds(times(b, NS, s), 1), :].rearrange("p o d -> p (o d)"),
                                            mv[:, s, 0:1], rstd[:, s:s + 1], ALU.subtract, ALU.mult).then_inc(vecs.sem, 1)

            def turn(b, s):
                qk = (chain_b, chain_a)[s][:, 0:2 * D].rearrange("p (h w) -> p h w", w=DK)
                w = DK // 2
                vec.wait_ge(act0.sem, act0.after(b, f"v{s}"))
                halves = (chain_b, chain_a)[s][:, 0:2 * D].rearrange("p (h w) -> p h w", w=w)
                nc.vector.tensor_tensor(turn_c[:, s].rearrange("p h (u w) -> p (h u) w", w=w), halves,
                                        cos[:, s].unsqueeze(1).broadcast_to([P, 4 * H, w]), ALU.mult).then_inc(vec0.sem, 1)
                sn = sin[:, s].unsqueeze(1).broadcast_to([P, 2 * H, w])
                nc.vector.scalar_tensor_tensor(out=turn_s[:, s, :, 0:w], in0=qk[:, :, w:], scalar=-1.0, in1=sn, op0=ALU.mult, op1=ALU.mult).then_inc(vec0.sem, 1)
                nc.vector.tensor_tensor(turn_s[:, s, :, w:], qk[:, :, 0:w], sn, ALU.mult).then_inc(vec0.sem, 1)

            def high_queries(b, s):
                vec.wait_ge(pool0.sem, pool0.after(b, f"turn{s}"))
                slots = qk_tok[:, b[1], s].rearrange("p h (c w) -> p h c w", w=DK)
                nc.vector.tensor_copy(slots[:, 0:H, 0:3:2, :], turned[:, s, 0:H].unsqueeze(2).broadcast_to([P, H, 2, DK])).then_inc(vec0.sem, 1)

            def max_of(b, k):
                vec.wait_ge(rows_ready, times(b, H, k + 1))
                nc.vector.tensor_reduce(nmax[:, k], row_bank[k % 2][:, 0:3 * P].rearrange("p (c t) -> p c t", t=P), AX.X, ALU.max, negate=True).then_inc(max_ready, 1)

            def place_max(b, half):
                vec.wait_ge(max_ready, times(b, H, 8 * (half + 1)))
                heads = slice(8 * half, 8 * half + 8)
                nc.vector.tensor_copy(qk_tok[:, b[1], 0, heads, 3 * DK], nmax[:, heads, 0]).then_inc(vec1.sem, 1)
                nc.vector.tensor_tensor(qk_tok[:, b[1], 1, heads, 3 * DK], nmax[:, heads, 1], nmax[:, heads, 2], ALU.min).then_inc(vec1.sem, 1)

            def divide(b, s):
                vec.wait_ge(pe3a.sem, pe3a.after(b, f"o{s}"))
                o = tail_bank[:].rearrange("p (h w) -> p h w", w=SLOT)
                nc.vector.reciprocal(rsum[:, s], o[:, :, DK]).then_inc(vec3a.sem, 1)
                vec.wait_ge(vec3a.sem, vec3a.after(b, f"rs{s}"))
                nc.vector.tensor_tensor(o_n[:, s].rearrange("p (h w) -> p h w", w=DK), o[:, :, 0:DK],
                                        rsum[:, s].unsqueeze(2).broadcast_to([P, H, DK]), ALU.mult).then_inc(vec3a.sem, 1)

            def low_out(b):
                vec.wait_ge(act3a.sem, act3a.after(b, "on_hi"))
                nc.vector.tensor_tensor(on_lo[:], tail_bank[:, 0:S], on_hi[:], ALU.subtract).then_inc(vec3a.sem, 1)

            def gate_out(b):
                m, par, _ = b
                vec.wait_ge(pe3a.sem, pe3a.after(b, "wo"))
                vec.wait_ge(mod_in[par], times((m, 0, 1), 16, 16))
                nc.vector.tensor_tensor(gated[:], tail_bank[:, 0:S].rearrange("p (s d) -> p s d", d=D),
                                        mod_b[:, par, 0:D].unsqueeze(1).broadcast_to([P, NS, D]), ALU.mult).then_inc(vec3a.sem, 1)

            def mean_square(b):
                vec.wait_ge(act3b.sem, act3b.after(b, "sq1"))
                nc.vector.tensor_scalar(ms[:], ssum[:], 1.0 / D, EPS_RMS, ALU.mult, ALU.add).then_inc(vec3b.sem, 1)

            def scale_norm(b):
                vec.wait_ge(pool3b.sem, pool3b.after(b, "rms"))
                for s in range(NS):
                    nc.vector.scalar_tensor_tensor(out=xn[:, s], in0=h_m[:, s], scalar=rms[:, s:s + 1], in1=lnw_sb[:], op0=ALU.mult, op1=ALU.mult).then_inc(vec3b.sem, 1)

            def route(b, part):
                if part == 0:
                    vec.wait_ge(pe3b.sem, pe3b.after(b, "logits"))
                    nc.vector.tensor_tensor(logits[:], chain_a[:, 0:NS * E].rearrange("p (s e) -> p s e", e=E),
                                            bg_sb[:].unsqueeze(1).broadcast_to([P, NS, E]), ALU.add).then_inc(vec3b.sem, 1)
                if part == 1:
                    vec.wait_ge(vec3b.sem, vec3b.after(b, "logits"))
                    vec.nop(nofuse=True)
                    for s in range(NS):
                        nc.vector.max(top[:, s], logits[:, s]).then_inc(vec3b.sem, 1)
                    vec.wait_ge(vec3b.sem, vec3b.after(b, "max1"))
                    vec.nop(nofuse=True)
                    for s in range(NS):
                        nc.vector.max_index(top_i[:, s], top[:, s], logits[:, s]).then_inc(vec3b.sem, 1)
                if part == 2:
                    vec.wait_ge(vec3b.sem, vec3b.after(b, "idx1"))
                    nc.vector.tensor_copy(top_f[:], top_i[:, :, 0:K]).then_inc(vec3b.sem, 1)
                    vec.wait_ge(vec3b.sem, vec3b.after(b, "idxf"))
                    nc.vector.tensor_tensor(chosen[:], c32[:, C_E:C_E + E].unsqueeze(1).unsqueeze(1).broadcast_to([P, NS, K, E]),
                                            top_f[:].unsqueeze(3).broadcast_to([P, NS, K, E]), ALU.is_equal).then_inc(vec3b.sem, 1)
                    vec.wait_ge(vec3b.sem, vec3b.after(b, "chosen"))
                    nc.vector.tensor_tensor(member[:], chosen[:, :, 0], chosen[:, :, 1], ALU.add).then_inc(vec3b.sem, 1)
                    nc.vector.tensor_tensor(gap[:], top[:, :, 1], top[:, :, 0], ALU.subtract).then_inc(vec3b.sem, 1)

            def place(b, k):
                to_send = send[:, b[1]]
                if k == 0:
                    vec.wait_ge(pe_rank.sem, pe_rank.after(b, "ranks"))
                    nc.vector.tensor_tensor(rank[:], tail_bank[:, 0:NS * E].rearrange("p (s e) -> p s e", e=E),
                                            filled[:].unsqueeze(1).broadcast_to([P, NS, E]), ALU.add).then_inc(vec_place.sem, 1)
                    vec.wait_ge(vec_place.sem, vec_place.after(b, "rank"))
                    nc.vector.tensor_tensor(filled[:], filled[:], tail_bank[:, NS * E:(NS + 1) * E], ALU.add).then_inc(vec_place.sem, 1)
                if k == 1:
                    vec.wait_ge(act3b.sem, act3b.after(b, "egap"))
                    nc.vector.tensor_scalar(den[:], egap[:], 1.0, None, ALU.add).then_inc(vec_place.sem, 1)
                if k == 2:
                    vec.wait_ge(vec_place.sem, vec_place.after(b, "den"))
                    if due(times((b[0], 0, 1), 64)):
                        vec.wait_ge(sent[b[1]], times((b[0], 0, 1), 64))
                    nc.vector.reciprocal(to_send[:, 0, :, W_WGT], den[:]).then_inc(vec_place.sem, 1)
                    nc.vector.tensor_tensor(at_e[:], chosen[:], rank[:].unsqueeze(2).broadcast_to([P, NS, K, E]), ALU.mult).then_inc(vec_place.sem, 1)
                if k == 3:
                    vec.wait_ge(vec_place.sem, vec_place.after(b, "at"))
                    nc.vector.tensor_tensor(to_send[:, 1, :, W_WGT], to_send[:, 0, :, W_WGT], egap[:], ALU.mult).then_inc(vec_place.sem, 1)
                    nc.vector.tensor_reduce(pos_f[:], at_e[:], AX.X, ALU.add).then_inc(vec_place.sem, 1)
                if k == 9:
                    vec.wait_ge(vec_place.sem, vec_place.after(b, "pos_f"))
                    nc.vector.tensor_copy(pos_i[:, b[1]], pos_f[:]).then_inc(vec_place.sem, 1)
                    nc.vector.tensor_copy(to_send[:, :, :, W_IDX].bitcast(I32), tok[:]).then_inc(vec_place.sem, 1)
                if k == 10:
                    vec.wait_ge(vec_place.sem, vec_place.after(b, "tok"))
                    nc.vector.tensor_scalar(tok[:], tok[:], float(S * K), None, ALU.add).then_inc(vec_place.sem, 1)

            def iteration(i, placing, routing, closing, s2, s1, s0, norm):
                bn, b0, b1, ba, bb, bs = plus(i, 3), plus(i, 2), plus(i, 1), plus(i, -1), plus(i, -2), plus(i, -3)
                if is_first(i, -2):
                    set_up()
                if is_first(i, 0):
                    vec.wait_ge(moe_consts_in, 16 * N_MOE_CONST)
                for k in range(H):
                    if s1:
                        max_of(b1, k)
                        if k == 7:
                            place_max(b1, 0)
                    if s0:
                        if k in (4, 5):
                            turn(b0, (4, 5).index(k))
                        if k in (8, 9):
                            high_queries(b0, (8, 9).index(k))
                    if closing:
                        if k == 3:
                            divide(ba, 0)
                        if k == 8:
                            divide(ba, 1)
                        if k == 11:
                            low_out(ba)
                        if k == 15:
                            gate_out(ba)
                    if norm:
                        if k == 7:
                            if is_first(bn, 0):
                                vec.wait_ge(x_in0, 16)
                            if is_first(bn, 2):
                                vec.wait_ge(x_in1, 16)
                            statistics(bn, vecn, st0)
                        if k == 8:
                            moments(bn, vecn, st0, mv0)
                        if k == 9:
                            variance(bn, vecn, mv0, ve0)
                        if k == 13:
                            normed(bn, vecn, pooln, mv0, rstd0, xhat0)
                    if routing:
                        if k == 0:
                            vec.wait_ge(pool3a.sem, pool3a.after(bb, "resid"))
                            statistics(bb, vec3b, st3)
                        if k == 1:
                            moments(bb, vec3b, st3, mv3)
                        if k == 3:
                            normed(bb, vec3b, pool3b, mv3, rstd3, xhat3)
                        if k == 7:
                            mean_square(bb)
                        if k == 9:
                            scale_norm(bb)
                        if k >= 13:
                            route(bb, k - 13)
                    if placing:
                        place(bs, k)
                    if routing and k == 1:
                        variance(bb, vec3b, mv3, ve3)
                if s1:
                    place_max(b1, 1)

            def set_up():
                vec.wait_ge(setup_pe.sem, 3)
                nc.vector.tensor_scalar(scale_in[:], banks[1][:, B:2 * B], 1.0, None, ALU.add).then_inc(setup_vec.sem, 1)
                nc.vector.tensor_copy(shift_in[:], banks[1][:, 0:B]).then_inc(setup_vec.sem, 1)
                nc.vector.tensor_copy(mod_sb[:], banks[3][0:B, :]).then_inc(setup_vec.sem, 1)
                vec.wait_ge(setup_act.sem, 2)
                nc.vector.tensor_tensor(w_lo[:], banks[2][:].rearrange("p (n d) -> p n d", d=D), w_hi[:], ALU.subtract).then_inc(setup_vec.sem, 1)
                gate = mod_sb[:].rearrange("p (g d) -> p g d", d=D)
                vec.wait_ge(setup_vec.sem, 4)
                for n, g in ((0, 0), (1, 3)):
                    nc.vector.tensor_scalar(square[0:B, n, :], gate[:, g], -1.0, None, ALU.mult).then_inc(setup_vec.sem, 1)
                vec.wait_ge(setup_vec.sem, 6)
                for n, g in ((0, 0), (1, 3)):
                    nc.vector.scalar_tensor_tensor(out=gated[0:B, n, :], in0=gate[:, g], scalar=0.25, in1=square[0:B, n, :], op0=ALU.max, op1=ALU.max).then_inc(setup_vec.sem, 1)
                for n, g in ((0, 0), (1, 3)):
                    nc.vector.tensor_scalar(h_s[0:B, n, :], gate[:, g], 0.0, 2.0, ALU.is_ge, ALU.mult).then_inc(setup_vec.sem, 1)
                vec.wait_ge(setup_vec.sem, 10)
                for n, g in ((0, 0), (1, 3)):
                    nc.vector.scalar_tensor_tensor(out=gate[:, g], in0=h_s[0:B, n, :], scalar=-1.0, in1=gated[0:B, n, :], op0=ALU.add, op1=ALU.mult).then_inc(setup_vec.sem, 1)
                nc.vector.tensor_scalar(gate[:, 2], gate[:, 2], 1.0, None, ALU.add).then_inc(setup_vec.sem, 1)
                vec.wait_ge(consts_in, 16 * N_CONST)
                nc.vector.tensor_copy(filled[:], c32[:, C_BASE:C_BASE + E]).then_inc(init_vec, 1)
                nc.vector.tensor_copy(tok[:].rearrange("p k s -> p (k s)"), c32[:, C_TOK:C_TOK + K * NS]).then_inc(init_vec, 1)

            pipeline(vec, iteration)

            base, iota_j = c32[:, C_BASE:C_BASE + E], c32[:, C_J:C_J + NT + 1]
            vec.wait_ge(vec_place.sem, vec_place.after(number(B - 1), "tok_on"))
            nc.vector.tensor_copy(tab_i[:, 0], filled[:]).then_inc(table, 1)
            vec.wait_ge(table, 1)
            nc.vector.scalar_tensor_tensor(out=tab[:, 0], in0=filled[:], scalar=float(TS - 1), in1=base, op0=ALU.add, op1=ALU.subtract).then_inc(table, 1)
            vec.wait_ge(table, 2)
            nc.vector.tensor_copy(tab_i[:, 1], tab[:, 0]).then_inc(table, 1)
            vec.wait_ge(table, 3)
            nc.vector.tensor_scalar(tab_i[:, 1], tab_i[:, 1], TS.bit_length() - 1, None, ALU.logical_shift_right).then_inc(table, 1)
            vec.wait_ge(table, 4)
            nc.vector.tensor_copy(tab[:, 1], tab_i[:, 1]).then_inc(table, 1)
            vec.wait_ge(table, 5)
            nc.vector.memset(tab[:, 2], 0.0).then_inc(table, 1)
            vec.wait_ge(table, 6)
            nc.vector.tensor_tensor_scan(tab[:, 3], tab[:, 1], tab[:, 2], 0.0, ALU.add, ALU.add).then_inc(table, 1)
            ends = tab[:, 3].unsqueeze(1).broadcast_to([P, NT + 1, E])
            vec.wait_ge(table, 7)
            nc.vector.tensor_tensor(cmp_j[:], iota_j.unsqueeze(2).broadcast_to([P, NT + 1, E]), ends, ALU.is_ge).then_inc(table, 1)
            vec.wait_ge(table, 8)
            nc.vector.tensor_reduce(tj[:, 0], cmp_j[:], AX.X, ALU.add).then_inc(table, 1)
            vec.wait_ge(table, 9)
            nc.vector.tensor_tensor(cmp_j[:], cmp_j[:], tab[:, 1].unsqueeze(1).broadcast_to([P, NT + 1, E]), ALU.mult).then_inc(table, 1)
            vec.wait_ge(table, 10)
            nc.vector.tensor_reduce(tj[:, 1], cmp_j[:], AX.X, ALU.add).then_inc(table, 1)
            vec.wait_ge(table, 11)
            nc.vector.tensor_tensor(tj[:, 2], iota_j, tj[:, 1], ALU.subtract).then_inc(table, 1)
            vec.wait_ge(table, 12)
            nc.vector.tensor_scalar(tj[:, 3], tj[:, 0], float(REGION), None, ALU.mult).then_inc(table, 1)
            vec.wait_ge(table, 13)
            nc.vector.scalar_tensor_tensor(out=tj[:, 4], in0=tj[:, 2], scalar=float(TS), in1=tj[:, 3], op0=ALU.mult, op1=ALU.add).then_inc(table, 1)
            vec.wait_ge(table, 14)
            nc.vector.tensor_scalar(tj[:, 4], tj[:, 4], float(E * REGION), None, ALU.min).then_inc(table, 1)
            vec.wait_ge(table, 15)
            nc.vector.tensor_copy(tile_row[:], tj[:, 4]).then_inc(table, 1)
            vec.wait_ge(table, 16)
            nc.vector.tensor_scalar(tj[:, 0], tj[:, 0], float(E - 1), None, ALU.min).then_inc(table, 1)
            vec.wait_ge(table, 17)
            nc.vector.tensor_copy(tile_e[:], tj[:, 0]).then_inc(table, 1)
            vec.wait_ge(table, TABLE_STEPS)

            def low(j, f):
                vec.wait_ge(act_hh, times(j, FB, f + 1))
                nc.vector.tensor_tensor(hl[:, j[1] % 2, f], h32[:, f], hh[:, j[1] % 2, f], ALU.subtract).then_inc(vec_hl, 1)

            known_experts, read_next_experts = experts_of(vec)

            def tile(j, finished=True):
                e, last, before_last = known_experts(j)
                if finished:
                    bias_out(plus(j, -2), before_last)
                for f in range(FB):
                    vec.wait_ge(act_silu, times(j, FB, f + 1))
                    if due(times(plus(j, -1), FB, f + 1)):
                        vec.wait_ge(vec_hl, times(plus(j, -1), FB, f + 1))
                    nc.vector.scalar_tensor_tensor(out=h32[:, f], in0=banks[f][:, TS:2 * TS], scalar=b1_sb[:, 1, bass.ds(e * FB + f, 1)],
                                                   in1=silu_a[:, f], op0=ALU.add, op1=ALU.mult).then_inc(vec_h, 1)
                    if f >= 2:
                        low(j, f - 2)
                    if f == 2:
                        read_next_experts(j)
                low(j, FB - 2)
                low(j, FB - 1)
                return e, last

            def bias_out(j, e):
                vec.wait_ge(pe_y, times(j, 1, 1))
                if due(times(plus(j, -2), NS, NS)):
                    vec.wait_ge(act_y, times(plus(j, -2), NS, NS))
                y = (o_bank, tail_bank)[j[1] % 2]
                nc.vector.tensor_tensor(yb[:, j[1] % 2], y[:, 0:NS * D].rearrange("p (s d) -> p s d", d=D),
                                        b2_sb[:, bass.ds(e, 1), :].broadcast_to([P, NS, D]), ALU.add).then_inc(vec_y, 1)

            tile(tile_number(0), finished=False)
            tile(tile_number(1), finished=False)
            in_fours(vec, 2, NT - 1, tile)
            e, last = tile(tile_number(NT - 1))
            bias_out(tile_number(NT - 2), last)
            bias_out(tile_number(NT - 1), e)

            vec.wait_ge(gb_in, 16)

            def finish(n):
                m, r, _ = n
                vec.wait_ge(pool_sum, times(n, 1, 1))
                nc.vector.tensor_tensor(ygate[:, r], ysum[:, r], gb_sb[:, bass.ds(times(n, 1), 1), :].broadcast_to([P, NS, D]), ALU.mult).then_inc(vec_gate, 1)
                vec.wait_ge(vec_gate, times(n, 1, 1))
                if due(times((m, 0, 1), 16)):
                    vec.wait_ge(out_done[r], times((m, 0, 1), 16))
                nc.vector.tensor_tensor(res[:, r], ygate[:, r], x_sb[:, bass.ds(times(n, NS), NS), :], ALU.add).then_inc(vec_res, 1)

            in_fours(vec, 0, B, finish)

        @block.tensor
        def _(pe):
            mm = nc.tensor.matmul

            def halves(o, l_hi, l_lo, r_hi, r_lo, start=True, stop=True):
                mm(o, l_hi, r_hi, start=start, stop=False, skip_group_check=True)
                mm(o, l_hi, r_lo, start=False, stop=False, skip_group_check=True)
                return mm(o, l_lo, r_hi, start=False, stop=stop, skip_group_check=True)

            pe.wait_ge(c_in_sem, 32)
            nc.tensor.transpose(banks[0][:, 0:B], c_sb[:], ident32[0:B, 0:B]).then_inc(setup_pe.sem, 1)
            pe.wait_ge(w_in_sem, 64)
            for n in range(4):
                t = nc.tensor.transpose(banks[2][:, D * n:D * n + D], wraw[:, n, :], ident32[:])
            t.then_inc(setup_pe.sem, 1)
            pe.wait_ge(wmod_in_sem, 16)
            pe.wait_ge(setup_act.sem, 1)
            for n in range(2):
                mm(banks[1][:, B * n:B * n + B], wmod_sb[:, D * n:D * n + D], silu_c[:], start=(n == 0), stop=True, skip_group_check=True)
            mm(banks[3][0:B, :], silu_c[:], wmod_sb[:, 2 * D:6 * D], start=True, stop=True).then_inc(setup_pe.sem, 1)
            pe.wait_ge(consts_in, 16 * N_CONST)
            pe.wait_ge(init_vec, 2)

            def turn_biases():
                pe.wait_ge(b1_in_sem, 32)
                for n in range(2):
                    t = nc.tensor.transpose(o_bank[:, E * FB * n:E * FB * (n + 1)], b1_rows[:, n, :], ident32[0:E * FB, 0:E * FB])
                t.then_inc(setup_pe.sem, 1)

            def project(b, s):
                at = slice(P * s, P * s + P)
                o = (chain_b, chain_a)[s][:, 0:3 * D]
                halves(o, ht_hi[:, at], ht_lo[:, at], w_hi[:, 0:3, :].rearrange("p n d -> p (n d)"), w_lo[:, 0:3, :].rearrange("p n d -> p (n d)")).then_inc(pe0.sem, 1)

            def turn_tile(b, s):
                o = (chain_a16, chain_b16)[s]
                tok_q = qk_tok[:, b[1], s].rearrange("p (j g) w -> p j (g w)", g=HG)
                for j in range(2 * HG):
                    t = nc.tensor.transpose(o[:, P * j:P * j + P], tok_q[:, j, :], ident16)
                t.then_inc(pe0.sem, 1)

            def turn_max(b, half):
                for j in range(2):
                    for s in range(NS):
                        q = qk_tok[:, b[1], s].rearrange("p (j g) w -> p j (g w)", g=HG)[:, 2 * half + j, :]
                        t = nc.tensor.transpose(chain_b16[:, S * j + P * s:S * j + P * s + P], q, ident16)
                t.then_inc(pe1.sem, 1)

            def masks(o, mask):
                diagonal = o[:, 0:4 * P].rearrange("p (c t) -> p c t", t=2 * P)[:, :, 0:P]
                return mm(diagonal, ident16, mask.unsqueeze(1).broadcast_to([P, 2, P]), start=False, stop=True, skip_group_check=True)

            def scores_by_query(b, k):
                j, par = k // HG, b[1]
                if k == 0:
                    pe.wait_ge(act0.sem, act0.after(b, "ev1"))
                if k % 8 < HG:
                    pe.wait_ge(pad_in[k // 8][par][k % HG], times((b[0], 0, 1), 16, 16))
                if due(times(b, H, k - 1)):
                    pe.wait_ge(max_ready, times(b, H, k - 1))
                o = row_bank[k % 2]
                mm(o[:, 0:P], qk_t[:, par, j, 0:P], k_pad[:, par, k, 0:P], start=True, stop=False, skip_group_check=True)
                mm(o[:, P:3 * P], qk_t[:, par, j, P:], k_pad[:, par, k, :], start=False, stop=False, skip_group_check=True)
                masks(o, mask_q).then_inc(rows_ready, 1)

            def scores_by_key(b, k):
                j, par = k // HG, b[1]
                if k % 8 == 0:
                    pe.wait_ge(act1.sem, act1.after(b, "ev" + "ab"[k // 8]))
                if due(times(b, H, k - 1)):
                    pe.wait_ge(probs_ready, times(b, H, k - 1))
                o = col_bank[k % 2]
                mm(o[:, 0:S], k_pad[:, par, k, 0:P], q_max[:, par, j, :], start=True, stop=False, skip_group_check=True)
                mm(o[:, S:S + P], k_pad[:, par, k, P:], q_max[:, par, j, P:], start=False, stop=False, skip_group_check=True)
                masks(o, mask_k).then_inc(cols_ready, 1)

            def values(b, k):
                g, par = k % HG, b[1]
                if g == 0:
                    if due(times(b, HG, k // HG)):
                        pe.wait_ge(group_saved, times(b, HG, k // HG))
                pe.wait_ge(probs_ready, times(b, H, k + 1))
                at = slice(SLOT * g, SLOT * g + SLOT)
                mm(o_bank[at, 0:S], v_aug[:, par, 0, k, :], probs[:, k % 4, 0:S], start=True, stop=False, skip_group_check=True)
                mm(o_bank[at, P:S], v_aug[:, par, 1, k, :], probs[:, k % 4, S:], start=False, stop=True, skip_group_check=True).then_inc(probs_used, 1)

            def out_rows(b, s):
                if s == 0:
                    pe.wait_ge(group_saved, times(b, HG, HG))
                    if due(vec_place.after(plus(b, -2), "filled")):
                        pe.wait_ge(vec_place.sem, vec_place.after(plus(b, -2), "filled"))
                else:
                    pe.wait_ge(vec3a.sem, vec3a.after(b, "on0"))
                for j in range(HG):
                    t = nc.tensor.transpose(tail_bank[:, P * j:P * j + P], o_t[:, b[1], j, P * s:P * s + P], ident32[:])
                t.then_inc(pe3a.sem, 1)

            def ranks(b):
                pe.wait_ge(vec3b.sem, vec3b.after(b, "member"))
                two = member[:].rearrange("p s e -> p (s e)")
                mm(tail_bank[:, 0:2 * E], before16, two, start=True, stop=False, skip_group_check=True)
                mm(tail_bank[:, E:2 * E], ones16, member[:, 0], start=False, stop=False, skip_group_check=True)
                mm(tail_bank[:, 2 * E:3 * E], ones16, member[:, 0], start=False, stop=False, skip_group_check=True)
                mm(tail_bank[:, 2 * E:3 * E], ones16, member[:, 1], start=False, stop=True, skip_group_check=True).then_inc(pe_rank.sem, 1)

            def iteration(i, placing, routing, closing, s2, s1, s0, norm):
                b0, b1, ba, bb, bs = plus(i, 2), plus(i, 1), plus(i, -1), plus(i, -2), plus(i, -3)
                if is_first(i, -1):
                    pe.wait_ge(init_pool, 5)
                    turn_biases()
                if is_first(i, 0):
                    pe.wait_ge(setup_act.sem, 3)
                for k in range(H):
                    if s1:
                        scores_by_query(b1, k)
                    if s2:
                        scores_by_key(i, k)
                    if k < 2 and closing:
                        values(ba, H - 2 + k)
                    if k % HG == 3 and s2:
                        values(i, k - 3)
                    if k >= 2 and k % HG != 2 and s2:
                        values(i, k - 2)
                    if k == 0 and placing:
                        if routing:
                            pe.wait_ge(vec3a.sem, vec3a.after(bb, "gated"))
                        ranks(bs)
                    if k == 1 and s2:
                        pe.wait_ge(vec1.sem, vec1.after(i, "m1b"))
                        if s1:
                            pe.wait_ge(act0.sem, act0.after(b1, "ev1"))
                        turn_max(i, 1)
                    if k == 9 and s1:
                        if s0:
                            pe.wait_ge(vec0.sem, vec0.after(b0, "sin0b"))
                        elif s2:
                            pe.wait_ge(act1.sem, act1.after(i, "evb"))
                        pe.wait_ge(vec1.sem, vec1.after(b1, "m1a"))
                        turn_max(b1, 0)
                    if closing:
                        if k == 2:
                            out_rows(ba, 0)
                        if k == 6:
                            out_rows(ba, 1)
                        if k == 10:
                            pe.wait_ge(vec3a.sem, vec3a.after(ba, "on1"))
                            for s in range(NS):
                                t = nc.tensor.transpose(tail_bank[:, P * s:P * s + P], o_n[:, s], ident32[:])
                            t.then_inc(pe3a.sem, 1)
                        if k == 14:
                            pe.wait_ge(vec3a.sem, vec3a.after(ba, "on_lo"))
                            for s in range(NS):
                                at = slice(P * s, P * s + P)
                                t = halves(tail_bank[:, at], on_hi[:, at], on_lo[:, at], w_hi[:, 3], w_lo[:, 3], start=(s == 0))
                            t.then_inc(pe3a.sem, 1)
                    if s0:
                        if k == 0:
                            pe.wait_ge(vecn.sem, vecn.after(b0, "xhat1"))
                            if due(act0.after(plus(b0, -1), "ev0")):
                                pe.wait_ge(act0.sem, act0.after(plus(b0, -1), "ev0"))
                            if placing:
                                pe.wait_ge(vec3b.sem, vec3b.after(bs, "logits"))
                            for s in range(NS):
                                t = nc.tensor.transpose(chain_a[:, P * s:P * s + P], xhat0[:, s], ident32[:])
                            t.then_inc(pe0.sem, 1)
                        if k == 3:
                            if is_first(i, -2):
                                pe.wait_ge(setup_vec.sem, 4)
                            pe.wait_ge(pool0.sem, pool0.after(b0, "h_lo"))
                            if due(act0.after(plus(b0, -1), "ev1")):
                                pe.wait_ge(act0.sem, act0.after(plus(b0, -1), "ev1"))
                            if s2:
                                pe.wait_ge(act1.sem, act1.after(i, "evb"))
                            project(b0, 0)
                        if k == 5:
                            project(b0, 1)
                        if k == 10:
                            pe.wait_ge(vec0.sem, vec0.after(b0, "sin1b"))
                            pe.wait_ge(pool0.sem, pool0.after(b0, "klo0"))
                            turn_tile(b0, 0)
                        if k == 12:
                            pe.wait_ge(pool0.sem, pool0.after(b0, "klo1"))
                            if s1:
                                pe.wait_ge(act1.sem, act1.after(b1, "eva"))
                            turn_tile(b0, 1)
                    if routing:
                        if k == 12:
                            pe.wait_ge(act0.sem, act0.after(b0 if s0 else number(B - 1), "ev0"))
                            if due(vec3b.after(plus(bb, -1), "logits")):
                                pe.wait_ge(vec3b.sem, vec3b.after(plus(bb, -1), "logits"))
                            pe.wait_ge(vec3b.sem, vec3b.after(bb, "xn1"))
                            for s in range(NS):
                                t = nc.tensor.transpose(chain_a[:, P * s:P * s + P], xn[:, s], ident32[:])
                            t.then_inc(pe3b.sem, 1)
                        if k == 13:
                            pe.wait_ge(act3b.sem, act3b.after(bb, "xn_t"))
                            for s in range(NS):
                                t = mm(chain_a[:, E * s:E * s + E], xn_t[:, P * s:P * s + P], wg_sb[:], start=(s == 0), stop=True, skip_group_check=True)
                            t.then_inc(pe3b.sem, 1)

            pipeline(pe, iteration)

            pe.wait_ge(table, TABLE_STEPS)

            def turn_rows(j):
                r = j[1]
                pe.wait_ge(g_arrived[r], times((j[0], 0, 1), 16, 16))
                if due(times(plus(j, -2), 1, 1)):
                    pe.wait_ge(act_x, times(plus(j, -2), 1, 1))
                o = (chain_a16, chain_b16)[r % 2]
                for h in range(2):
                    for s in range(NS):
                        words = g_in[:, r, s, 0:D].bitcast(F16)
                        t = nc.tensor.transpose(o[:, TS * h + P * s:TS * h + P * s + P], words[:, D * h:D * h + D], ident16)
                t.then_inc(pe_x, 1)

            known_experts, read_next_experts = experts_of(pe)

            def hidden(j, more=True):
                e, last, _ = known_experts(j)
                x_hi, x_lo = xt[:, j[1] % 2, 0, :], xt[:, j[1] % 2, 1, :]
                pe.wait_ge(act_x, times(j, 1, 1))
                for f in range(FB):
                    if due(times(plus(j, -1), FB, f + 1)):
                        pe.wait_ge(vec_h, times(plus(j, -1), FB, f + 1))
                    at = bass.ds(e * F + f * P, P)
                    for n in range(2):
                        o = banks[f][:, TS * n:TS * n + TS]
                        mm(o, we_hi[:, n, at], x_hi, start=(n == 0), stop=False, skip_group_check=True)
                        mm(o, we_hi[:, n, at], x_lo, start=False, stop=False, skip_group_check=True)
                        t = mm(o, we_lo[:, n, at], x_hi, start=False, stop=True, skip_group_check=True)
                    t.then_inc(pe_ab, 1)
                    if f == 1 and more:
                        turn_rows(plus(j, 1))
                    if f == 2:
                        read_next_experts(j)
                return e, last

            def project_out(j, e):
                par = j[1] % 2
                pe.wait_ge(vec_hl, times(j, FB, FB))
                if due(times(plus(j, -2), 1, 1)):
                    pe.wait_ge(vec_y, times(plus(j, -2), 1, 1))
                y = (o_bank, tail_bank)[par]
                for f in range(FB):
                    at = bass.ds(e * F + f * P, P)
                    for s in range(NS):
                        o = y[:, D * s:D * s + D]
                        tok_s = slice(P * s, P * s + P)
                        mm(o, hh[:, par, f, tok_s], we_hi[:, 2, at], start=(s == 0 and f == 0), stop=False, skip_group_check=True)
                        mm(o, hh[:, par, f, tok_s], we_lo[:, 2, at], start=False, stop=False, skip_group_check=True)
                        t = mm(o, hl[:, par, f, tok_s], we_hi[:, 2, at], start=False, stop=(f == FB - 1), skip_group_check=True)
                t.then_inc(pe_y, 1)

            def tile_and_last(j, more=True):
                e, last = hidden(j, more)
                project_out(plus(j, -1), last)
                return e

            turn_rows(tile_number(0))
            hidden(tile_number(0))
            in_fours(pe, 1, NT - 1, tile_and_last)
            project_out(tile_number(NT - 1), tile_and_last(tile_number(NT - 1), False))


def constants():
    f = np.float32
    theta = (f(1.0) / f(10000.0) ** (np.arange(0, DK, 2, dtype=f) / f(DK))).astype(f)
    angle = np.outer(np.arange(S, dtype=f), theta).astype(f).reshape(NS, P, DK // 2).transpose(1, 0, 2).reshape(P, -1)
    p = np.arange(P)
    c = np.zeros((P, NC32 + P), f)
    c[:, C_COS:C_COS + 8] = np.cos(angle)
    c[:, C_SIN:C_SIN + 8] = np.sin(angle)
    c[:, C_E:C_E + E] = np.arange(E)
    c[:, C_BASE:C_BASE + E] = np.arange(E) * REGION
    for k in range(K):
        for s in range(NS):
            c[:, C_TOK + k * NS + s] = K * (s * P + p) + k
    c[:, C_POW:C_POW + 4] = -0.5
    c[:, C_J:C_J + NT + 1] = np.arange(NT + 1)
    c[:, NC32:] = np.eye(P)
    c16 = np.stack([np.eye(P), p[:, None] < p[None, :], np.ones((P, P))], 1).astype(np.float16)
    after = p[None, :] > p[:, None]
    masks = np.stack([np.where(after, MASKED, 0.0), np.where(after.T, MASKED, 0.0)], 1)
    dummy = np.zeros((TS, ROWW), f)
    dummy[:, W_IDX] = (NOUT + np.arange(TS)).astype(np.int32).view(f)
    return c, c16, masks, dummy


_INS = ['L0_attn_x', 'L0_attn_W_Q', 'L0_attn_W_K', 'L0_attn_W_V', 'L0_attn_W_O', 'L0_ffn_ln_w', 'L0_ffn_Wg', 'L0_ffn_bg',
        'L0_ffn_W1a', 'L0_ffn_b1a', 'L0_ffn_W1b', 'L0_ffn_b1b', 'L0_ffn_W2', 'L0_ffn_b2', 'L0_c', 'L0_wmod']


def kernel(**inputs):
    import ml_dtypes
    import concourse.bacc as _bacc
    from concourse import mybir as _mybir
    from concourse.bass_utils import run_bass_kernel_spmd as _run

    nc = _bacc.Bacc("TRN2", target_bir_lowering=False, num_devices=1)
    c, c16, masks, dummy = constants()
    arrays, args = {}, []
    named = [(name, np.ascontiguousarray(inputs[name])) for name in _INS]
    named += [("const32", c), ("const16", c16), ("constb", masks.astype(ml_dtypes.bfloat16)), ("dummy", dummy)]
    for name, a in named:
        arrays[f"in_{name}_dram"] = a
        args.append(nc.dram_tensor(f"in_{name}_dram", a.shape, _mybir.dt.from_np(a.dtype), kind="ExternalInput").ap())
    o = nc.dram_tensor("out_0_dram", (B, S, D), F32, kind="ExternalOutput").ap()
    build(nc, *args, o)
    r = _run(nc, [arrays], core_ids=[0])
    return r.results[0]["out_0_dram"]
```
